# Optimizing a Trainium2 kernel written in Bass

```python
import numpy as np
import jax
import jax.numpy as jnp

def _softmax(x, axis=-1):
    return jax.nn.softmax(x, axis=axis)

def _gelu(x):
    return jax.nn.gelu(x, approximate=True)

def _silu(x):
    return jax.nn.silu(x)

def _sigmoid(x):
    return jax.nn.sigmoid(x)

def _layernorm(x, axis=-1, eps=1e-05):
    m = jnp.mean(x, axis=axis, keepdims=True)
    v = jnp.var(x, axis=axis, keepdims=True)
    return (x - m) / jnp.sqrt(v + eps)

def _scatter_add(tgt, idx, src, axis=0):
    return tgt.at[idx].add(src)

def _segment_sum(src, seg, n):
    return jax.ops.segment_sum(src, seg, n)
kernel_name = 'mk_adaln_d1_jaxref_r4_c5922b'

def setup_inputs(seed: int=0):
    np.random.seed(seed)
    _w = jnp.asarray

    def _L0_attn_setup():
        import jax, jax.numpy as jnp
        import numpy as np
        D_MODEL, N_HEADS, BATCH, SEQ = (256, 16, 2, 512)

        def get_freqs(seq, n_dim):
            inv_freq = 1.0 / 10000.0 ** (jnp.arange(0, n_dim, 2, dtype=jnp.float32) / n_dim)
            pos = jnp.arange(seq, dtype=jnp.float32)
            return pos[:, None] * inv_freq[None, :]

        def rope(x, freq):
            cos = jnp.cos(freq)[None, :, None, :]
            sin = jnp.sin(freq)[None, :, None, :]
            x1, x2 = (x[..., ::2], x[..., 1::2])
            r1 = x1 * cos - x2 * sin
            r2 = x1 * sin + x2 * cos
            return jnp.stack([r1, r2], axis=-1).reshape(x.shape)
        key = jax.random.key(seed)
        ks = jax.random.split(key, 5)
        w_scale = 0.01
        return {'x': jax.random.normal(ks[0], (BATCH, SEQ, D_MODEL), dtype=jnp.float32), 'qw': jax.random.normal(ks[1], (D_MODEL, D_MODEL), dtype=jnp.float32) * w_scale, 'kw': jax.random.normal(ks[2], (D_MODEL, D_MODEL), dtype=jnp.float32) * w_scale, 'vw': jax.random.normal(ks[3], (D_MODEL, D_MODEL), dtype=jnp.float32) * w_scale, 'ow': jax.random.normal(ks[4], (D_MODEL, D_MODEL), dtype=jnp.float32) * w_scale}
    _L0_attn_in = _L0_attn_setup()

    def _L0_ffn_setup():
        import jax, jax.numpy as jnp
        import numpy as np
        B, S, H, F, E = (1, 512, 256, 512, 8)

        def _swiglu(x, wg, wu, wd):
            return jax.nn.silu(x @ wg.T) * (x @ wu.T) @ wd.T
        key = jax.random.key(seed)
        ks = jax.random.split(key, 8)
        sc = 1.0 / np.sqrt(H)
        scf = 1.0 / np.sqrt(F)
        return {'hidden_states': jax.random.normal(ks[0], (B, S, H), jnp.float32), 'gate_w': jax.random.normal(ks[1], (E, H), jnp.float32) * sc, 'shared_gate': jax.random.normal(ks[2], (F, H), jnp.float32) * sc, 'shared_up': jax.random.normal(ks[3], (F, H), jnp.float32) * sc, 'shared_down': jax.random.normal(ks[4], (H, F), jnp.float32) * scf, 'r_gate': jax.random.normal(ks[5], (E, F, H), jnp.float32) * sc, 'r_up': jax.random.normal(ks[6], (E, F, H), jnp.float32) * sc, 'r_down': jax.random.normal(ks[7], (E, H, F), jnp.float32) * scf}
    _L0_ffn_in = _L0_ffn_setup()
    _L0_c = _w((lambda *s: np.random.randn(*s).astype(np.float32) * 0.05)(8, 256))
    _L0_wmod = _w((lambda *s: np.random.randn(*s).astype(np.float32) * 0.05)(256, 6 * 256) * 256 ** (-0.5))
    _d = {'L0_attn_x': _L0_attn_in['x'], 'L0_attn_qw': _L0_attn_in['qw'], 'L0_attn_kw': _L0_attn_in['kw'], 'L0_attn_vw': _L0_attn_in['vw'], 'L0_attn_ow': _L0_attn_in['ow'], 'L0_ffn_gate_w': _L0_ffn_in['gate_w'], 'L0_ffn_shared_gate': _L0_ffn_in['shared_gate'], 'L0_ffn_shared_up': _L0_ffn_in['shared_up'], 'L0_ffn_shared_down': _L0_ffn_in['shared_down'], 'L0_ffn_r_gate': _L0_ffn_in['r_gate'], 'L0_ffn_r_up': _L0_ffn_in['r_up'], 'L0_ffn_r_down': _L0_ffn_in['r_down'], 'L0_c': _L0_c, 'L0_wmod': _L0_wmod}
    _x0 = _d['L0_attn_x']
    _d['L0_attn_x'] = jax.random.normal(jax.random.fold_in(jax.random.key(seed), 1), (8, 512, 256), dtype=_x0.dtype)
    del _x0
    return _d

def reference(L0_attn_x, L0_attn_qw, L0_attn_kw, L0_attn_vw, L0_attn_ow, L0_ffn_gate_w, L0_ffn_shared_gate, L0_ffn_shared_up, L0_ffn_shared_down, L0_ffn_r_gate, L0_ffn_r_up, L0_ffn_r_down, L0_c, L0_wmod):

    def _L0_attn_ref(x, qw, kw, vw, ow):
        import jax, jax.numpy as jnp
        import numpy as np
        D_MODEL, N_HEADS, BATCH, SEQ = (256, 16, 2, 512)

        def get_freqs(seq, n_dim):
            inv_freq = 1.0 / 10000.0 ** (jnp.arange(0, n_dim, 2, dtype=jnp.float32) / n_dim)
            pos = jnp.arange(seq, dtype=jnp.float32)
            return pos[:, None] * inv_freq[None, :]

        def rope(x, freq):
            cos = jnp.cos(freq)[None, :, None, :]
            sin = jnp.sin(freq)[None, :, None, :]
            x1, x2 = (x[..., ::2], x[..., 1::2])
            r1 = x1 * cos - x2 * sin
            r2 = x1 * sin + x2 * cos
            return jnp.stack([r1, r2], axis=-1).reshape(x.shape)
        batch, seq, dim = x.shape
        n_heads = N_HEADS
        n_dim = dim // n_heads
        Q = (x @ qw).astype(jnp.float32).reshape(batch, seq, n_heads, n_dim)
        K = (x @ kw).astype(jnp.float32).reshape(batch, seq, n_heads, n_dim)
        V = (x @ vw).astype(jnp.float32).reshape(batch, seq, n_heads, n_dim)
        freq = get_freqs(seq, n_dim)
        Q = rope(Q, freq)
        K = rope(K, freq)
        Q = jnp.transpose(Q, (0, 2, 1, 3))
        K = jnp.transpose(K, (0, 2, 1, 3))
        V = jnp.transpose(V, (0, 2, 1, 3))
        scale = jnp.sqrt(jnp.float32(n_dim))
        score = jnp.einsum('bhqd,bhkd->bhqk', Q, K) / scale
        causal = jnp.tril(jnp.ones((1, 1, seq, seq), dtype=jnp.float32))
        score = score - 10000000000.0 * (1.0 - causal)
        score = score - jnp.max(score, axis=-1, keepdims=True)
        weights = jax.nn.softmax(score, axis=-1)
        attn = jnp.einsum('bhqk,bhkd->bhqd', weights, V)
        merged = jnp.transpose(attn, (0, 2, 1, 3)).reshape(batch, seq, dim)
        return (merged @ ow).astype(x.dtype)

    def _L0_ffn_ref(hidden_states, gate_w, shared_gate, shared_up, shared_down, r_gate, r_up, r_down):
        import jax, jax.numpy as jnp
        import numpy as np
        B, S, H, F, E = (1, 512, 256, 512, 8)

        def _swiglu(x, wg, wu, wd):
            return jax.nn.silu(x @ wg.T) * (x @ wu.T) @ wd.T
        b, s, h = hidden_states.shape
        x = hidden_states.reshape(-1, h)
        shared_out = _swiglu(x, shared_gate, shared_up, shared_down)
        logits = x @ gate_w.T
        top_id = jnp.argmax(logits, axis=-1)
        score = jax.nn.sigmoid(jnp.max(logits, axis=-1))
        xs = x * score[:, None]

        def body(acc, ws):
            wg, wu, wd, e = ws
            xe = jnp.where((top_id == e)[:, None], xs, 0.0)
            return (acc + _swiglu(xe, wg, wu, wd), None)
        acc0 = jnp.zeros_like(x)
        routed_out, _ = jax.lax.scan(body, acc0, (r_gate, r_up, r_down, jnp.arange(E)))
        return (shared_out + routed_out).reshape(b, s, h)
    x = L0_attn_x
    mod = (_silu(L0_c) @ L0_wmod).reshape(L0_c.shape[0], 6, 1, -1)
    sa, ca, ga, sb, cb, gb = (mod[:, 0], mod[:, 1], mod[:, 2], mod[:, 3], mod[:, 4], mod[:, 5])
    ga = (2 * (ga >= 0) - 1) * jnp.maximum(jnp.abs(ga), 0.25)
    gb = (2 * (gb >= 0) - 1) * jnp.maximum(jnp.abs(gb), 0.25)
    h = _layernorm(x, axis=-1) * (1 + ca) + sa
    x = x + ga * _L0_attn_ref(h, L0_attn_qw, L0_attn_kw, L0_attn_vw, L0_attn_ow)
    h = _layernorm(x, axis=-1) * (1 + cb) + sb
    x = x + gb * _L0_ffn_ref(h, L0_ffn_gate_w, L0_ffn_shared_gate, L0_ffn_shared_up, L0_ffn_shared_down, L0_ffn_r_gate, L0_ffn_r_up, L0_ffn_r_down)
    return x

_drawn_inputs = setup_inputs


def setup_inputs(seed=0):
    import zlib

    import numpy as np

    out = dict(_drawn_inputs(seed))
    spreads = {}
    factors = {'L0_attn_qw': 8.0, 'L0_attn_kw': 8.0, 'L0_attn_vw': 8.0, 'L0_attn_ow': 8.0}
    for name, (base, spread) in spreads.items():
        noise = np.random.default_rng([zlib.crc32(name.encode()), seed]).standard_normal(out[name].shape)
        drawn = base * np.exp(spread * noise) if base else spread * noise
        out[name] = jnp.asarray(drawn.astype(out[name].dtype))
    for name, factor in factors.items():
        out[name] = (out[name] * factor).astype(out[name].dtype)
    return out
```

```python
from contextlib import ExitStack

import concourse.bass as bass
import numpy as np
from concourse import mybir

F32 = mybir.dt.float32
F32R = mybir.dt.float32r
BF16 = mybir.dt.bfloat16
I32 = mybir.dt.int32
U32 = mybir.dt.uint32
ALU = mybir.AluOpType
ACT = mybir.ActivationFunctionType
AX = mybir.AxisListType

P = 128
B, S, D = 8, 512, 256
NH, HD = 16, 16
F, NE = 512, 8
KT = S // P
DC = D // P
FC = F // P
NT = B * KT
ST = NT + NE - 1
GH = 4
NG = NH // GH
PAIRW = 2 * 1280
MAXB = 10
EXPB = 10
EPS = 1e-5
NEG = -1e10


def constants():
    row = np.arange(P) % HD
    inv = (1.0 / np.float32(10000.0) ** (np.arange(0, HD, 2, dtype=np.float32) / HD)).astype(np.float32)
    ang = (np.arange(S, dtype=np.float32)[None, :] * inv[row // 2][:, None]).astype(np.float32)
    cos, sin = np.cos(ang), np.sin(ang) * np.where(row % 2 == 0, -1.0, 1.0)[:, None]
    rope = np.stack([cos / 4, sin / 4, cos, sin], axis=1).astype(np.float32)
    ident = np.eye(P, dtype=np.float32)
    mask = np.zeros((P, S), np.float32)
    mask[:, S - P:] = np.where(np.arange(P)[None, :] > np.arange(P)[:, None], NEG, 0.0)
    before = (np.arange(P)[:, None] < np.arange(P)[None, :]).astype(np.float32)
    experts = np.broadcast_to(np.arange(NE, dtype=np.float32), (P, NE))
    starts = np.broadcast_to(P * np.arange(40, dtype=np.float32)[:, None], (P, 40, NE))
    return {
        "c_rope": rope, "c_ident": ident, "c_mask": mask, "c_before": before,
        "c_experts": np.ascontiguousarray(experts), "c_starts": np.ascontiguousarray(starts),
    }


RSQRT_STEPS = 14


def wait_apart(eng, sem, value):
    eng.wait_ge(sem, value)
    if not isinstance(value, int):
        eng.nop(nofuse=True)


def rsqrt_steps(pool, step, base, out, var, v, a):
    n = 0

    def then(ins):
        nonlocal n
        n += 1
        ins.then_inc(step, 1)
        wait_apart(pool, step, base + n)

    then(pool.tensor_scalar(v, var, EPS, None, ALU.add))
    then(pool.tensor_scalar(out.bitcast(I32), v.bitcast(I32), -0.5, float(0x5F3759DF), ALU.mult, ALU.add))
    for _ in range(3):
        then(pool.tensor_tensor(a, out, out, ALU.mult))
        then(pool.tensor_tensor(a, a, v, ALU.mult))
        then(pool.tensor_scalar(a, a, -0.5, 1.5, ALU.mult, ALU.add))
        then(pool.tensor_tensor(out, out, a, ALU.mult))
    assert n == RSQRT_STEPS


def setup(nc, d, t):
    with ExitStack() as ctx:
        sb = lambda n, s, dt=F32: ctx.enter_context(nc.sbuf_tensor(n, s, dt))
        sem = lambda n: ctx.enter_context(nc.semaphore(n))
        w32 = sb("w32", [P, DC, 4 * D])
        wmod = sb("wmod", [P, DC, 6 * D])
        cT = sb("cT", [P, DC, B])
        ce = sb("ce", [P, DC, B])
        sc = sb("sc", [P, DC, B])
        modrow = sb("modrow", [B, 6 * D])
        sgn = sb("sgn", [B, 2, D])
        zero = sb("zero", [P, 20 * D])
        pm = [ctx.enter_context(nc.psum_tensor(f"pm{i}", [P, 512], F32)) for i in range(3)]
        pt = ctx.enter_context(nc.psum_tensor("pt", [P, 512], F32))
        loaded, cloaded, split = sem("set_loaded"), sem("set_cloaded"), sem("set_split")
        step, scdone, rows, cols = sem("set_step"), sem("set_sc"), sem("set_rows"), sem("set_cols")
        ex, rowsb, stored = sem("set_exp"), sem("set_rowsb"), sem("set_stored")
        tables = sem("set_tables")
        with nc.Block() as block:

            @block.sync
            def _(sp):
                sp.dma_start(cT[:], d["cT"].rearrange("(c p) b -> p c b", p=P)).then_inc(cloaded, 16)
                sp.dma_start(wmod[:], d["wmod"].rearrange("(c p) n -> p c n", p=P)).then_inc(cloaded, 16)
                for i, n in enumerate(("qw", "kw", "vw", "ow")):
                    sp.dma_start(w32[:, :, i * D:(i + 1) * D],
                                 d[n].rearrange("(c p) n -> p c n", p=P)).then_inc(loaded, 16)
                sp.dma_start(t["rope"][:], d["c_rope"]).then_inc(tables, 16)
                sp.dma_start(t["ident"][:], d["c_ident"]).then_inc(tables, 16)
                sp.dma_start(t["mask"][:], d["c_mask"]).then_inc(tables, 16)
                sp.wait_ge(rowsb, 3)
                sp.dma_start(d["mod"], modrow[:]).then_inc(stored, 16)
                sp.wait_ge(step, 1)
                for i in range(2):
                    sp.dma_start(d["sorted"][i * 20 * P:(i + 1) * 20 * P, :].rearrange("(p r) n -> p (r n)", p=P),
                                 zero[:]).then_inc(stored, 16)
                sp.wait_ge(stored, 48)
                sp.wait_ge(tables, 48)

            @block.scalar
            def _(act):
                act.wait_ge(cloaded, 32)
                act.activation(ce[:], cT[:], ACT.Exp, scale=-1.0).then_inc(ex, 1)

            @block.vector
            def _(dve):
                dve.wait_ge(ex, 1)
                dve.tensor_scalar(ce[:], ce[:], 1.0, None, ALU.add).then_inc(scdone, 1)
                dve.wait_ge(scdone, 1)
                dve.reciprocal(ce[:], ce[:]).then_inc(scdone, 1)
                dve.wait_ge(scdone, 2)
                dve.tensor_tensor(sc[:], cT[:], ce[:], ALU.mult).then_inc(scdone, 1)
                dve.wait_ge(loaded, 64)
                dve.tensor_copy(t["wh"][:], w32[:]).then_inc(split, 1)
                dve.wait_ge(cols, 1)
                dve.tensor_copy(t["modT"][:, 0:2, :], pt[:, 0:16].rearrange("p (k b) -> p k b", b=B)).then_inc(split, 1)
                dve.tensor_scalar(t["modT"][:, 2:4, :], pt[:, 16:32].rearrange("p (k b) -> p k b", b=B),
                                  1.0, None, ALU.add).then_inc(split, 1)
                dve.wait_ge(rows, 1)
                dve.tensor_copy(modrow[:, 0:512], pm[0][0:B, :]).then_inc(rowsb, 1)
                dve.tensor_copy(modrow[:, 768:1024], pm[1][0:B, 256:512]).then_inc(rowsb, 1)
                dve.tensor_scalar(modrow[:, 1024:1280], pm[2][0:B, 0:256], 1.0, None, ALU.add)
                gates = [(pm[1][0:B, 0:256], modrow[:, 512:768]), (pm[2][0:B, 256:512], modrow[:, 1280:1536])]
                n = 3
                for k, (g, out) in enumerate(gates):
                    dve.tensor_scalar(sgn[:, k, :], g, 0.0, 2.0, ALU.is_ge, ALU.mult).then_inc(scdone, 1)
                    dve.wait_ge(scdone, n + 1)
                    dve.tensor_scalar(sgn[:, k, :], sgn[:, k, :], -1.0, None, ALU.add).then_inc(scdone, 1)
                    dve.wait_ge(scdone, n + 2)
                    dve.tensor_tensor(out, g, sgn[:, k, :], ALU.mult).then_inc(scdone, 1)
                    dve.wait_ge(scdone, n + 3)
                    n += 3
                    ins = dve.scalar_tensor_tensor(out, out, 0.25, sgn[:, k, :], ALU.max, ALU.mult)
                ins.then_inc(rowsb, 1)

            @block.gpsimd
            def _(pool):
                pool.memset(zero[:], 0.0).then_inc(step, 1)
                pool.memset(t["ks"][:].bitcast(F32), 1.0)
                pool.memset(t["vaug"][:], 1.0)
                pool.wait_ge(split, 1)
                pool.tensor_tensor(t["wl"][:], w32[:], t["wh"][:].bitcast(F32), ALU.subtract)

            @block.tensor
            def _(pe):
                pe.wait_ge(scdone, 3)
                for k in range(4):
                    for c in range(DC):
                        mm = pe.matmul(pt[:, k * B:(k + 1) * B], wmod[:, c, k * P:(k + 1) * P], sc[:, c, :],
                                       start=(c == 0), stop=(c == DC - 1))
                mm.then_inc(cols, 1)
                for k in range(3):
                    for c in range(DC):
                        mm = pe.matmul(pm[k][0:B, :], sc[:, c, :], wmod[:, c, k * 512:(k + 1) * 512],
                                       start=(c == 0), stop=(c == DC - 1))
                mm.then_inc(rows, 1)


def max_banks():
    return ([[(2, h, 0), (0, h, 384)] for h in range(GH)] + [[(1, h, 0), (1, h + 2, 256)] for h in range(2)]
            + [[(3, h, 0)] for h in range(GH)])


def exp_banks():
    out = []
    for pair in range(2):
        for u in range(2):
            h, base = pair + 2 * u, pair * PAIRW + u * 1024
            out.append(([(0, h, 0)], base))
            out.append(([(1, h, 0), (3, h, 384)], base + 512))
        out.append(([(2, pair, 0), (2, pair + 2, 256)], pair * PAIRW + 2048))
    return out


def prob_column(kt, h):
    base, u = (h % 2) * PAIRW, h // 2
    return base + {0: u * 1024, 1: u * 1024 + 512, 3: u * 1024 + 896, 2: 2048 + u * 256}[kt]


PRODUCTS = ((0, 0), (0, 1), (1, 0))


def attention(nc, d, t):
    with ExitStack() as ctx:
        sb = lambda n, s, dt=F32: ctx.enter_context(nc.sbuf_tensor(n, s, dt))
        ps = lambda n: ctx.enter_context(nc.psum_tensor(n, [P, 512], F32))
        sem = lambda n: ctx.enter_context(nc.semaphore(n))
        W = (t["wh"], t["wl"])
        ident, mask, rope, modT = t["ident"], t["mask"], t["rope"], t["modT"]
        qs, ks, vaug = t["qs"], t["ks"], t["vaug"]
        xb = sb("xb", [P, KT, D])
        xn = sb("xn", [P, KT, D])
        stats = sb("stats", [P, KT, 6])
        mv = sb("mv", [P, KT, 2])
        rstd, nv, na = sb("rstd", [P, KT]), sb("nv", [P, KT]), sb("na", [P, KT])
        ht32 = sb("ht32", [P, DC, S])
        hT = (sb("hTh", [P, DC, S], F32R), sb("hTl", [P, DC, S], F32R))
        qk = sb("qk", [P, 4, S])
        qksw = sb("qksw", [P, 4, S])
        qkh = sb("qkh", [P, 4, S], F32R)
        qkl = sb("qkl", [P, 4, S], F32R)
        mx = sb("mx", [P, 2, KT, GH])
        mrow = [sb(f"mrow{i}", [GH, S], F32R) for i in range(2)]
        probs = sb("probs", [P, 2, 2 * PAIRW])
        oT = sb("oT", [P, NG, S])
        rden = sb("rden", [P, KT, NH])
        att = sb("att", [P, KT, D])
        attT = (sb("attTh", [P, DC, S], F32R), sb("attTl", [P, DC, S], F32R))
        gab = sb("gab", [P, D])
        xr = sb("xr", [P, KT, D])
        yo = sb("yo", [P, KT, D])
        pM, pS, pO, pX = ([ps(f"p{n}{i}") for i in range(2)] for n in "MSOX")

        x_in, x_free = sem("x_in"), sem("x_free")
        ln_a, ln_b, ln_s = sem("ln_stats"), sem("ln_rstd"), sem("ln_step")
        xn_done = sem("xn_done")
        v_full, qk_full, xt_full = sem("v_full"), sem("qk_full"), sem("xt_full")
        v_ready, th_done, tl_done, qk_ev = sem("v_ready"), sem("th_done"), sem("tl_done"), sem("qk_ev")
        swapped, rope1, rope2, rope3 = sem("swapped"), sem("rope1"), sem("rope2"), sem("rope3")
        qkh_done, qkl_done, bounced = sem("qkh_done"), sem("qkl_done"), sem("bounced")
        stk = [sem("stack_lo"), sem("stack_hi")]
        m_full, m_free, s_full, s_free = sem("m_full"), sem("m_free"), sem("s_full"), sem("s_free")
        neg_full, mrow_done, mrow_in = sem("neg_full"), sem("mrow_done"), sem("mrow_in")
        sel_done, o_full, o_free = sem("sel_done"), sem("o_full"), sem("o_free")
        ot_full, rd_done, att_done = sem("ot_full"), sem("rd_done"), sem("att_done")
        at_full, ath_done, atl_done = sem("at_full"), sem("ath_done"), sem("atl_done")
        y_full, y_ga, x1_done, x1_out = sem("y_full"), sem("y_ga"), sem("x1_done"), sem("x1_out")
        aux_in = sem("aux_in")

        def stack(tile, h, rows, cols):
            r = 64 * (h % 2)
            return tile[r:r + rows, h // 2, cols]

        with nc.Block() as block:

            @block.tensor
            def _(pe):
                read = [None, None]

                def take(k, signal, value):
                    if read[k] is not None:
                        pe.wait_ge(*read[k])
                    read[k] = (signal, value)
                    return pX[k]

                def max_bank(b, g, i):
                    n = 10 * (4 * b + g) + i
                    if not (isinstance(n, int) and n < 2):
                        pe.wait_ge(m_free, n - 1)
                    for qt, h, col in max_banks()[i]:
                        hh = GH * g + h
                        mm = pe.matmul(pM[i % 2][:, col:col + P * (qt + 1)],
                                       stack(qs, hh, 48, slice(qt * P, qt * P + P)),
                                       stack(ks, hh, 48, slice(0, P * (qt + 1))), start=True, stop=True)
                    mm.then_inc(m_full, 1)

                def exp_bank(b, g, i):
                    n = 40 * b + 10 * g + i
                    if not (isinstance(n, int) and n < 2):
                        pe.wait_ge(s_free, n - 1)
                    for kt, h, col in exp_banks()[i][0]:
                        hh = GH * g + h
                        mm = pe.matmul(pS[i % 2][:, col:col + S - kt * P],
                                       stack(ks, hh, 49, slice(kt * P, kt * P + P)),
                                       stack(qs, hh, 49, slice(kt * P, S)), start=True, stop=True)
                    mm.then_inc(s_full, 1)
                    return mm

                def group(b, g, nxt):
                    pe.wait_ge(mrow_in, 32 * (4 * b + g + 1))
                    if nxt is not None and nxt[1] in (0, 2):
                        pe.wait_ge(stk[nxt[1] // 2], 192 * (nxt[0] + 1))
                    for i in range(MAXB):
                        if i < EXPB:
                            mm = exp_bank(b, g, i)
                        if nxt is not None:
                            max_bank(*nxt, i)

                def negate(b, g):
                    s = 4 * b + g
                    bank = take(0, mrow_done, s + 1)
                    pe.wait_ge(m_free, 10 * (s + 1))
                    for qt in range(KT):
                        mm = pe.transpose(bank[0:GH, qt * P:(qt + 1) * P], mx[:, g % 2, qt, :], ident[:])
                    mm.then_inc(neg_full, 1)

                def values(b, g):
                    s = 4 * b + g
                    pe.wait_ge(sel_done, 2 * (s + 1))
                    if not (isinstance(s, int) and s < 2):
                        pe.wait_ge(o_free, s - 1)
                    if g == 0:
                        pe.wait_ge(v_ready, 2 * (b + 1))
                    for kt in range(KT):
                        for h in range(GH):
                            at = prob_column(kt, h)
                            mm = pe.matmul(pO[g % 2][32 * h:32 * h + 32, kt * P:S],
                                           vaug[:, kt, GH * g + h, :],
                                           probs[:, g % 2, at:at + S - kt * P],
                                           start=(kt == 0), stop=(kt == KT - 1))
                    mm.then_inc(o_full, 1)

                def v_proj(b):
                    for half in range(2):
                        bank = take(half, v_ready, 2 * b + half + 1)
                        for k2 in range(2):
                            kt = 2 * half + k2
                            for n, (c, (s_, m_)) in enumerate((c, p) for c in range(DC) for p in PRODUCTS):
                                mm = pe.matmul(bank[:, k2 * D:(k2 + 1) * D], hT[s_][:, c, kt * P:(kt + 1) * P],
                                               W[m_][:, c, 2 * D:3 * D], start=(n == 0), stop=(n == 5))
                        mm.then_inc(v_full, 1)

                def x_transpose(b):
                    pe.wait_ge(xn_done, 4 * (b + 1))
                    for c in range(DC):
                        bank = take(c, th_done, 4 * b + 2 * c + 2)
                        for kt in range(KT):
                            mm = pe.transpose(bank[:, kt * P:(kt + 1) * P], xn[:, kt, c * P:(c + 1) * P], ident[:])
                        mm.then_inc(xt_full, 1)

                def qk_proj(b):
                    pe.wait_ge(tl_done, 2 * (b + 1))
                    for i in range(4):
                        bank = take(i % 2, qk_ev, 4 * b + i + 1)
                        for n, (c, (s_, m_)) in enumerate((c, p) for c in range(DC) for p in PRODUCTS):
                            mm = pe.matmul(bank[:], W[s_][:, c, i * P:(i + 1) * P], hT[m_][:, c, :],
                                           start=(n == 0), stop=(n == 5))
                        mm.then_inc(qk_full, 1)

                def out_transpose(b):
                    pe.wait_ge(o_free, 4 * (b + 1))
                    for qt in range(KT):
                        bank = take(qt % 2, att_done, 4 * b + qt + 1)
                        for g in range(NG):
                            mm = pe.transpose(bank[:, g * P:(g + 1) * P], oT[:, g, qt * P:(qt + 1) * P], ident[:])
                        mm.then_inc(ot_full, 1)

                def att_transpose(b):
                    pe.wait_ge(att_done, 4 * (b + 1))
                    for c in range(DC):
                        bank = take(c, atl_done, 2 * b + c + 1)
                        for qt in range(KT):
                            mm = pe.transpose(bank[:, qt * P:(qt + 1) * P], att[:, qt, c * P:(c + 1) * P], ident[:])
                        mm.then_inc(at_full, 1)

                def out_proj(b):
                    pe.wait_ge(atl_done, 2 * (b + 1))
                    for half in range(2):
                        bank = take(half, y_ga, 2 * b + half + 1)
                        for q2 in range(2):
                            qt = 2 * half + q2
                            for n, (c, (s_, m_)) in enumerate((c, p) for c in range(DC) for p in PRODUCTS):
                                mm = pe.matmul(bank[:, q2 * D:(q2 + 1) * D], attT[s_][:, c, qt * P:(qt + 1) * P],
                                               W[m_][:, c, 3 * D:4 * D], start=(n == 0), stop=(n == 5))
                        mm.then_inc(y_full, 1)

                def batch(b, first=False, last=False):
                    group(b, 0, (b, 1))
                    v_proj(b)
                    if not first:
                        out_transpose(b - 1)
                    negate(b, 1)
                    values(b, 0)
                    group(b, 1, (b, 2))
                    if not last:
                        x_transpose(b + 1)
                    if not first:
                        att_transpose(b - 1)
                        out_proj(b - 1)
                    if not last:
                        qk_proj(b + 1)
                    negate(b, 2)
                    values(b, 1)
                    group(b, 2, (b, 3))
                    negate(b, 3)
                    values(b, 2)
                    group(b, 3, None if last else (b + 1, 0))
                    if not last:
                        negate(b + 1, 0)
                    values(b, 3)

                x_transpose(0)
                qk_proj(0)
                pe.wait_ge(stk[0], 192)
                for i in range(MAXB):
                    max_bank(0, 0, i)
                negate(0, 0)
                batch(0, first=True)
                with pe.Fori(1, B - 1) as b:
                    read[:] = (mrow_done, 4 * b + 1), (qk_ev, 4 * b + 4)
                    batch(b)
                read[:] = (mrow_done, 4 * (B - 1) + 1), (qk_ev, 4 * B)
                batch(B - 1, last=True)
                out_transpose(B - 1)
                att_transpose(B - 1)
                out_proj(B - 1)

            @block.scalar
            def _(act):
                def exps(b, g):
                    s = 4 * b + g
                    if not (isinstance(s, int) and s < 2):
                        act.wait_ge(o_full, s - 1)
                    for i, (_, at) in enumerate(exp_banks()):
                        act.wait_ge(s_full, 10 * s + i + 1)
                        act.activation(probs[:, g % 2, at:at + 512], pS[i % 2][:], ACT.Exp).then_inc(s_free, 1)

                def max_row(b, g):
                    s = 4 * b + g
                    act.wait_ge(neg_full, s + 1)
                    if not (isinstance(s, int) and s < 2):
                        act.wait_ge(mrow_in, 32 * (s - 1))
                    act.activation(mrow[g % 2][:], pX[0][0:GH, :], ACT.Copy, scale=-1.0).then_inc(mrow_done, 1)

                def out_evac(b, g):
                    act.wait_ge(o_full, 4 * b + g + 1)
                    if g == 0 and not (isinstance(b, int) and b == 0):
                        act.wait_ge(ot_full, 4 * b)
                    act.activation(oT[:, g, :], pO[g % 2][:], ACT.Copy).then_inc(o_free, 1)

                def v_evac(b):
                    for half in range(2):
                        act.wait_ge(v_full, 2 * b + half + 1)
                        if half == 0 and not (isinstance(b, int) and b == 0):
                            act.wait_ge(o_full, 4 * b)
                        act.activation(vaug[:, 2 * half:2 * half + 2, :, 0:HD],
                                       pX[half][:].rearrange("p (k h e) -> p k h e", k=2, h=NH),
                                       ACT.Copy).then_inc(v_ready, 1)

                def x_evac(b):
                    for c in range(DC):
                        act.wait_ge(xt_full, 2 * b + c + 1)
                        if c == 0 and not (isinstance(b, int) and b == 0):
                            act.wait_ge(v_full, 2 * b)
                            act.wait_ge(tl_done, 2 * b)
                        scale, bias = modT[:, 2 + c, bass.ds(b, 1)], modT[:, c, bass.ds(b, 1)]
                        act.activation(ht32[:, c, :], pX[c][:], ACT.Identity, scale=scale, bias=bias).then_inc(th_done, 1)
                        act.activation(hT[0][:, c, :], pX[c][:], ACT.Identity, scale=scale, bias=bias).then_inc(th_done, 1)

                def qk_evac(b):
                    for i in range(4):
                        act.wait_ge(qk_full, 4 * b + i + 1)
                        if i == 0 and not (isinstance(b, int) and b == 0):
                            act.wait_ge(qkl_done, b)
                        act.activation(qk[:, i, :], pX[i % 2][:], ACT.Copy).then_inc(qk_ev, 1)

                def att_high(b):
                    for c in range(DC):
                        act.wait_ge(at_full, 2 * b + c + 1)
                        if c == 0 and not (isinstance(b, int) and b == 0):
                            act.wait_ge(y_full, 2 * b)
                        act.activation(attT[0][:, c, :], pX[c][:], ACT.Copy).then_inc(ath_done, 1)

                def batch(b, first=False, last=False):
                    if not first:
                        out_evac(b - 1, 3)
                    exps(b, 0)
                    v_evac(b)
                    max_row(b, 1)
                    out_evac(b, 0)
                    exps(b, 1)
                    if not last:
                        x_evac(b + 1)
                    if not first:
                        att_high(b - 1)
                    if not last:
                        qk_evac(b + 1)
                    max_row(b, 2)
                    out_evac(b, 1)
                    exps(b, 2)
                    max_row(b, 3)
                    out_evac(b, 2)
                    exps(b, 3)
                    if not last:
                        max_row(b + 1, 0)

                x_evac(0)
                qk_evac(0)
                max_row(0, 0)
                batch(0, first=True)
                with act.Fori(1, B - 1) as b:
                    batch(b)
                batch(B - 1, last=True)
                out_evac(B - 1, 3)
                att_high(B - 1)

            @block.vector
            def _(dve):
                def maxima(b, g):
                    s = 4 * b + g
                    if not (isinstance(s, int) and s < 2):
                        dve.wait_ge(neg_full, s - 1)
                    for i, bank in enumerate(max_banks()):
                        wait_apart(dve, m_full, 10 * s + i + 1)
                        for qt, h, col in bank:
                            w = P * (qt + 1)
                            scores = pM[i % 2][:, col:col + w]
                            ins = dve.tensor_tensor_reduce(
                                out=scores, in0=scores, in1=mask[:, S - w:S],
                                scale=1.0, scalar=-3e38, op0=ALU.add, op1=ALU.max,
                                accum_out=mx[:, g % 2, qt, h:h + 1])
                        ins.then_inc(m_free, 1)

                def ln_stats(b):
                    dve.wait_ge(x_in, 16 * (b + 1))
                    for k in range(KT):
                        ins = dve.bn_stats(stats[:, k, :], xb[:, k, :])
                    ins.then_inc(ln_s, 1)
                    wait_apart(dve, ln_s, 2 * b + 1)
                    for k in range(KT):
                        ins = dve.bn_aggr(mv[:, k, :], stats[:, k, :])
                    ins.then_inc(ln_s, 1)

                def ln_apply(b):
                    dve.wait_ge(ln_s, 2 * b + 2)
                    dve.wait_ge(ln_b, RSQRT_STEPS * (b + 1))
                    if not (isinstance(b, int) and b == 0):
                        dve.wait_ge(xt_full, 2 * b)
                    for k in range(KT):
                        dve.tensor_scalar(xn[:, k, :], xb[:, k, :], mv[:, k, 0:1], rstd[:, k:k + 1],
                                          ALU.subtract, ALU.mult).then_inc(xn_done, 1)

                def rotate(b):
                    dve.wait_ge(swapped, 32 * (b + 1))
                    for j in range(2):
                        dve.tensor_tensor(qk[:, 2 * j:2 * j + 2, :], qk[:, 2 * j:2 * j + 2, :],
                                          rope[:, 2 * j, None, :].broadcast_to([P, 2, S]), ALU.mult).then_inc(rope1, 1)
                    dve.wait_ge(rope1, 2 * b + 2)
                    dve.wait_ge(rope2, 2 * b + 2)
                    dve.tensor_tensor(qk[:], qk[:], qksw[:], ALU.add).then_inc(rope3, 1)
                    dve.wait_ge(rope3, b + 1)
                    if not (isinstance(b, int) and b == 0):
                        dve.wait_ge(bounced, 32 * b)
                    dve.tensor_copy(qkh[:], qk[:]).then_inc(qkh_done, 1)

                def normalise(b):
                    for qt in range(KT):
                        dve.wait_ge(ot_full, 4 * b + qt + 1)
                        o = pX[qt % 2][:].rearrange("p (h e) -> p h e", e=32)
                        dve.reciprocal(rden[:, qt, :], o[:, :, HD]).then_inc(rd_done, 1)
                        dve.wait_ge(rd_done, 4 * b + qt + 1)
                        if qt == 0 and not (isinstance(b, int) and b == 0):
                            dve.wait_ge(at_full, 2 * b)
                        dve.tensor_tensor(att[:, qt, :].rearrange("p (h e) -> p h e", e=HD), o[:, :, 0:HD],
                                          rden[:, qt, :, None].broadcast_to([P, NH, HD]), ALU.mult).then_inc(att_done, 1)

                def att_low(b):
                    for c in range(DC):
                        dve.wait_ge(ath_done, 2 * b + c + 1)
                        dve.tensor_tensor(attT[1][:, c, :], pX[c][:], attT[0][:, c, :].bitcast(F32),
                                          ALU.subtract).then_inc(atl_done, 1)

                def gate(b):
                    dve.wait_ge(aux_in, 32 * (b + 1))
                    if not (isinstance(b, int) and b == 0):
                        dve.wait_ge(x1_done, b)
                    for half in range(2):
                        dve.wait_ge(y_full, 2 * b + half + 1)
                        dve.tensor_tensor(yo[:, 2 * half:2 * half + 2, :], pX[half][:].rearrange("p (k n) -> p k n", k=2),
                                          gab[:, None, :].broadcast_to([P, 2, D]), ALU.mult).then_inc(y_ga, 1)

                def batch(b, first=False, last=False):
                    maxima(b, 1)
                    if not last:
                        ln_stats(b + 1)
                    if not first:
                        normalise(b - 1)
                    if not last:
                        ln_apply(b + 1)
                    maxima(b, 2)
                    if not first:
                        att_low(b - 1)
                        gate(b - 1)
                    maxima(b, 3)
                    if not last:
                        rotate(b + 1)
                        maxima(b + 1, 0)

                ln_stats(0)
                ln_apply(0)
                rotate(0)
                maxima(0, 0)
                batch(0, first=True)
                with dve.Fori(1, B - 1) as b:
                    batch(b)
                batch(B - 1, last=True)
                normalise(B - 1)
                att_low(B - 1)
                gate(B - 1)

            @block.gpsimd
            def _(pool):
                def rsqrt(b):
                    pool.wait_ge(ln_s, 2 * b + 2)
                    if not (isinstance(b, int) and b == 0):
                        wait_apart(pool, xn_done, 4 * b)
                    rsqrt_steps(pool, ln_b, RSQRT_STEPS * b, rstd[:], mv[:, :, 1], nv[:], na[:])

                def low(b):
                    for c in range(DC):
                        pool.wait_ge(th_done, 4 * b + 2 * c + 2)
                        pool.tensor_tensor(hT[1][:, c, :], ht32[:, c, :], hT[0][:, c, :].bitcast(F32),
                                           ALU.subtract).then_inc(tl_done, 1)

                def rotate(b):
                    pool.wait_ge(swapped, 32 * (b + 1))
                    for j in range(2):
                        pool.tensor_tensor(qksw[:, 2 * j:2 * j + 2, :], qksw[:, 2 * j:2 * j + 2, :],
                                           rope[:, 2 * j + 1, None, :].broadcast_to([P, 2, S]), ALU.mult).then_inc(rope2, 1)

                def rotate_low(b):
                    pool.wait_ge(qkh_done, b + 1)
                    pool.tensor_tensor(qkl[:], qk[:], qkh[:].bitcast(F32), ALU.subtract).then_inc(qkl_done, 1)

                def select(b, g):
                    s = 4 * b + g
                    for pair in range(2):
                        wait_apart(pool, s_free, 10 * s + 5 * pair + 5)
                        pp = probs[:, g % 2, pair * PAIRW:(pair + 1) * PAIRW]
                        heads = pp[:, 0:2048].rearrange("p (u n) -> p u n", u=2)
                        for view, pat in (
                            (heads.rearrange("p u (k n) -> p u k n", k=2)[:, :, :, 0:P], [[0, 2], [0, 2], [1, P]]),
                            (heads[:, :, 896:1024], [[0, 2], [1, P]]),
                            (pp[:, 2048:2560].rearrange("p (u n) -> p u n", u=2)[:, :, 0:P], [[0, 2], [1, P]]),
                        ):
                            ins = pool.affine_select(out=view, in_=view, compare_op=ALU.is_ge, fill=0.0, base=0,
                                                     pattern=pat, channel_multiplier=-1)
                        ins.then_inc(sel_done, 1)

                def residual(b):
                    pool.wait_ge(y_ga, 2 * b + 2)
                    if not (isinstance(b, int) and b == 0):
                        wait_apart(pool, x1_out, 16 * b)
                    pool.tensor_tensor(xr[:], xr[:], yo[:], ALU.add).then_inc(x1_done, 1)

                def batch(b, first=False, last=False):
                    select(b, 0)
                    if not last:
                        rsqrt(b + 1)
                    select(b, 1)
                    if not last:
                        low(b + 1)
                    if not first:
                        residual(b - 1)
                    if not last:
                        rotate(b + 1)
                    select(b, 2)
                    if not last:
                        rotate_low(b + 1)
                    select(b, 3)

                rsqrt(0)
                low(0)
                rotate(0)
                rotate_low(0)
                batch(0, first=True)
                with pool.Fori(1, B - 1) as b:
                    batch(b)
                batch(B - 1, last=True)
                residual(B - 1)

            @block.sync
            def _(sp):
                def rows(ap, b):
                    return ap[bass.ds(b * S, S), :].rearrange("(k p) n -> p k n", p=P)

                def load_x(b):
                    if not (isinstance(b, int) and b == 0):
                        sp.wait_ge(xn_done, 4 * b)
                    sp.dma_start(xb[:], rows(d["x"], b)).then_inc(x_in, 16)

                def load_aux(b):
                    if not (isinstance(b, int) and b == 0):
                        wait_apart(sp, x1_out, 16 * b)
                        sp.wait_ge(y_ga, 2 * b)
                    sp.dma_start(xr[:], rows(d["x"], b)).then_inc(aux_in, 16)
                    sp.dma_start(gab[:], d["mod"][bass.ds(b, 1), 2 * D:3 * D].broadcast_to([P, D])).then_inc(aux_in, 16)
                def max_rows(b, g):
                    s = 4 * b + g
                    sp.wait_ge(mrow_done, s + 1)
                    for u in range(2):
                        sp.dma_start(qs[48:128:64, 2 * g + u, :].bitcast(F32), mrow[g % 2][2 * u:2 * u + 2, :].bitcast(F32)).then_inc(mrow_in, 16)

                def swap(b):
                    sp.wait_ge(qk_ev, 4 * (b + 1))
                    if not (isinstance(b, int) and b == 0):
                        sp.wait_ge(rope3, b)
                    for k in range(2):
                        sp.dma_start(qksw[k:P:2, :, :], qk[1 - k:P:2, :, :]).then_inc(swapped, 16)

                def bounce(b):
                    if not (isinstance(b, int) and b == 0):
                        sp.wait_ge(stk[1], 192 * b)
                        sp.wait_ge(stk[0], 192 * b)
                    sp.wait_ge(qkh_done, b + 1)
                    sp.dma_start(d["qk"][0], qkh[:].bitcast(F32)).then_inc(bounced, 16)
                    sp.wait_ge(qkl_done, b + 1)
                    sp.dma_start(d["qk"][1], qkl[:].bitcast(F32)).then_inc(bounced, 16)

                def load_stacks(b, half):
                    if half == 0:
                        sp.wait_ge(bounced, 32 * (b + 1))
                    if not (isinstance(b, int) and b == 0):
                        sp.wait_ge(s_full, 40 * (b - 1) + 20 * half + 20)
                    for tile, which, parts in ((qs, half, (0, 0, 1)), (ks, 2 + half, (0, 1, 0))):
                        for part, hl in enumerate(parts):
                            src = d["qk"][hl, :, which, :].rearrange("(t s e) n -> s e t n", s=2, e=HD)
                            for s in range(2):
                                r = 64 * s + HD * part
                                sp.dma_start(tile[r:r + HD, 4 * half:4 * half + 4, :].bitcast(F32), src[s]).then_inc(stk[half], 16)

                def store(b):
                    sp.wait_ge(x1_done, b + 1)
                    sp.dma_start(rows(d["x1"], b), xr[:]).then_inc(x1_out, 16)

                def batch(b, first=False, last=False):
                    if not last:
                        load_x(b + 1)
                    max_rows(b, 1)
                    max_rows(b, 2)
                    if not last:
                        swap(b + 1)
                    if not first:
                        store(b - 1)
                        load_aux(b)
                    max_rows(b, 3)
                    if not last:
                        bounce(b + 1)
                        load_stacks(b + 1, 0)
                        max_rows(b + 1, 0)
                        load_stacks(b + 1, 1)

                load_x(0)
                load_aux(0)
                swap(0)
                bounce(0)
                load_stacks(0, 0)
                load_stacks(0, 1)
                max_rows(0, 0)
                batch(0, first=True)
                with sp.Fori(1, B - 1) as b:
                    batch(b)
                batch(B - 1, last=True)
                store(B - 1)
                sp.wait_ge(x1_out, 16 * B)


def shared_expert(nc, d, t):
    with ExitStack() as ctx:
        sb = lambda n, s, dt=F32: ctx.enter_context(nc.sbuf_tensor(n, s, dt))
        ps = lambda n: ctx.enter_context(nc.psum_tensor(n, [P, 512], F32))
        sem = lambda n: ctx.enter_context(nc.semaphore(n))
        ident, rgu, rdn, h2all = t["ident"], t["rgu"], t["rdn"], t["h2all"]
        wgu = (sb("wguh", [P, DC, 2 * F], F32R), sb("wgul", [P, DC, 2 * F], F32R))
        wdn = (sb("wdnh", [P, FC, D], F32R), sb("wdnl", [P, FC, D], F32R))
        wr = (sb("wrh", [P, DC, NE], F32R), sb("wrl", [P, DC, NE], F32R))
        room = rdn[:].rearrange("p c e n -> p (c e n)")
        wgu32 = room[:, 0:2 * DC * F].rearrange("p (c n) -> p c n", c=DC)
        wdn32 = room[:, 2 * DC * F:2 * DC * F + FC * D].rearrange("p (c n) -> p c n", c=FC)
        wr32 = sb("wr32", [P, DC, NE])
        xa = sb("xa", [P, KT, D])
        xr = sb("xr2", [P, KT, D])
        bsc = sb("bsc", [P, 2, D])
        bg = sb("bg", [P, D])
        xn = sb("xn2", [P, KT, D])
        h2 = sb("h2", [P, KT, D])
        stats, mv = sb("stats2", [P, KT, 6]), sb("mv2", [P, KT, 2])
        rstd, nv, na = sb("rstd2", [P, KT]), sb("nv2", [P, KT]), sb("na2", [P, KT])
        hT = (sb("h2Th", [P, DC, S], F32R), sb("h2Tl", [P, DC, S], F32R))
        lg, m8 = sb("lg", [P, KT, NE]), sb("m8", [P, KT, 8])
        i8, top = sb("i8", [P, KT, 8], U32), sb("top", [P, KT])
        sg = sb("sg", [P, 2, S])
        hid = sb("hid", [P, 2, S])
        hidT = (sb("hidh", [P, FC, S], F32R), sb("hidl", [P, FC, S], F32R))
        yo = sb("yo2", [P, 2, D])
        pT, pG, pU, pD = ([ps(f"q{n}{i}") for i in range(2)] for n in "TGUD")

        w_in, wr_in, w_high, w_low = sem("w_in"), sem("wr_in"), sem("w_high"), sem("w_low")
        big_in = t["big_in"]
        x_in, bs_in, aux_in = sem("x2_in"), sem("bs_in"), sem("aux2_in")
        ln_s, ln_b, xn_done, xm_done, h2_done = sem("ln2_s"), sem("ln2_b"), sem("xn2_done"), sem("xm_done"), sem("h2_done")
        h2_kept = sem("h2_kept")
        ht_full, hh_done, hl_done = sem("ht_full"), sem("hh_done"), sem("hl_done")
        lg_full, lg_done, top_step, oh_done = sem("lg_full"), sem("lg_done"), sem("top_step"), sem("oh_done")
        g_full, u_full, silu_done, hid_done = sem("g_full"), sem("u_full"), sem("silu_done"), sem("hid_done")
        hidh_done, hidl_done = sem("hidh_done"), sem("hidl_done")
        d_full, y_done, x2_done, x2_out = sem("d_full"), sem("y_done"), sem("x2_done"), sem("x2_out")

        with nc.Block() as block:

            @block.tensor
            def _(pe):
                def transpose(b):
                    pe.wait_ge(h2_done, b + 1)
                    for c in range(DC):
                        if not (isinstance(b, int) and b == 0):
                            if c == 0:
                                pe.wait_ge(lg_done, b)
                            else:
                                pe.wait_ge(hl_done, 2 * b)
                        for k in range(KT):
                            mm = pe.transpose(pT[c][:, k * P:(k + 1) * P], h2[:, k, c * P:(c + 1) * P], ident[:])
                        mm.then_inc(ht_full, 1)

                def logits(b):
                    pe.wait_ge(hl_done, 2 * (b + 1))
                    for k in range(KT):
                        for n, (c, (s_, m_)) in enumerate((c, p) for c in range(DC) for p in PRODUCTS):
                            mm = pe.matmul(pT[0][:, k * NE:(k + 1) * NE], hT[s_][:, c, k * P:(k + 1) * P],
                                           wr[m_][:, c, :], start=(n == 0), stop=(n == 5))
                    mm.then_inc(lg_full, 1)

                def gate_up(b):
                    for m in range(FC):
                        n = FC * b + m
                        for bank, off, free, full in ((pG[m % 2], 0, silu_done, g_full), (pU[m % 2], F, hid_done, u_full)):
                            if not (isinstance(n, int) and n < 2):
                                pe.wait_ge(free, n - 1)
                            for k, (c, (s_, m_)) in enumerate((c, p) for c in range(DC) for p in PRODUCTS):
                                mm = pe.matmul(bank[:], wgu[s_][:, c, off + m * P:off + (m + 1) * P], hT[m_][:, c, :],
                                               start=(k == 0), stop=(k == 5))
                            mm.then_inc(full, 1)

                def down(b):
                    pe.wait_ge(hidl_done, FC * (b + 1))
                    for half in range(2):
                        if not (isinstance(b, int) and b == 0):
                            pe.wait_ge(y_done, 2 * b - 1 + half)
                        for q2 in range(2):
                            q = 2 * half + q2
                            for n, (m, (s_, m_)) in enumerate((m, p) for m in range(FC) for p in PRODUCTS):
                                mm = pe.matmul(pD[half][:, q2 * D:(q2 + 1) * D], hidT[s_][:, m, q * P:(q + 1) * P],
                                               wdn[m_][:, m, :], start=(n == 0), stop=(n == 11))
                        mm.then_inc(d_full, 1)

                def batch(b, last=False):
                    gate_up(b)
                    if not last:
                        transpose(b + 1)
                        logits(b + 1)
                    down(b)

                transpose(0)
                pe.wait_ge(w_low, 3)
                pe.wait_ge(w_high, 3)
                logits(0)
                batch(0)
                with pe.Fori(1, B - 1) as b:
                    batch(b)
                batch(B - 1, last=True)

            @block.scalar
            def _(act):
                def keep(b):
                    act.wait_ge(h2_done, b + 1)
                    act.activation(h2all[:, bass.ds(KT * b, KT), :], h2[:], ACT.Copy).then_inc(h2_kept, 1)

                def high(b):
                    for c in range(DC):
                        act.wait_ge(ht_full, 2 * b + c + 1)
                        if c == 0 and not (isinstance(b, int) and b == 0):
                            act.wait_ge(u_full, FC * b)
                            act.wait_ge(lg_full, b)
                        act.activation(hT[0][:, c, :], pT[c][:], ACT.Copy).then_inc(hh_done, 1)

                def silu(b):
                    for m in range(FC):
                        n = FC * b + m
                        act.wait_ge(g_full, n + 1)
                        if not (isinstance(n, int) and n < 2):
                            act.wait_ge(hid_done, n - 1)
                        act.activation(sg[:, m % 2, :], pG[m % 2][:], ACT.Silu).then_inc(silu_done, 1)
                        act.wait_ge(hid_done, n + 1)
                        if m == 0 and not (isinstance(b, int) and b == 0):
                            act.wait_ge(d_full, 2 * b)
                        act.activation(hidT[0][:, m, :], hid[:, m % 2, :], ACT.Copy).then_inc(hidh_done, 1)

                act.wait_ge(w_in, 32)
                act.activation(wgu[0][:], wgu32, ACT.Copy).then_inc(w_high, 1)
                act.activation(wdn[0][:], wdn32, ACT.Copy).then_inc(w_high, 1)
                act.wait_ge(wr_in, 32)
                act.activation(wr[0][:], wr32[:], ACT.Copy).then_inc(w_high, 1)
                keep(0)
                high(0)
                silu(0)
                keep(1)
                high(1)
                with act.Fori(1, B - 1) as b:
                    silu(b)
                    keep(b + 1)
                    high(b + 1)
                silu(B - 1)

            @block.vector
            def _(dve):
                def layernorm(b):
                    dve.wait_ge(x_in, 16 * (b + 1))
                    for k in range(KT):
                        ins = dve.bn_stats(stats[:, k, :], xa[:, k, :])
                    ins.then_inc(ln_s, 1)
                    wait_apart(dve, ln_s, 2 * b + 1)
                    for k in range(KT):
                        ins = dve.bn_aggr(mv[:, k, :], stats[:, k, :])
                    ins.then_inc(ln_s, 1)
                    dve.wait_ge(ln_s, 2 * b + 2)
                    dve.wait_ge(ln_b, RSQRT_STEPS * (b + 1))
                    if not (isinstance(b, int) and b == 0):
                        dve.wait_ge(h2_done, b)
                    for k in range(KT):
                        dve.tensor_scalar(xn[:, k, :], xa[:, k, :], mv[:, k, 0:1], rstd[:, k:k + 1],
                                          ALU.subtract, ALU.mult).then_inc(xn_done, 1)
                    dve.wait_ge(xn_done, 4 * (b + 1))
                    dve.wait_ge(bs_in, 16 * (b + 1))
                    dve.tensor_tensor(xn[:], xn[:], bsc[:, 1, None, :].broadcast_to([P, KT, D]),
                                      ALU.mult).then_inc(xm_done, 1)

                def low(b):
                    for c in range(DC):
                        dve.wait_ge(hh_done, 2 * b + c + 1)
                        dve.tensor_tensor(hT[1][:, c, :], pT[c][:], hT[0][:, c, :].bitcast(F32),
                                          ALU.subtract).then_inc(hl_done, 1)

                def choose(b):
                    dve.wait_ge(lg_full, b + 1)
                    dve.tensor_copy(lg[:], pT[0][:, 0:KT * NE].rearrange("p (k e) -> p k e", e=NE)).then_inc(lg_done, 1)
                    wait_apart(dve, lg_done, b + 1)
                    for k in range(KT):
                        ins = dve.max(m8[:, k, :], lg[:, k, :])
                    ins.then_inc(top_step, 1)
                    wait_apart(dve, top_step, 3 * b + 1)
                    for k in range(KT):
                        ins = dve.max_index(i8[:, k, :], m8[:, k, :], lg[:, k, :])
                    ins.then_inc(top_step, 1)
                    dve.wait_ge(top_step, 3 * b + 2)
                    dve.tensor_copy(t["best"][:, bass.ds(KT * b, KT)], m8[:, :, 0])
                    dve.tensor_copy(top[:], i8[:, :, 0]).then_inc(top_step, 1)
                    dve.wait_ge(top_step, 3 * b + 3)
                    dve.tensor_tensor(t["onehot"][:, bass.ds(KT * b, KT), :],
                                      top[:, :, None].broadcast_to([P, KT, NE]),
                                      t["experts"][:, None, :].broadcast_to([P, KT, NE]), ALU.is_equal).then_inc(oh_done, 1)

                def hidden(b):
                    for m in range(FC):
                        n = FC * b + m
                        dve.wait_ge(silu_done, n + 1)
                        dve.wait_ge(u_full, n + 1)
                        if not (isinstance(n, int) and n < 2):
                            dve.wait_ge(hidl_done, n - 1)
                        dve.tensor_tensor(hid[:, m % 2, :], pU[m % 2][:], sg[:, m % 2, :], ALU.mult).then_inc(hid_done, 1)

                def gate(b):
                    dve.wait_ge(aux_in, 32 * (b + 1))
                    for half in range(2):
                        dve.wait_ge(d_full, 2 * b + half + 1)
                        if half == 1 or not (isinstance(b, int) and b == 0):
                            dve.wait_ge(x2_done, 2 * b + half)
                        dve.tensor_tensor(yo[:], pD[half][:].rearrange("p (k n) -> p k n", k=2),
                                          bg[:, None, :].broadcast_to([P, 2, D]), ALU.mult).then_inc(y_done, 1)

                layernorm(0)
                low(0)
                choose(0)
                hidden(0)
                layernorm(1)
                low(1)
                choose(1)
                gate(0)
                with dve.Fori(1, B - 1) as b:
                    hidden(b)
                    layernorm(b + 1)
                    low(b + 1)
                    choose(b + 1)
                    gate(b)
                hidden(B - 1)
                gate(B - 1)

            @block.gpsimd
            def _(pool):
                def norm(b):
                    pool.wait_ge(ln_s, 2 * b + 2)
                    if not (isinstance(b, int) and b == 0):
                        wait_apart(pool, xn_done, 4 * b)
                    rsqrt_steps(pool, ln_b, RSQRT_STEPS * b, rstd[:], mv[:, :, 1], nv[:], na[:])
                    pool.wait_ge(xm_done, b + 1)
                    if not (isinstance(b, int) and b == 0):
                        pool.wait_ge(ht_full, 2 * b)
                        pool.wait_ge(h2_kept, b)
                    pool.tensor_tensor(h2[:], xn[:], bsc[:, 0, None, :].broadcast_to([P, KT, D]), ALU.add).then_inc(h2_done, 1)

                def low(b):
                    for m in range(FC):
                        pool.wait_ge(hidh_done, FC * b + m + 1)
                        pool.tensor_tensor(hidT[1][:, m, :], hid[:, m % 2, :], hidT[0][:, m, :].bitcast(F32),
                                           ALU.subtract).then_inc(hidl_done, 1)

                def residual(b):
                    for half in range(2):
                        pool.wait_ge(y_done, 2 * b + half + 1)
                        rows = xr[:, 2 * half:2 * half + 2, :]
                        pool.tensor_tensor(rows, rows, yo[:], ALU.add).then_inc(x2_done, 1)

                norm(0)
                pool.wait_ge(w_high, 3)
                pool.tensor_tensor(wgu[1][:], wgu32, wgu[0][:].bitcast(F32), ALU.subtract).then_inc(w_low, 1)
                pool.tensor_tensor(wdn[1][:], wdn32, wdn[0][:].bitcast(F32), ALU.subtract).then_inc(w_low, 1)
                pool.tensor_tensor(wr[1][:], wr32[:], wr[0][:].bitcast(F32), ALU.subtract).then_inc(w_low, 1)
                low(0)
                norm(1)
                residual(0)
                with pool.Fori(1, B - 1) as b:
                    low(b)
                    norm(b + 1)
                    residual(b)
                low(B - 1)
                residual(B - 1)

            @block.sync
            def _(sp):
                def rows(ap, b):
                    return ap[bass.ds(b * S, S), :].rearrange("(k p) n -> p k n", p=P)

                def load_x(b):
                    if not (isinstance(b, int) and b == 0):
                        sp.wait_ge(xn_done, 4 * b)
                    sp.dma_start(xa[:], rows(d["x1"], b)).then_inc(x_in, 16)
                    if not (isinstance(b, int) and b == 0):
                        sp.wait_ge(h2_done, b)
                    sp.dma_start(bsc[:].rearrange("p k n -> p (k n)"),
                                 d["mod"][bass.ds(b, 1), 3 * D:5 * D].broadcast_to([P, 2 * D])).then_inc(bs_in, 16)

                def load_aux(b):
                    if not (isinstance(b, int) and b == 0):
                        wait_apart(sp, x2_out, 16 * b)
                        sp.wait_ge(y_done, 2 * b)
                    sp.dma_start(xr[:], rows(d["x1"], b)).then_inc(aux_in, 16)
                    sp.dma_start(bg[:], d["mod"][bass.ds(b, 1), 5 * D:6 * D].broadcast_to([P, D])).then_inc(aux_in, 16)

                def store(b):
                    sp.wait_ge(x2_done, 2 * b + 2)
                    sp.dma_start(rows(d["x2"], b), xr[:]).then_inc(x2_out, 16)

                load_x(0)
                sp.dma_start(wgu32, d["sgu"].rearrange("(c p) n -> p c n", p=P)).then_inc(w_in, 16)
                sp.dma_start(wdn32, d["sdn"].rearrange("(c p) n -> p c n", p=P)).then_inc(w_in, 16)
                sp.dma_start(wr32[:], d["wr"].rearrange("(c p) n -> p c n", p=P)).then_inc(wr_in, 16)
                sp.dma_start(t["experts"][:], d["c_experts"]).then_inc(wr_in, 16)
                load_aux(0)
                for c in range(DC):
                    sp.dma_start(rgu[:, c], d["rgu"][c * P:(c + 1) * P]).then_inc(big_in, 16)
                sp.wait_ge(w_low, 3)
                for c in range(FC):
                    sp.dma_start(rdn[:, c], d["rdn"][c * P:(c + 1) * P]).then_inc(big_in, 16)
                load_x(1)
                store(0)
                load_aux(1)
                with sp.Fori(1, B - 1) as b:
                    load_x(b + 1)
                    store(b)
                    load_aux(b + 1)
                store(B - 1)
                sp.wait_ge(x2_out, 16 * B)
                sp.wait_ge(big_in, 16 * (DC + FC))
                sp.wait_ge(wr_in, 32)


def route(nc, d, t):
    with ExitStack() as ctx:
        sb = lambda n, s, dt=F32: ctx.enter_context(nc.sbuf_tensor(n, s, dt))
        sem = lambda n: ctx.enter_context(nc.semaphore(n))
        onehot, best, h2all = t["onehot"], t["best"], t["h2all"]
        before = sb("before", [P, P])
        beforeb, onesb = sb("beforeb", [P, P], BF16), sb("onesb", [P, P], BF16)
        ohb = sb("ohb", [P, NT, NE], BF16)
        starts = sb("starts", [P, 40, NE])
        ones = sb("ones", [P, NT])
        count = sb("count", [P, NT, NE])
        upto = sb("upto", [P, NT, NE])
        over = sb("over", [P, NE, NT])
        tiles, ends, base = sb("tiles", [P, NE]), sb("ends", [P, NE]), sb("base", [P, NE])
        slot, slotf = sb("slot", [P, NT, NE]), sb("slotf", [P, NT])
        past, eidf = sb("past", [P, 40, NE]), sb("eidf", [P, 40])
        score = sb("score", [P, NT])
        pR = ctx.enter_context(nc.psum_tensor("pR", [P, 512], F32))
        pC = ctx.enter_context(nc.psum_tensor("pC", [P, 512], F32))
        c_in, r, mm_done, ex, sc_done, scaled = sem("c3_in"), sem("r_step"), sem("r_mm"), sem("r_exp"), sem("score_done"), sem("scaled")
        scattered = sem("scattered")
        with nc.Block() as block:

            @block.sync
            def _(sp):
                sp.dma_start(before[:], d["c_before"]).then_inc(c_in, 16)
                sp.dma_start(starts[:], d["c_starts"]).then_inc(c_in, 16)

            @block.tensor
            def _(pe):
                pe.wait_ge(r, 4)
                pe.matmul(pR[:, 0:NT * NE], beforeb[:], ohb[:], start=True, stop=True).then_inc(mm_done, 1)
                pe.matmul(pC[:, 0:NT * NE], onesb[:], ohb[:], start=True, stop=True).then_inc(mm_done, 1)

            @block.scalar
            def _(act):
                act.activation(score[:], best[:], ACT.Exp, scale=-1.0).then_inc(ex, 1)

            @block.vector
            def _(dve):
                n = 4

                def then(ins):
                    nonlocal n
                    n += 1
                    ins.then_inc(r, 1)
                    dve.wait_ge(r, n)

                dve.memset(onesb[:], 1.0).then_inc(r, 1)
                dve.memset(ones[:], 1.0).then_inc(r, 1)
                dve.tensor_copy(ohb[:], onehot[:]).then_inc(r, 1)
                dve.wait_ge(c_in, 32)
                dve.tensor_copy(beforeb[:], before[:]).then_inc(r, 1)
                dve.wait_ge(r, 4)
                dve.wait_ge(ex, 1)
                then(dve.tensor_scalar(score[:], score[:], 1.0, None, ALU.add))
                dve.reciprocal(score[:], score[:]).then_inc(sc_done, 1)
                dve.wait_ge(mm_done, 2)
                then(dve.tensor_copy(count[:], pC[:, 0:NT * NE].rearrange("p (k e) -> p k e", e=NE)))
                for e in range(NE):
                    ins = dve.tensor_tensor_scan(upto[:, :, e], ones[:], count[:, :, e], 0.0, ALU.mult, ALU.add)
                then(ins)
                then(dve.tensor_tensor(over[:], upto[:, NT - 1, :, None].broadcast_to([P, NE, NT]),
                                       starts[:, 0:NT, 0][:, None, :].broadcast_to([P, NE, NT]), ALU.is_gt))
                then(dve.tensor_reduce(tiles[:], over[:], AX.X, ALU.add))
                then(dve.tensor_tensor_scan(ends[:], ones[:, 0:NE], tiles[:], 0.0, ALU.mult, ALU.add))
                then(dve.tensor_tensor(base[:], ends[:], tiles[:], ALU.subtract))
                then(dve.tensor_scalar(base[:], base[:], float(P), None, ALU.mult))
                then(dve.tensor_scalar(ends[:], ends[:], float(P), None, ALU.mult))
                then(dve.tensor_tensor(slot[:], pR[:, 0:NT * NE].rearrange("p (k e) -> p k e", e=NE), upto[:], ALU.add))
                then(dve.tensor_tensor(slot[:], slot[:], count[:], ALU.subtract))
                then(dve.tensor_tensor(slot[:], slot[:], base[:, None, :].broadcast_to([P, NT, NE]), ALU.add))
                then(dve.tensor_tensor(slot[:], slot[:], onehot[:], ALU.mult))
                then(dve.tensor_reduce(slotf[:], slot[:], AX.X, ALU.add))
                then(dve.tensor_copy(t["slots"][:], slotf[:]))
                then(dve.tensor_tensor(past[:], ends[:, None, :].broadcast_to([P, 40, NE]), starts[:], ALU.is_le))
                then(dve.tensor_reduce(eidf[:], past[:], AX.X, ALU.add))
                then(dve.tensor_scalar(eidf[:], eidf[:], float(NE - 1), None, ALU.min))
                then(dve.tensor_copy(t["eid"][:], eidf[:]))
                dve.wait_ge(sc_done, 1)
                for k in range(NT):
                    dve.tensor_scalar(h2all[:, k, :], h2all[:, k, :], score[:, k:k + 1], None, ALU.mult).then_inc(scaled, 1)

            @block.gpsimd
            def _(pool):
                for k in range(NT):
                    pool.wait_ge(scaled, k + 1)
                    pool.indirect_dma_start(
                        out=d["sorted"], out_offset=bass.IndirectOffsetOnAxis(ap=t["slots"][:, k:k + 1].bitcast(U32), axis=0),
                        in_=h2all[:, k, :], in_offset=None).then_inc(scattered, 16)
                pool.wait_ge(scattered, 16 * NT)


def routed_experts(nc, d, t):
    with ExitStack() as ctx:
        sb = lambda n, s, dt=F32: ctx.enter_context(nc.sbuf_tensor(n, s, dt))
        ps = lambda n: ctx.enter_context(nc.psum_tensor(n, [P, 512], F32))
        sem = lambda n: ctx.enter_context(nc.semaphore(n))
        ident, rgu, rdn, eid = t["ident"], t["rgu"], t["rdn"], t["eid"]
        xs = sb("xs", [P, 2, D])
        xT = sb("xT", [P, 2, DC, P])
        sg = sb("sg4", [P, 2, F])
        hid = sb("hid4", [P, 2, F])
        hT = sb("hT4", [P, 2, FC, P])
        y = sb("y4", [P, 2, D])
        pX, pH = ps("rX"), ps("rH")
        pG, pU, pY = ([ps(f"r{n}{i}") for i in range(2)] for n in "GUY")
        xs_in = [sem(f"xs_in{k}") for k in range(2)]
        y_out = [sem(f"y4_out{k}") for k in range(2)]
        xt_full, xt_done = sem("xt4_full"), sem("xt4_done")
        g_full, u_full, silu_done, hid_done = sem("g4_full"), sem("u4_full"), sem("silu4"), sem("hid4")
        h_full, h_done, y_full, y_done = sem("h4_full"), sem("h4_done"), sem("y4_full"), sem("y4_done")
        early = lambda n, k: isinstance(n, int) and n < k

        with nc.Block() as block:

            @block.tensor
            def _(pe):
                def x_transpose(s, k):
                    pe.wait_ge(xs_in[k], 8 * (s - k) + 16)
                    if not early(s, 1):
                        pe.wait_ge(xt_done, s)
                    for c in range(DC):
                        mm = pe.transpose(pX[:, c * P:(c + 1) * P], xs[:, k, c * P:(c + 1) * P], ident[:])
                    mm.then_inc(xt_full, 1)

                def gate_up(s, k):
                    e = pe.value_load(eid[0:1, bass.ds(s, 1)], min_val=0, max_val=NE - 1)
                    pe.wait_ge(xt_done, s + 1)
                    for bank, off, free, full in ((pG[k], 0, silu_done, g_full), (pU[k], F, hid_done, u_full)):
                        if not early(s, 2):
                            pe.wait_ge(free, s - 1)
                        for c in range(DC):
                            mm = pe.matmul(bank[:], xT[:, k, c, :],
                                           rgu[:, c, bass.ds(e, 1), off:off + F].rearrange("p o n -> p (o n)"),
                                           start=(c == 0), stop=(c == DC - 1))
                        mm.then_inc(full, 1)
                    return e

                def h_transpose(s, k):
                    pe.wait_ge(hid_done, s + 1)
                    if not early(s, 1):
                        pe.wait_ge(h_done, s)
                    for m in range(FC):
                        mm = pe.transpose(pH[:, m * P:(m + 1) * P], hid[:, k, m * P:(m + 1) * P], ident[:])
                    mm.then_inc(h_full, 1)

                def down(s, k):
                    e = pe.value_load(eid[0:1, bass.ds(s, 1)], min_val=0, max_val=NE - 1)
                    pe.wait_ge(h_done, s + 1)
                    if not early(s, 2):
                        pe.wait_ge(y_done, s - 1)
                    for m in range(FC):
                        mm = pe.matmul(pY[k][:, 0:D], hT[:, k, m, :],
                                       rdn[:, m, bass.ds(e, 1), :].rearrange("p o n -> p (o n)"),
                                       start=(m == 0), stop=(m == FC - 1))
                    mm.then_inc(y_full, 1)

                def step(s, k):
                    x_transpose(s + 1, 1 - k)
                    h_transpose(s, k)
                    gate_up(s + 1, 1 - k)
                    down(s, k)

                x_transpose(0, 0)
                gate_up(0, 0)
                step(0, 0)
                step(1, 1)
                with pe.Fori(1, ST // 2) as i:
                    step(2 * i, 0)
                    step(2 * i + 1, 1)
                h_transpose(ST - 1, 0)
                down(ST - 1, 0)

            @block.scalar
            def _(act):
                def x_evac(s, k):
                    act.wait_ge(xt_full, s + 1)
                    if not early(s, 2):
                        act.wait_ge(u_full, s - 1)
                    act.activation(xT[:, k], pX[:, 0:D].rearrange("p (c n) -> p c n", c=DC), ACT.Copy).then_inc(xt_done, 1)

                def silu(s, k):
                    act.wait_ge(g_full, s + 1)
                    if not early(s, 2):
                        act.wait_ge(hid_done, s - 1)
                    act.activation(sg[:, k, :], pG[k][:], ACT.Silu).then_inc(silu_done, 1)

                def y_evac(s, k):
                    act.wait_ge(y_full, s + 1)
                    if not early(s, 2):
                        act.wait_ge(y_out[k], 8 * (s - k))
                    act.activation(y[:, k, :], pY[k][:, 0:D], ACT.Copy).then_inc(y_done, 1)

                def step(s, k):
                    x_evac(s + 1, 1 - k)
                    silu(s + 1, 1 - k)
                    y_evac(s, k)

                x_evac(0, 0)
                silu(0, 0)
                step(0, 0)
                step(1, 1)
                with act.Fori(1, ST // 2) as i:
                    step(2 * i, 0)
                    step(2 * i + 1, 1)
                y_evac(ST - 1, 0)

            @block.vector
            def _(dve):
                def hidden(s, k):
                    dve.wait_ge(silu_done, s + 1)
                    dve.wait_ge(u_full, s + 1)
                    if not early(s, 2):
                        dve.wait_ge(h_full, s - 1)
                    dve.tensor_tensor(hid[:, k, :], pU[k][:], sg[:, k, :], ALU.mult).then_inc(hid_done, 1)

                def h_evac(s, k):
                    dve.wait_ge(h_full, s + 1)
                    if not early(s, 2):
                        dve.wait_ge(y_full, s - 1)
                    dve.tensor_copy(hT[:, k], pH[:].rearrange("p (m n) -> p m n", m=FC)).then_inc(h_done, 1)

                def step(s, k):
                    h_evac(s, k)
                    hidden(s + 1, 1 - k)

                hidden(0, 0)
                step(0, 0)
                step(1, 1)
                with dve.Fori(1, ST // 2) as i:
                    step(2 * i, 0)
                    step(2 * i + 1, 1)
                h_evac(ST - 1, 0)

            @block.sync
            def _(sp):
                def load(s, k):
                    if not early(s, 2):
                        sp.wait_ge(xt_full, s - 1)
                    sp.dma_start(xs[:, k, :], d["sorted"][bass.ds(s * P, P), :]).then_inc(xs_in[k], 16)

                def store(s, k):
                    sp.wait_ge(y_done, s + 1)
                    sp.dma_start(d["ysorted"][bass.ds(s * P, P), :], y[:, k, :]).then_inc(y_out[k], 16)

                load(0, 0)
                load(1, 1)
                with sp.Fori(0, ST // 2) as i:
                    load(2 * i + 2, 0)
                    store(2 * i, 0)
                    if True:
                        load(2 * i + 3, 1)
                    store(2 * i + 1, 1)
                store(ST - 1, 0)
                sp.wait_ge(y_out[0], 16 * (ST // 2 + 1))
                sp.wait_ge(y_out[1], 16 * (ST // 2))


def combine(nc, d, t):
    with ExitStack() as ctx:
        sb = lambda n, s, dt=F32: ctx.enter_context(nc.sbuf_tensor(n, s, dt))
        sem = lambda n: ctx.enter_context(nc.semaphore(n))
        yg = sb("yg", [P, NT, D])
        x2 = sb("x2", [P, NT, D])
        bg = sb("bg5", [P, B, D])
        g_in, x_in, b_in, gated, summed, out_s = sem("g5_in"), sem("x5_in"), sem("b5_in"), sem("gated"), sem("summed"), sem("out_stored")
        g_in = [sem(f"g5_in{b}") for b in range(B)]
        with nc.Block() as block:

            @block.gpsimd
            def _(pool):
                for k in range(NT):
                    pool.indirect_dma_start(
                        out=yg[:, k, :], out_offset=None, in_=d["ysorted"],
                        in_offset=bass.IndirectOffsetOnAxis(ap=t["slots"][:, k:k + 1].bitcast(U32), axis=0),
                    ).then_inc(g_in[k // KT], 16)

            @block.sync
            def _(sp):
                sp.dma_start(bg[:], d["mod"][:, 5 * D:6 * D][None].broadcast_to([P, B, D])).then_inc(b_in, 16)
                sp.dma_start(x2[:], d["x2"].rearrange("(k p) n -> p k n", p=P)).then_inc(x_in, 16)
                for b in range(B):
                    sp.wait_ge(summed, b + 1)
                    sp.dma_start(d["out"][b * S:(b + 1) * S, :].rearrange("(k p) n -> p k n", p=P),
                                 x2[:, b * KT:(b + 1) * KT, :]).then_inc(out_s, 16)
                sp.wait_ge(out_s, 16 * B)

            @block.vector
            def _(dve):
                dve.wait_ge(b_in, 16)
                dve.wait_ge(x_in, 16)
                for b in range(B):
                    rows = slice(b * KT, (b + 1) * KT)
                    dve.wait_ge(g_in[b], 16 * KT)
                    dve.tensor_tensor(yg[:, rows, :], yg[:, rows, :], bg[:, b, None, :].broadcast_to([P, KT, D]),
                                      ALU.mult).then_inc(gated, 1)
                    dve.wait_ge(gated, b + 1)
                    dve.tensor_tensor(x2[:, rows, :], x2[:, rows, :], yg[:, rows, :], ALU.add).then_inc(summed, 1)


def program(nc, d):
    with ExitStack() as whole:
        keep = lambda n, s, dt=F32: whole.enter_context(nc.sbuf_tensor(n, s, dt))
        t = {"ident": keep("ident", [P, P]), "slots": keep("slots", [P, NT], I32), "eid": keep("eid", [P, 40], I32),
             "best": keep("best", [P, NT]), "onehot": keep("onehot", [P, NT, NE]), "experts": keep("experts", [P, NE]),
             "big_in": whole.enter_context(nc.semaphore("big_in"))}
        with ExitStack() as ctx:
            sb = lambda n, s, dt=F32: ctx.enter_context(nc.sbuf_tensor(n, s, dt))
            t |= {
                "wh": sb("wh", [P, DC, 4 * D], F32R), "wl": sb("wl", [P, DC, 4 * D], F32R),
                "rope": sb("rope", [P, 4, S]), "mask": sb("mask", [P, S]),
                "modT": sb("modT", [P, 4, B]),
                "qs": sb("qs", [P, NH // 2, S], F32R), "ks": sb("ks", [P, NH // 2, S], F32R),
                "vaug": sb("vaug", [P, KT, NH, 32]),
            }
            setup(nc, d, t)
            attention(nc, d, t)
        with ExitStack() as ctx:
            sb = lambda n, s, dt=F32: ctx.enter_context(nc.sbuf_tensor(n, s, dt))
            t |= {"rgu": sb("rgu", [P, DC, NE, 2 * F]), "rdn": sb("rdn", [P, FC, NE, D])}
            with ExitStack() as rows:
                t["h2all"] = rows.enter_context(nc.sbuf_tensor("h2all", [P, NT, D], F32))
                shared_expert(nc, d, t)
                route(nc, d, t)
            routed_experts(nc, d, t)
        combine(nc, d, t)


def kernel(**inputs):
    import numpy as _np
    import concourse.bacc as _bacc
    from concourse.bass_utils import run_bass_kernel_spmd as _run

    i = {k: _np.asarray(v) for k, v in inputs.items()}
    arrays = {
        "x": i["L0_attn_x"].reshape(B * S, D),
        "cT": i["L0_c"].T, "wmod": i["L0_wmod"],
        "qw": i["L0_attn_qw"], "kw": i["L0_attn_kw"], "vw": i["L0_attn_vw"], "ow": i["L0_attn_ow"],
        "wr": i["L0_ffn_gate_w"].T,
        "sgu": _np.concatenate([i["L0_ffn_shared_gate"], i["L0_ffn_shared_up"]], axis=0).T,
        "sdn": i["L0_ffn_shared_down"].T,
        "rgu": _np.concatenate([i["L0_ffn_r_gate"], i["L0_ffn_r_up"]], axis=1).transpose(2, 0, 1),
        "rdn": i["L0_ffn_r_down"].transpose(2, 0, 1),
        **constants(),
    }
    arrays = {f"in_{k}": _np.ascontiguousarray(v) for k, v in arrays.items()}
    nc = _bacc.Bacc("TRN2", target_bir_lowering=False, num_devices=1)
    d = {k[3:]: nc.dram_tensor(k, v.shape, mybir.dt.from_np(v.dtype), kind="ExternalInput").ap()
         for k, v in arrays.items()}
    for name, shape in (("mod", (B, 6 * D)), ("qk", (2, P, 4, S)), ("x1", (B * S, D)), ("x2", (B * S, D)),
                        ("sorted", ((ST + 1) * P, D)), ("ysorted", (ST * P, D))):
        d[name] = nc.dram_tensor(f"scratch_{name}", shape, F32, kind="Internal").ap()
    d["out"] = nc.dram_tensor("out_0", (B * S, D), F32, kind="ExternalOutput").ap()
    program(nc, d)
    r = _run(nc, [arrays], core_ids=[0])
    return r.results[0]["out_0"].reshape(B, S, D)
```

```python
from contextlib import ExitStack

import concourse.bass as bass
import numpy as np
from concourse import mybir

F32 = mybir.dt.float32
F32R = mybir.dt.float32r
BF16 = mybir.dt.bfloat16
I32 = mybir.dt.int32
U32 = mybir.dt.uint32
ALU = mybir.AluOpType
ACT = mybir.ActivationFunctionType
AX = mybir.AxisListType

P = 128
B, S, D = 8, 512, 256
NH, HD = 16, 16
F, NE = 512, 8
KT = S // P
DC = D // P
FC = F // P
NT = B * KT
ST = NT + NE - 1
GH = 4
NG = NH // GH
PAIRW = 2 * 1280
MAXB = 10
EXPB = 10
EPS = 1e-5
NEG = -1e10


def constants():
    row = np.arange(P) % HD
    inv = (1.0 / np.float32(10000.0) ** (np.arange(0, HD, 2, dtype=np.float32) / HD)).astype(np.float32)
    ang = (np.arange(S, dtype=np.float32)[None, :] * inv[row // 2][:, None]).astype(np.float32)
    cos, sin = np.cos(ang), np.sin(ang) * np.where(row % 2 == 0, -1.0, 1.0)[:, None]
    rope = np.stack([cos, sin], axis=1).astype(np.float32)
    ident = np.eye(P, dtype=np.float32)
    mask = np.zeros((P, S), np.float32)
    mask[:, S - P:] = np.where(np.arange(P)[None, :] > np.arange(P)[:, None], NEG, 0.0)
    before = (np.arange(P)[:, None] < np.arange(P)[None, :]).astype(np.float32)
    experts = np.broadcast_to(np.arange(NE, dtype=np.float32), (P, NE))
    sel = np.zeros((4, P, 4, P), np.float32)
    for pair in range(4):
        for s_ in range(2):
            for e in range(HD):
                for kind, parts in enumerate(((0, 1), (2,), (0, 2), (1,))):
                    for part in parts:
                        sel[kind, 32 * pair + HD * s_ + e, pair, 64 * s_ + HD * part + e] = 1.0
    ones = np.zeros((P, 1), np.float32)
    ones[48::64] = 1.0
    starts = np.broadcast_to(P * np.arange(40, dtype=np.float32)[:, None], (P, 40, NE))
    return {
        "c_rope": rope, "c_ident": ident, "c_mask": mask, "c_before": before,
        "c_sel": np.ascontiguousarray(sel.transpose(1, 0, 2, 3)), "c_ones": ones,
        "c_experts": np.ascontiguousarray(experts), "c_starts": np.ascontiguousarray(starts),
    }


RSQRT_STEPS = 14


def wait_apart(eng, sem, value):
    eng.wait_ge(sem, value)
    if not isinstance(value, int):
        eng.nop(nofuse=True)


def rsqrt_steps(pool, step, base, out, var, v, a):
    n = 0

    def then(ins):
        nonlocal n
        n += 1
        ins.then_inc(step, 1)
        wait_apart(pool, step, base + n)

    then(pool.tensor_scalar(v, var, EPS, None, ALU.add))
    then(pool.tensor_scalar(out.bitcast(I32), v.bitcast(I32), -0.5, float(0x5F3759DF), ALU.mult, ALU.add))
    for _ in range(3):
        then(pool.tensor_tensor(a, out, out, ALU.mult))
        then(pool.tensor_tensor(a, a, v, ALU.mult))
        then(pool.tensor_scalar(a, a, -0.5, 1.5, ALU.mult, ALU.add))
        then(pool.tensor_tensor(out, out, a, ALU.mult))
    assert n == RSQRT_STEPS


def setup(nc, d, t):
    with ExitStack() as ctx:
        sb = lambda n, s, dt=F32: ctx.enter_context(nc.sbuf_tensor(n, s, dt))
        sem = lambda n: ctx.enter_context(nc.semaphore(n))
        w32 = sb("w32", [P, DC, 4 * D])
        sel32 = sb("sel32", [P, 4, 4, P])
        wmod = sb("wmod", [P, DC, 6 * D])
        cT = sb("cT", [P, DC, B])
        ce = sb("ce", [P, DC, B])
        sc = sb("sc", [P, DC, B])
        modrow = sb("modrow", [B, 6 * D])
        sgn = sb("sgn", [B, 2, D])
        zero = sb("zero", [P, 20 * D])
        pm = [ctx.enter_context(nc.psum_tensor(f"pm{i}", [P, 512], F32)) for i in range(3)]
        pt = ctx.enter_context(nc.psum_tensor("pt", [P, 512], F32))
        loaded, cloaded, split = sem("set_loaded"), sem("set_cloaded"), sem("set_split")
        step, scdone, rows, cols = sem("set_step"), sem("set_sc"), sem("set_rows"), sem("set_cols")
        ex, rowsb, stored = sem("set_exp"), sem("set_rowsb"), sem("set_stored")
        tables, sel_in = sem("set_tables"), sem("sel_in")
        with nc.Block() as block:

            @block.sync
            def _(sp):
                sp.dma_start(cT[:], d["cT"].rearrange("(c p) b -> p c b", p=P)).then_inc(cloaded, 16)
                sp.dma_start(wmod[:], d["wmod"].rearrange("(c p) n -> p c n", p=P)).then_inc(cloaded, 16)
                for i, n in enumerate(("qw", "kw", "vw", "ow")):
                    sp.dma_start(w32[:, :, i * D:(i + 1) * D],
                                 d[n].rearrange("(c p) n -> p c n", p=P)).then_inc(loaded, 16)
                sp.dma_start(t["rope"][:], d["c_rope"]).then_inc(tables, 16)
                sp.dma_start(t["ident"][:], d["c_ident"]).then_inc(tables, 16)
                sp.dma_start(t["mask"][:], d["c_mask"]).then_inc(tables, 16)
                sp.dma_start(t["ones"][:], d["c_ones"]).then_inc(tables, 16)
                sp.dma_start(sel32[:], d["c_sel"]).then_inc(sel_in, 16)
                sp.wait_ge(rowsb, 3)
                sp.dma_start(d["mod"], modrow[:]).then_inc(stored, 16)
                sp.wait_ge(step, 1)
                for i in range(2):
                    sp.dma_start(d["sorted"][i * 20 * P:(i + 1) * 20 * P, :].rearrange("(p r) n -> p (r n)", p=P),
                                 zero[:]).then_inc(stored, 16)
                sp.wait_ge(stored, 48)
                sp.wait_ge(tables, 64)

            @block.scalar
            def _(act):
                act.wait_ge(cloaded, 32)
                act.activation(ce[:], cT[:], ACT.Exp, scale=-1.0).then_inc(ex, 1)
                act.wait_ge(sel_in, 16)
                act.activation(t["sel"][:], sel32[:], ACT.Copy)

            @block.vector
            def _(dve):
                dve.wait_ge(ex, 1)
                dve.tensor_scalar(ce[:], ce[:], 1.0, None, ALU.add).then_inc(scdone, 1)
                dve.wait_ge(scdone, 1)
                dve.reciprocal(ce[:], ce[:]).then_inc(scdone, 1)
                dve.wait_ge(scdone, 2)
                dve.tensor_tensor(sc[:], cT[:], ce[:], ALU.mult).then_inc(scdone, 1)
                dve.wait_ge(loaded, 64)
                dve.tensor_copy(t["wh"][:], w32[:]).then_inc(split, 1)
                dve.wait_ge(cols, 1)
                dve.tensor_copy(t["modT"][:, 0:2, :], pt[:, 0:16].rearrange("p (k b) -> p k b", b=B)).then_inc(split, 1)
                dve.tensor_scalar(t["modT"][:, 2:4, :], pt[:, 16:32].rearrange("p (k b) -> p k b", b=B),
                                  1.0, None, ALU.add).then_inc(split, 1)
                dve.wait_ge(rows, 1)
                dve.tensor_copy(modrow[:, 0:512], pm[0][0:B, :]).then_inc(rowsb, 1)
                dve.tensor_copy(modrow[:, 768:1024], pm[1][0:B, 256:512]).then_inc(rowsb, 1)
                dve.tensor_scalar(modrow[:, 1024:1280], pm[2][0:B, 0:256], 1.0, None, ALU.add)
                gates = [(pm[1][0:B, 0:256], modrow[:, 512:768]), (pm[2][0:B, 256:512], modrow[:, 1280:1536])]
                n = 3
                for k, (g, out) in enumerate(gates):
                    dve.tensor_scalar(sgn[:, k, :], g, 0.0, 2.0, ALU.is_ge, ALU.mult).then_inc(scdone, 1)
                    dve.wait_ge(scdone, n + 1)
                    dve.tensor_scalar(sgn[:, k, :], sgn[:, k, :], -1.0, None, ALU.add).then_inc(scdone, 1)
                    dve.wait_ge(scdone, n + 2)
                    dve.tensor_tensor(out, g, sgn[:, k, :], ALU.mult).then_inc(scdone, 1)
                    dve.wait_ge(scdone, n + 3)
                    n += 3
                    ins = dve.scalar_tensor_tensor(out, out, 0.25, sgn[:, k, :], ALU.max, ALU.mult)
                ins.then_inc(rowsb, 1)

            @block.gpsimd
            def _(pool):
                pool.memset(zero[:], 0.0).then_inc(step, 1)
                pool.memset(t["ks"][:].bitcast(F32), 0.0)
                pool.memset(t["vaug"][:], 1.0)
                pool.wait_ge(split, 1)
                pool.tensor_tensor(t["wl"][:], w32[:], t["wh"][:].bitcast(F32), ALU.subtract)

            @block.tensor
            def _(pe):
                pe.wait_ge(scdone, 3)
                for k in range(4):
                    for c in range(DC):
                        mm = pe.matmul(pt[:, k * B:(k + 1) * B], wmod[:, c, k * P:(k + 1) * P], sc[:, c, :],
                                       start=(c == 0), stop=(c == DC - 1))
                mm.then_inc(cols, 1)
                for k in range(3):
                    for c in range(DC):
                        mm = pe.matmul(pm[k][0:B, :], sc[:, c, :], wmod[:, c, k * 512:(k + 1) * 512],
                                       start=(c == 0), stop=(c == DC - 1))
                mm.then_inc(rows, 1)


def max_banks():
    return ([[(2, h, 0), (0, h, 384)] for h in range(GH)] + [[(1, h, 0), (1, h + 2, 256)] for h in range(2)]
            + [[(3, h, 0)] for h in range(GH)])


def exp_banks():
    out = []
    for pair in range(2):
        for u in range(2):
            h, base = pair + 2 * u, pair * PAIRW + u * 1024
            out.append(([(0, h, 0)], base))
            out.append(([(1, h, 0), (3, h, 384)], base + 512))
        out.append(([(2, pair, 0), (2, pair + 2, 256)], pair * PAIRW + 2048))
    return out


def prob_column(kt, h):
    base, u = (h % 2) * PAIRW, h // 2
    return base + {0: u * 1024, 1: u * 1024 + 512, 3: u * 1024 + 896, 2: 2048 + u * 256}[kt]


PRODUCTS = ((0, 0), (0, 1), (1, 0))


def attention(nc, d, t):
    with ExitStack() as ctx:
        sb = lambda n, s, dt=F32: ctx.enter_context(nc.sbuf_tensor(n, s, dt))
        ps = lambda n: ctx.enter_context(nc.psum_tensor(n, [P, 512], F32))
        sem = lambda n: ctx.enter_context(nc.semaphore(n))
        W = (t["wh"], t["wl"])
        ident, mask, rope, modT = t["ident"], t["mask"], t["rope"], t["modT"]
        qs, ks, vaug, sel, ones = t["qs"], t["ks"], t["vaug"], t["sel"], t["ones"]
        xb = sb("xb", [P, KT, D])
        xn = sb("xn", [P, KT, D])
        att = xn
        stats = sb("stats", [P, KT, 6])
        mv = sb("mv", [P, KT, 2])
        rstd, nv, na = sb("rstd", [P, KT]), sb("nv", [P, KT]), sb("na", [P, KT])
        ht32 = sb("ht32", [P, DC, S])
        hT = (sb("hTh", [P, DC, S], F32R), sb("hTl", [P, DC, S], F32R))
        qk = sb("qk", [P, 4, S])
        qkl = sb("qkl", [P, 4, S], F32R)
        qksw = sb("qksw", [P, 4, S])
        qkh = sb("qkh", [P, 4, S], F32R)
        mx = sb("mx", [P, 2, KT, GH])
        mrow = [sb(f"mrow{i}", [GH, S], F32R) for i in range(2)]
        probs = sb("probs", [P, 2, 2 * PAIRW])
        oT = sb("oT", [P, NG, S])
        rden = sb("rden", [P, KT, NH])
        attT = (sb("attTh", [P, DC, S], F32R), sb("attTl", [P, DC, S], F32R))
        gab = sb("gab", [P, D])
        xr = sb("xr", [P, KT, D])
        yo = sb("yo", [P, 2, D])
        pM, pS, pO, pX = ([ps(f"p{n}{i}") for i in range(2)] for n in "MSOX")

        x_in, x_free = sem("x_in"), sem("x_free")
        ln_a, ln_b, ln_s = sem("ln_stats"), sem("ln_rstd"), sem("ln_step")
        xn_done = sem("xn_done")
        v_full, qk_full, xt_full = sem("v_full"), sem("qk_full"), sem("xt_full")
        v_ready, th_done, tl_done, qk_ev = sem("v_ready"), sem("th_done"), sem("tl_done"), sem("qk_ev")
        swapped, rope1, rope2, rope3 = sem("swapped"), sem("rope1"), sem("rope2"), sem("rope3")
        qkh_done, qkl_done = sem("qkh_done"), sem("qkl_done")
        hh_done, stk_full, qs_done, ks_done = sem("hh_done"), sem("stk_full"), sem("qs_done"), sem("ks_done")
        m_full, m_free, s_full, s_free = sem("m_full"), sem("m_free"), sem("s_full"), sem("s_free")
        neg_full, mrow_done, mrow_in = sem("neg_full"), sem("mrow_done"), sem("mrow_in")
        sel_done, o_full, o_free = sem("sel_done"), sem("o_full"), sem("o_free")
        ot_full, rd_done, att_done = sem("ot_full"), sem("rd_done"), sem("att_done")
        at_full, ath_done, atl_done = sem("at_full"), sem("ath_done"), sem("atl_done")
        y_full, y_ga, x1_done, x1_out = sem("y_full"), sem("y_ga"), sem("x1_done"), sem("x1_out")
        aux_in = sem("aux_in")

        with nc.Block() as block:

            @block.tensor
            def _(pe):
                read = [None, None]

                def take(k, signal, value):
                    if read[k] is not None:
                        pe.wait_ge(*read[k])
                    read[k] = (signal, value)
                    return pX[k]

                def max_bank(b, g, i):
                    n = 10 * (4 * b + g) + i
                    if not (isinstance(n, int) and n < 2):
                        pe.wait_ge(m_free, n - 1)
                    for qt, h, col in max_banks()[i]:
                        hh = GH * g + h
                        mm = pe.matmul(pM[i % 2][:, col:col + P * (qt + 1)],
                                       qs[:, hh // 2, qt * P:qt * P + P], ks[:, hh, 0:P * (qt + 1)], start=True, stop=True)
                    mm.then_inc(m_full, 1)

                def exp_bank(b, g, i):
                    n = 40 * b + 10 * g + i
                    if not (isinstance(n, int) and n < 2):
                        pe.wait_ge(s_free, n - 1)
                    for kt, h, col in exp_banks()[i][0]:
                        hh = GH * g + h
                        mm = pe.matmul(pS[i % 2][:, col:col + S - kt * P],
                                       ks[:, hh, kt * P:kt * P + P], qs[:, hh // 2, kt * P:S], start=True, stop=True)
                    mm.then_inc(s_full, 1)
                    return mm

                def group(b, g, nxt, vals=None):
                    pe.wait_ge(mrow_in, 32 * (4 * b + g + 1))
                    if nxt is not None and nxt[1] < 2:
                        tiles = 8 * nxt[0] + 4 + 4 * nxt[1]
                        pe.wait_ge(qs_done, tiles)
                        pe.wait_ge(ks_done, tiles)
                    for i in range(MAXB):
                        exp_bank(b, g, i)
                        if nxt is not None:
                            max_bank(*nxt, i)
                        if vals is not None and i in (2, 4, 6, 8):
                            values(*vals, i // 2 - 1)

                def negate(b, g):
                    s = 4 * b + g
                    bank = take(0, mrow_done, s + 1)
                    pe.wait_ge(m_free, 10 * (s + 1))
                    for qt in range(KT):
                        mm = pe.transpose(bank[0:GH, qt * P:(qt + 1) * P], mx[:, g % 2, qt, :], ident[:])
                    mm.then_inc(neg_full, 1)

                def values(b, g, kt):
                    s = 4 * b + g
                    if kt == 0:
                        pe.wait_ge(sel_done, 2 * (s + 1))
                        if not (isinstance(s, int) and s < 2):
                            pe.wait_ge(o_free, s - 1)
                        if g == 0:
                            pe.wait_ge(v_ready, 2 * (b + 1))
                    for h in range(GH):
                        at = prob_column(kt, h)
                        mm = pe.matmul(pO[g % 2][32 * h:32 * h + 32, kt * P:S],
                                       vaug[:, kt, GH * g + h, :],
                                       probs[:, g % 2, at:at + S - kt * P],
                                       start=(kt == 0), stop=(kt == KT - 1))
                    if kt == KT - 1:
                        mm.then_inc(o_full, 1)

                def v_proj(b, halves):
                    for half in halves:
                        bank = take(half, v_ready, 2 * b + half + 1)
                        for k2 in range(2):
                            kt = 2 * half + k2
                            for n, (c, (s_, m_)) in enumerate((c, p) for c in range(DC) for p in PRODUCTS):
                                mm = pe.matmul(bank[:, k2 * D:(k2 + 1) * D], hT[s_][:, c, kt * P:(kt + 1) * P],
                                               W[m_][:, c, 2 * D:3 * D], start=(n == 0), stop=(n == 5))
                        mm.then_inc(v_full, 1)

                def x_transpose(b):
                    pe.wait_ge(xn_done, 4 * (b + 1))
                    for c in range(DC):
                        bank = take(c, th_done, 2 * b + c + 1)
                        for kt in range(KT):
                            mm = pe.transpose(bank[:, kt * P:(kt + 1) * P], xn[:, kt, c * P:(c + 1) * P], ident[:])
                        mm.then_inc(xt_full, 1)

                def qk_proj(b):
                    pe.wait_ge(tl_done, 2 * (b + 1))
                    for i in range(4):
                        bank = take(i % 2, qk_ev, 4 * b + i + 1)
                        for n, (c, (s_, m_)) in enumerate((c, p) for c in range(DC) for p in PRODUCTS):
                            mm = pe.matmul(bank[:], W[s_][:, c, i * P:(i + 1) * P], hT[m_][:, c, :],
                                           start=(n == 0), stop=(n == 5))
                        mm.then_inc(qk_full, 1)

                def stacks(b, half):
                    pe.wait_ge(qkl_done, b + 1)
                    n = 8 * b + 4 * half
                    for pair in range(4):
                        for k, done in ((0, qs_done), (1, ks_done)):
                            bank = (pX, pM, pS, pX)[pair][k]
                            if pair == 0:
                                take(k, done, n + 4)
                            elif pair == 2 and not (isinstance(n, int) and n < 8):
                                pe.wait_ge(s_free, 40 * b + 10 * half - 10)
                            elif pair == 3:
                                pe.wait_ge(done, n + 1)
                            pe.matmul(bank[:], sel[:, 2 * k, pair, :], qkh[:, 2 * k + half, :], start=True, stop=False)
                            pe.matmul(bank[:], sel[:, 2 * k + 1, pair, :], qkl[:, 2 * k + half, :],
                                      start=False, stop=True).then_inc(stk_full, 1)

                def out_transpose(b):
                    pe.wait_ge(o_free, 4 * (b + 1))
                    for qt in range(KT):
                        bank = take(qt % 2, att_done, 4 * b + qt + 1)
                        for g in range(NG):
                            mm = pe.transpose(bank[:, g * P:(g + 1) * P], oT[:, g, qt * P:(qt + 1) * P], ident[:])
                        mm.then_inc(ot_full, 1)

                def att_transpose(b):
                    pe.wait_ge(att_done, 4 * (b + 1))
                    for c in range(DC):
                        bank = take(c, atl_done, 2 * b + c + 1)
                        for qt in range(KT):
                            mm = pe.transpose(bank[:, qt * P:(qt + 1) * P], att[:, qt, c * P:(c + 1) * P], ident[:])
                        mm.then_inc(at_full, 1)

                def out_proj(b):
                    pe.wait_ge(atl_done, 2 * (b + 1))
                    for half in range(2):
                        bank = take(half, y_ga, 2 * b + half + 1)
                        for q2 in range(2):
                            qt = 2 * half + q2
                            for n, (c, (s_, m_)) in enumerate((c, p) for c in range(DC) for p in PRODUCTS):
                                mm = pe.matmul(bank[:, q2 * D:(q2 + 1) * D], attT[s_][:, c, qt * P:(qt + 1) * P],
                                               W[m_][:, c, 3 * D:4 * D], start=(n == 0), stop=(n == 5))
                        mm.then_inc(y_full, 1)

                def batch(b, first=False, nxt=True, nxt2=True):
                    group(b, 0, (b, 1), None if first else (b - 1, 3))
                    v_proj(b, [0])
                    negate(b, 1)
                    v_proj(b, [1])
                    if not first:
                        out_transpose(b - 1)
                    if nxt:
                        qk_proj(b + 1)
                    group(b, 1, (b, 2), (b, 0))
                    if not first:
                        att_transpose(b - 1)
                    negate(b, 2)
                    if not first:
                        out_proj(b - 1)
                    group(b, 2, (b, 3), (b, 1))
                    negate(b, 3)
                    if nxt:
                        stacks(b + 1, 0)
                    group(b, 3, (b + 1, 0) if nxt else None, (b, 2))
                    if nxt:
                        negate(b + 1, 0)
                        stacks(b + 1, 1)
                    if nxt2:
                        x_transpose(b + 2)

                x_transpose(0)
                qk_proj(0)
                x_transpose(1)
                stacks(0, 0)
                stacks(0, 1)
                pe.wait_ge(qs_done, 8)
                pe.wait_ge(ks_done, 8)
                for i in range(MAXB):
                    max_bank(0, 0, i)
                negate(0, 0)
                batch(0, first=True)
                with pe.Fori(1, B - 2) as b:
                    read[:] = (th_done, 2 * b + 3), (th_done, 2 * b + 4)
                    batch(b)
                read[:] = (th_done, 2 * B - 1), (th_done, 2 * B)
                batch(B - 2, nxt2=False)
                batch(B - 1, nxt=False, nxt2=False)
                for kt in range(KT):
                    values(B - 1, 3, kt)
                out_transpose(B - 1)
                att_transpose(B - 1)
                out_proj(B - 1)

            @block.scalar
            def _(act):
                def exps(b, g):
                    s = 4 * b + g
                    if not (isinstance(s, int) and s < 2):
                        act.wait_ge(o_full, s - 1)
                    for i, (_, at) in enumerate(exp_banks()):
                        act.wait_ge(s_full, 10 * s + i + 1)
                        act.activation(probs[:, g % 2, at:at + 512], pS[i % 2][:], ACT.Exp).then_inc(s_free, 1)

                def max_row(b, g):
                    s = 4 * b + g
                    act.wait_ge(neg_full, s + 1)
                    if not (isinstance(s, int) and s < 2):
                        act.wait_ge(mrow_in, 32 * (s - 1))
                    act.activation(mrow[g % 2][:], pX[0][0:GH, :], ACT.Copy, scale=-1.0).then_inc(mrow_done, 1)

                def out_evac(b, g):
                    act.wait_ge(o_full, 4 * b + g + 1)
                    if g == 0 and not (isinstance(b, int) and b == 0):
                        act.wait_ge(ot_full, 4 * b)
                    act.activation(oT[:, g, :], pO[g % 2][:], ACT.Copy).then_inc(o_free, 1)

                def v_evac(b, halves):
                    for half in halves:
                        act.wait_ge(v_full, 2 * b + half + 1)
                        if half == 0 and not (isinstance(b, int) and b == 0):
                            act.wait_ge(o_full, 4 * b)
                        act.activation(vaug[:, 2 * half:2 * half + 2, :, 0:HD],
                                       pX[half][:].rearrange("p (k h e) -> p k h e", k=2, h=NH),
                                       ACT.Copy).then_inc(v_ready, 1)

                def x_evac(b):
                    for c in range(DC):
                        act.wait_ge(xt_full, 2 * b + c + 1)
                        if c == 0 and not (isinstance(b, int) and b == 0):
                            act.wait_ge(tl_done, 2 * b)
                        scale, bias = modT[:, 2 + c, bass.ds(b, 1)], modT[:, c, bass.ds(b, 1)]
                        act.activation(ht32[:, c, :], pX[c][:], ACT.Identity, scale=scale, bias=bias).then_inc(th_done, 1)

                def high(b):
                    for c in range(DC):
                        act.wait_ge(th_done, 2 * b + c + 1)
                        if c == 0 and not (isinstance(b, int) and b == 0):
                            act.wait_ge(v_full, 2 * b)
                        act.activation(hT[0][:, c, :], ht32[:, c, :], ACT.Copy).then_inc(hh_done, 1)

                def rotated_high(b):
                    act.wait_ge(rope3, b + 1)
                    if not (isinstance(b, int) and b == 0):
                        act.wait_ge(stk_full, 16 * b)
                    act.activation(qkh[:], qk[:], ACT.Copy).then_inc(qkh_done, 1)

                def key_stacks(b, half):
                    for pair in range(4):
                        n = 8 * b + 4 * half + pair
                        act.wait_ge(stk_full, 2 * n + 2)
                        if pair == 0 and not (isinstance(b, int) and b == 0):
                            act.wait_ge(s_full, 40 * (b - 1) + 20 * half + 20)
                        bank = (pX, pM, pS, pX)[pair][1]
                        for h in range(2):
                            half_rows = slice(64 * h, 64 * h + 64)
                            ins = act.activation(ks[half_rows, 8 * half + 2 * pair + h, :], bank[half_rows, :], ACT.Identity,
                                                 bias=ones[half_rows, :])
                        ins.then_inc(ks_done, 1)

                def qk_evac(b):
                    for i in range(4):
                        act.wait_ge(qk_full, 4 * b + i + 1)
                        if i == 0 and not (isinstance(b, int) and b == 0):
                            act.wait_ge(qkl_done, b)
                        act.activation(qk[:, i, :], pX[i % 2][:], ACT.Copy, scale=HD ** -0.5 if i < 2 else 1.0).then_inc(qk_ev, 1)

                def att_high(b):
                    for c in range(DC):
                        act.wait_ge(at_full, 2 * b + c + 1)
                        if c == 0 and not (isinstance(b, int) and b == 0):
                            act.wait_ge(y_full, 2 * b)
                        act.activation(attT[0][:, c, :], pX[c][:], ACT.Copy).then_inc(ath_done, 1)

                def batch(b, first=False, nxt=True, nxt2=True):
                    exps(b, 0)
                    if not first:
                        out_evac(b - 1, 3)
                    v_evac(b, [0])
                    max_row(b, 1)
                    v_evac(b, [1])
                    if nxt:
                        high(b + 1)
                        qk_evac(b + 1)
                    exps(b, 1)
                    if not first:
                        att_high(b - 1)
                    max_row(b, 2)
                    out_evac(b, 0)
                    if nxt:
                        rotated_high(b + 1)
                    exps(b, 2)
                    max_row(b, 3)
                    if nxt:
                        key_stacks(b + 1, 0)
                    out_evac(b, 1)
                    exps(b, 3)
                    if nxt:
                        max_row(b + 1, 0)
                        key_stacks(b + 1, 1)
                    out_evac(b, 2)
                    if nxt2:
                        x_evac(b + 2)

                x_evac(0)
                high(0)
                qk_evac(0)
                x_evac(1)
                rotated_high(0)
                key_stacks(0, 0)
                key_stacks(0, 1)
                max_row(0, 0)
                batch(0, first=True)
                with act.Fori(1, B - 2) as b:
                    batch(b)
                batch(B - 2, nxt2=False)
                batch(B - 1, nxt=False, nxt2=False)
                out_evac(B - 1, 3)
                att_high(B - 1)

            @block.vector
            def _(dve):
                def maxima(b, g):
                    s = 4 * b + g
                    if not (isinstance(s, int) and s < 2):
                        dve.wait_ge(neg_full, s - 1)
                    for i, bank in enumerate(max_banks()):
                        wait_apart(dve, m_full, 10 * s + i + 1)
                        for qt, h, col in bank:
                            w = P * (qt + 1)
                            scores = pM[i % 2][:, col:col + w]
                            ins = dve.tensor_tensor_reduce(
                                out=scores, in0=scores, in1=mask[:, S - w:S],
                                scale=1.0, scalar=-3e38, op0=ALU.add, op1=ALU.max,
                                accum_out=mx[:, g % 2, qt, h:h + 1])
                        ins.then_inc(m_free, 1)

                def ln_stats(b):
                    dve.wait_ge(x_in, 16 * (b + 1))
                    for k in range(KT):
                        ins = dve.bn_stats(stats[:, k, :], xb[:, k, :])
                    ins.then_inc(ln_s, 1)
                    wait_apart(dve, ln_s, 2 * b + 1)
                    for k in range(KT):
                        ins = dve.bn_aggr(mv[:, k, :], stats[:, k, :])
                    ins.then_inc(ln_s, 1)

                def ln_apply(b):
                    dve.wait_ge(ln_s, 2 * b + 2)
                    dve.wait_ge(ln_b, RSQRT_STEPS * (b + 1))
                    if not (isinstance(b, int) and b == 0):
                        dve.wait_ge(xt_full, 2 * b)
                    if not (isinstance(b, int) and b < 3):
                        dve.wait_ge(at_full, 2 * b - 4)
                    for k in range(KT):
                        dve.tensor_scalar(xn[:, k, :], xb[:, k, :], mv[:, k, 0:1], rstd[:, k:k + 1],
                                          ALU.subtract, ALU.mult).then_inc(xn_done, 1)

                def low(b):
                    for c in range(DC):
                        dve.wait_ge(hh_done, 2 * b + c + 1)
                        dve.tensor_tensor(hT[1][:, c, :], ht32[:, c, :], hT[0][:, c, :].bitcast(F32),
                                          ALU.subtract).then_inc(tl_done, 1)

                def rotate(b):
                    dve.wait_ge(swapped, 32 * (b + 1))
                    dve.tensor_tensor(qk[:], qk[:], rope[:, 0, None, :].broadcast_to([P, 4, S]), ALU.mult).then_inc(rope1, 1)
                    dve.wait_ge(rope1, b + 1)
                    dve.wait_ge(rope2, b + 1)
                    dve.tensor_tensor(qk[:], qk[:], qksw[:], ALU.add).then_inc(rope3, 1)

                def query_stacks(b, half):
                    for pair in range(4):
                        n = 8 * b + 4 * half + pair
                        dve.wait_ge(stk_full, 2 * n + 1)
                        if pair == 0 and not (isinstance(b, int) and b == 0):
                            dve.wait_ge(s_full, 40 * (b - 1) + 20 * half + 20)
                        dve.tensor_copy(qs[:, 4 * half + pair, :], (pX, pM, pS, pX)[pair][0][:]).then_inc(qs_done, 1)

                def normalise(b):
                    for qt in range(KT):
                        dve.wait_ge(ot_full, 4 * b + qt + 1)
                        o = pX[qt % 2][:].rearrange("p (h e) -> p h e", e=32)
                        dve.reciprocal(rden[:, qt, :], o[:, :, HD]).then_inc(rd_done, 1)
                        dve.wait_ge(rd_done, 4 * b + qt + 1)
                        if qt == 0:
                            dve.wait_ge(xt_full, min(2 * b + 6, 2 * B) if isinstance(b, int) else 2 * b + 6)
                        dve.tensor_tensor(att[:, qt, :].rearrange("p (h e) -> p h e", e=HD), o[:, :, 0:HD],
                                          rden[:, qt, :, None].broadcast_to([P, NH, HD]), ALU.mult).then_inc(att_done, 1)

                def att_low(b):
                    for c in range(DC):
                        dve.wait_ge(ath_done, 2 * b + c + 1)
                        dve.tensor_tensor(attT[1][:, c, :], pX[c][:], attT[0][:, c, :].bitcast(F32),
                                          ALU.subtract).then_inc(atl_done, 1)

                def gate(b):
                    dve.wait_ge(aux_in, 32 * (b + 1))
                    for half in range(2):
                        dve.wait_ge(y_full, 2 * b + half + 1)
                        if half == 1 or not (isinstance(b, int) and b == 0):
                            dve.wait_ge(x1_done, 2 * b + half)
                        dve.tensor_tensor(yo[:], pX[half][:].rearrange("p (k n) -> p k n", k=2),
                                          gab[:, None, :].broadcast_to([P, 2, D]), ALU.mult).then_inc(y_ga, 1)

                def batch(b, first=False, nxt=True, nxt2=True):
                    maxima(b, 1)
                    if nxt:
                        low(b + 1)
                    if not first:
                        normalise(b - 1)
                    if nxt2:
                        ln_stats(b + 2)
                    maxima(b, 2)
                    if not first:
                        att_low(b - 1)
                    if nxt:
                        rotate(b + 1)
                    if not first:
                        gate(b - 1)
                    maxima(b, 3)
                    if nxt:
                        query_stacks(b + 1, 0)
                    if nxt2:
                        ln_apply(b + 2)
                    if nxt:
                        maxima(b + 1, 0)
                        query_stacks(b + 1, 1)

                ln_stats(0)
                ln_apply(0)
                low(0)
                ln_stats(1)
                ln_apply(1)
                rotate(0)
                query_stacks(0, 0)
                query_stacks(0, 1)
                maxima(0, 0)
                batch(0, first=True)
                with dve.Fori(1, B - 2) as b:
                    batch(b)
                batch(B - 2, nxt2=False)
                batch(B - 1, nxt=False, nxt2=False)
                normalise(B - 1)
                att_low(B - 1)
                gate(B - 1)

            @block.gpsimd
            def _(pool):
                def rsqrt(b):
                    pool.wait_ge(ln_s, 2 * b + 2)
                    if not (isinstance(b, int) and b == 0):
                        wait_apart(pool, xn_done, 4 * b)
                    rsqrt_steps(pool, ln_b, RSQRT_STEPS * b, rstd[:], mv[:, :, 1], nv[:], na[:])

                def rotate(b):
                    pool.wait_ge(swapped, 32 * (b + 1))
                    pool.tensor_tensor(qksw[:], qksw[:], rope[:, 1, None, :].broadcast_to([P, 4, S]),
                                       ALU.mult).then_inc(rope2, 1)

                def rotate_low(b):
                    pool.wait_ge(qkh_done, b + 1)
                    pool.tensor_tensor(qkl[:], qk[:], qkh[:].bitcast(F32), ALU.subtract).then_inc(qkl_done, 1)

                def select(b, g):
                    s = 4 * b + g
                    for pair in range(2):
                        wait_apart(pool, s_free, 10 * s + 5 * pair + 5)
                        pp = probs[:, g % 2, pair * PAIRW:(pair + 1) * PAIRW]
                        heads = pp[:, 0:2048].rearrange("p (u n) -> p u n", u=2)
                        for view, pat in (
                            (heads.rearrange("p u (k n) -> p u k n", k=2)[:, :, :, 0:P], [[0, 2], [0, 2], [1, P]]),
                            (heads[:, :, 896:1024], [[0, 2], [1, P]]),
                            (pp[:, 2048:2560].rearrange("p (u n) -> p u n", u=2)[:, :, 0:P], [[0, 2], [1, P]]),
                        ):
                            ins = pool.affine_select(out=view, in_=view, compare_op=ALU.is_ge, fill=0.0, base=0,
                                                     pattern=pat, channel_multiplier=-1)
                        ins.then_inc(sel_done, 1)

                def residual(b):
                    if not (isinstance(b, int) and b == 0):
                        wait_apart(pool, x1_out, 16 * b)
                    for half in range(2):
                        pool.wait_ge(y_ga, 2 * b + half + 1)
                        rows = xr[:, 2 * half:2 * half + 2, :]
                        pool.tensor_tensor(rows, rows, yo[:], ALU.add).then_inc(x1_done, 1)

                def batch(b, first=False, nxt=True, nxt2=True):
                    select(b, 0)
                    if nxt:
                        rotate(b + 1)
                    select(b, 1)
                    if not first:
                        residual(b - 1)
                    if nxt:
                        rotate_low(b + 1)
                    if nxt2:
                        rsqrt(b + 2)
                    select(b, 2)
                    select(b, 3)

                rsqrt(0)
                rsqrt(1)
                rotate(0)
                rotate_low(0)
                batch(0, first=True)
                with pool.Fori(1, B - 2) as b:
                    batch(b)
                batch(B - 2, nxt2=False)
                batch(B - 1, nxt=False, nxt2=False)
                residual(B - 1)

            @block.sync
            def _(sp):
                def rows(ap, b):
                    return ap[bass.ds(b * S, S), :].rearrange("(k p) n -> p k n", p=P)

                def load_x(b):
                    if not (isinstance(b, int) and b == 0):
                        sp.wait_ge(xn_done, 4 * b)
                    sp.dma_start(xb[:], rows(d["x"], b)).then_inc(x_in, 16)

                def load_aux(b):
                    if not (isinstance(b, int) and b == 0):
                        wait_apart(sp, x1_out, 16 * b)
                        sp.wait_ge(y_ga, 2 * b)
                    sp.dma_start(xr[:], rows(d["x"], b)).then_inc(aux_in, 16)
                    sp.dma_start(gab[:], d["mod"][bass.ds(b, 1), 2 * D:3 * D].broadcast_to([P, D])).then_inc(aux_in, 16)

                def max_rows(b, g):
                    s = 4 * b + g
                    sp.wait_ge(mrow_done, s + 1)
                    for u in range(2):
                        sp.dma_start(qs[48:128:64, 2 * g + u, :].bitcast(F32), mrow[g % 2][2 * u:2 * u + 2, :].bitcast(F32)).then_inc(mrow_in, 16)

                def swap(b):
                    wait_apart(sp, qk_ev, 4 * (b + 1))
                    if not (isinstance(b, int) and b == 0):
                        sp.wait_ge(rope3, b)
                    for k in range(2):
                        sp.dma_start(qksw[k:P:2, :, :], qk[1 - k:P:2, :, :]).then_inc(swapped, 16)

                def store(b):
                    sp.wait_ge(x1_done, 2 * b + 2)
                    sp.dma_start(rows(d["x1"], b), xr[:]).then_inc(x1_out, 16)

                def batch(b, first=False, nxt=True, nxt2=True):
                    if nxt2:
                        load_x(b + 2)
                    max_rows(b, 1)
                    if nxt:
                        swap(b + 1)
                    max_rows(b, 2)
                    max_rows(b, 3)
                    if not first:
                        store(b - 1)
                        load_aux(b)
                    if nxt:
                        max_rows(b + 1, 0)

                load_x(0)
                load_aux(0)
                load_x(1)
                swap(0)
                max_rows(0, 0)
                batch(0, first=True)
                with sp.Fori(1, B - 2) as b:
                    batch(b)
                batch(B - 2, nxt2=False)
                batch(B - 1, nxt=False, nxt2=False)
                store(B - 1)
                sp.wait_ge(x1_out, 16 * B)


def shared_expert(nc, d, t):
    with ExitStack() as ctx:
        sb = lambda n, s, dt=F32: ctx.enter_context(nc.sbuf_tensor(n, s, dt))
        ps = lambda n: ctx.enter_context(nc.psum_tensor(n, [P, 512], F32))
        sem = lambda n: ctx.enter_context(nc.semaphore(n))
        ident, rgu, rdn, h2all = t["ident"], t["rgu"], t["rdn"], t["h2all"]
        wgu = (sb("wguh", [P, DC, 2 * F], F32R), sb("wgul", [P, DC, 2 * F], F32R))
        wdn = (sb("wdnh", [P, FC, D], F32R), sb("wdnl", [P, FC, D], F32R))
        wr = (sb("wrh", [P, DC, NE], F32R), sb("wrl", [P, DC, NE], F32R))
        room = rdn[:].rearrange("p c e n -> p (c e n)")
        wgu32 = room[:, 0:2 * DC * F].rearrange("p (c n) -> p c n", c=DC)
        wdn32 = room[:, 2 * DC * F:2 * DC * F + FC * D].rearrange("p (c n) -> p c n", c=FC)
        wr32 = sb("wr32", [P, DC, NE])
        xa = sb("xa", [P, KT, D])
        xr = sb("xr2", [P, KT, D])
        bsc = sb("bsc", [P, 2, D])
        bg = sb("bg", [P, D])
        xn = sb("xn2", [P, KT, D])
        h2 = sb("h2", [P, KT, D])
        stats, mv = sb("stats2", [P, KT, 6]), sb("mv2", [P, KT, 2])
        rstd, nv, na = sb("rstd2", [P, KT]), sb("nv2", [P, KT]), sb("na2", [P, KT])
        hT = (sb("h2Th", [P, DC, S], F32R), sb("h2Tl", [P, DC, S], F32R))
        lgT = sb("lgT", [NE, S])
        lg, m8 = sb("lg", [P, KT, NE]), sb("m8", [P, KT, 8])
        i8, top = sb("i8", [P, KT, 8], U32), sb("top", [P, KT])
        sg = sb("sg", [P, 2, S])
        hid = sb("hid", [P, 2, S])
        hidT = (sb("hidh", [P, FC, S], F32R), sb("hidl", [P, FC, S], F32R))
        pT, pG, pU, pD = ([ps(f"q{n}{i}") for i in range(2)] for n in "TGUD")

        w_in, wr_in, w_high, w_low = sem("w_in"), sem("wr_in"), sem("w_high"), sem("w_low")
        big_in = t["big_in"]
        x_in, bs_in, aux_in = sem("x2_in"), sem("bs_in"), sem("aux2_in")
        ln_s, ln_b, xn_done, xm_done, h2_done = sem("ln2_s"), sem("ln2_b"), sem("xn2_done"), sem("xm_done"), sem("h2_done")
        h2_kept = sem("h2_kept")
        ht_full, hh_done, hl_done = sem("ht_full"), sem("hh_done"), sem("hl_done")
        lt_full, lt_done = sem("lt_full"), sem("lt_done")
        lg_full, lg_done, top_step, oh_done = sem("lg_full"), sem("lg_done"), sem("top_step"), sem("oh_done")
        g_full, u_full, silu_done, hid_done = sem("g_full"), sem("u_full"), sem("silu_done"), sem("hid_done")
        hidh_done, hidl_done = sem("hidh_done"), sem("hidl_done")
        d_full, y_done, x2_done, x2_out = sem("d_full"), sem("y_done"), sem("x2_done"), sem("x2_out")

        with nc.Block() as block:

            @block.tensor
            def _(pe):
                def transpose(b):
                    pe.wait_ge(h2_done, b + 1)
                    for c in range(DC):
                        if c == 0 and not (isinstance(b, int) and b == 0):
                            pe.wait_ge(lg_done, b)
                        for k in range(KT):
                            mm = pe.transpose(pT[c][:, k * P:(k + 1) * P], h2[:, k, c * P:(c + 1) * P], ident[:])
                        mm.then_inc(ht_full, 1)

                def logits(b):
                    pe.wait_ge(hl_done, 2 * (b + 1))
                    for n, (c, (s_, m_)) in enumerate((c, p) for c in range(DC) for p in PRODUCTS):
                        mm = pe.matmul(pT[0][0:NE, :], wr[s_][:, c, :], hT[m_][:, c, :], start=(n == 0), stop=(n == 5))
                    mm.then_inc(lt_full, 1)

                def logits_back(b):
                    wait_apart(pe, lt_done, b + 1)
                    for k in range(KT):
                        mm = pe.transpose(pT[1][:, k * NE:(k + 1) * NE], lgT[:, k * P:(k + 1) * P], ident[0:NE, 0:NE])
                    mm.then_inc(lg_full, 1)

                def gate_up(b, first, last):
                    for m in range(first, last):
                        n = FC * b + m
                        for bank, off, free, full in ((pG[m % 2], 0, silu_done, g_full), (pU[m % 2], F, hid_done, u_full)):
                            if not (isinstance(n, int) and n < 2):
                                pe.wait_ge(free, n - 1)
                            for k, (c, (s_, m_)) in enumerate((c, p) for c in range(DC) for p in PRODUCTS):
                                mm = pe.matmul(bank[:], wgu[s_][:, c, off + m * P:off + (m + 1) * P], hT[m_][:, c, :],
                                               start=(k == 0), stop=(k == 5))
                            mm.then_inc(full, 1)

                def down(b):
                    pe.wait_ge(hidh_done, FC * (b + 1))
                    for q, low in ((0, 0), (2, 0), (0, 1), (1, 0), (1, 1), (2, 1), (3, 0), (3, 1)):
                        half = q // 2
                        if (q, low) in ((0, 0), (2, 0)) and not (isinstance(b, int) and b == 0):
                            pe.wait_ge(y_done, 2 * b - 1 + half)
                        if (q, low) == (0, 1):
                            pe.wait_ge(hidl_done, FC * (b + 1))
                        steps = [(m, p) for m in range(FC) for p in PRODUCTS if p[0] == low]
                        for n, (m, (s_, m_)) in enumerate(steps):
                            mm = pe.matmul(pD[half][:, (q % 2) * D:(q % 2 + 1) * D], hidT[s_][:, m, q * P:(q + 1) * P],
                                           wdn[m_][:, m, :], start=(n == 0 and not low),
                                           stop=(n == len(steps) - 1 and bool(low)))
                        if (q, low) in ((1, 1), (3, 1)):
                            mm.then_inc(d_full, 1)

                def batch(b, nxt=True):
                    gate_up(b, 0, 2)
                    logits_back(b)
                    gate_up(b, 2, FC)
                    if nxt:
                        transpose(b + 1)
                    down(b)
                    if nxt:
                        logits(b + 1)

                transpose(0)
                pe.wait_ge(w_low, 3)
                pe.wait_ge(w_high, 3)
                logits(0)
                batch(0)
                with pe.Fori(1, B - 1) as b:
                    batch(b)
                batch(B - 1, nxt=False)

            @block.scalar
            def _(act):
                def keep(b):
                    act.wait_ge(h2_done, b + 1)
                    act.activation(h2all[:, bass.ds(KT * b, KT), :], h2[:], ACT.Copy).then_inc(h2_kept, 1)

                def high(b):
                    for c in range(DC):
                        act.wait_ge(ht_full, 2 * b + c + 1)
                        if c == 0 and not (isinstance(b, int) and b == 0):
                            act.wait_ge(u_full, FC * b)
                            act.wait_ge(lt_full, b)
                        act.activation(hT[0][:, c, :], pT[c][:], ACT.Copy).then_inc(hh_done, 1)

                def silu(b):
                    for m in range(FC):
                        n = FC * b + m
                        act.wait_ge(g_full, n + 1)
                        if not (isinstance(n, int) and n < 2):
                            act.wait_ge(hid_done, n - 1)
                        act.activation(sg[:, m % 2, :], pG[m % 2][:], ACT.Silu).then_inc(silu_done, 1)
                        act.wait_ge(hid_done, n + 1)
                        if m == 0 and not (isinstance(b, int) and b == 0):
                            act.wait_ge(d_full, 2 * b)
                        act.activation(hidT[0][:, m, :], hid[:, m % 2, :], ACT.Copy).then_inc(hidh_done, 1)

                act.wait_ge(w_in, 32)
                act.activation(wgu[0][:], wgu32, ACT.Copy).then_inc(w_high, 1)
                act.activation(wdn[0][:], wdn32, ACT.Copy).then_inc(w_high, 1)
                act.wait_ge(wr_in, 32)
                act.activation(wr[0][:], wr32[:], ACT.Copy).then_inc(w_high, 1)
                def batch(b, nxt=True):
                    silu(b)
                    if nxt:
                        high(b + 1)
                        keep(b + 1)

                keep(0)
                high(0)
                batch(0)
                with act.Fori(1, B - 1) as b:
                    batch(b)
                batch(B - 1, nxt=False)

            @block.vector
            def _(dve):
                def ln_stats(b):
                    dve.wait_ge(x_in, 16 * (b + 1))
                    for k in range(KT):
                        ins = dve.bn_stats(stats[:, k, :], xa[:, k, :])
                    ins.then_inc(ln_s, 1)
                    wait_apart(dve, ln_s, 2 * b + 1)
                    for k in range(KT):
                        ins = dve.bn_aggr(mv[:, k, :], stats[:, k, :])
                    ins.then_inc(ln_s, 1)

                def ln_apply(b):
                    dve.wait_ge(ln_s, 2 * b + 2)
                    dve.wait_ge(ln_b, RSQRT_STEPS * (b + 1))
                    if not (isinstance(b, int) and b == 0):
                        dve.wait_ge(h2_done, b)
                    if not (isinstance(b, int) and b < 2):
                        dve.wait_ge(x2_done, 2 * b - 2)
                    for k in range(KT):
                        dve.tensor_scalar(xn[:, k, :], xa[:, k, :], mv[:, k, 0:1], rstd[:, k:k + 1],
                                          ALU.subtract, ALU.mult).then_inc(xn_done, 1)
                    dve.wait_ge(xn_done, 4 * (b + 1))
                    dve.wait_ge(bs_in, 16 * (b + 1))
                    dve.tensor_tensor(xn[:], xn[:], bsc[:, 1, None, :].broadcast_to([P, KT, D]),
                                      ALU.mult).then_inc(xm_done, 1)

                def low(b):
                    for c in range(DC):
                        dve.wait_ge(hh_done, 2 * b + c + 1)
                        dve.tensor_tensor(hT[1][:, c, :], pT[c][:], hT[0][:, c, :].bitcast(F32),
                                          ALU.subtract).then_inc(hl_done, 1)

                def logits_out(b):
                    dve.wait_ge(lt_full, b + 1)
                    dve.tensor_copy(lgT[:], pT[0][0:NE, :]).then_inc(lt_done, 1)

                def choose(b):
                    dve.wait_ge(lg_full, b + 1)
                    dve.tensor_copy(lg[:], pT[1][:, 0:KT * NE].rearrange("p (k e) -> p k e", e=NE)).then_inc(lg_done, 1)
                    wait_apart(dve, lg_done, b + 1)
                    for k in range(KT):
                        ins = dve.max(m8[:, k, :], lg[:, k, :])
                    ins.then_inc(top_step, 1)
                    wait_apart(dve, top_step, 3 * b + 1)
                    for k in range(KT):
                        ins = dve.max_index(i8[:, k, :], m8[:, k, :], lg[:, k, :])
                    ins.then_inc(top_step, 1)
                    dve.wait_ge(top_step, 3 * b + 2)
                    dve.tensor_copy(t["best"][:, bass.ds(KT * b, KT)], m8[:, :, 0])
                    dve.tensor_copy(top[:], i8[:, :, 0]).then_inc(top_step, 1)
                    dve.wait_ge(top_step, 3 * b + 3)
                    dve.tensor_tensor(t["onehot"][:, bass.ds(KT * b, KT), :],
                                      top[:, :, None].broadcast_to([P, KT, NE]),
                                      t["experts"][:, None, :].broadcast_to([P, KT, NE]), ALU.is_equal).then_inc(oh_done, 1)

                def hidden(b, first, last):
                    for m in range(first, last):
                        n = FC * b + m
                        dve.wait_ge(silu_done, n + 1)
                        dve.wait_ge(u_full, n + 1)
                        if not (isinstance(n, int) and n < 2):
                            dve.wait_ge(hidl_done, n - 1)
                        dve.tensor_tensor(hid[:, m % 2, :], pU[m % 2][:], sg[:, m % 2, :], ALU.mult).then_inc(hid_done, 1)

                def gate(b):
                    dve.wait_ge(aux_in, 32 * (b + 1))
                    for half in range(2):
                        dve.wait_ge(d_full, 2 * b + half + 1)
                        if half == 0:
                            dve.wait_ge(h2_done, min(b + 2, B) if isinstance(b, int) else b + 2)
                        dve.tensor_tensor(xn[:, 2 * half:2 * half + 2, :], pD[half][:].rearrange("p (k n) -> p k n", k=2),
                                          bg[:, None, :].broadcast_to([P, 2, D]), ALU.mult).then_inc(y_done, 1)

                def batch(b, nxt=True, nxt2=True):
                    hidden(b, 0, 1)
                    if nxt:
                        ln_apply(b + 1)
                    hidden(b, 1, 2)
                    choose(b)
                    hidden(b, 2, FC)
                    if nxt:
                        low(b + 1)
                    gate(b)
                    if nxt:
                        logits_out(b + 1)
                    if nxt2:
                        ln_stats(b + 2)

                ln_stats(0)
                ln_apply(0)
                for n, (high, low_, whole) in enumerate(((wgu[0], wgu[1], wgu32), (wdn[0], wdn[1], wdn32), (wr[0], wr[1], wr32[:]))):
                    dve.wait_ge(w_high, n + 1)
                    dve.tensor_tensor(low_[:], whole, high[:].bitcast(F32), ALU.subtract).then_inc(w_low, 1)
                low(0)
                ln_stats(1)
                logits_out(0)
                batch(0)
                with dve.Fori(1, B - 2) as b:
                    batch(b)
                batch(B - 2, nxt2=False)
                batch(B - 1, nxt=False, nxt2=False)

            @block.gpsimd
            def _(pool):
                def rsqrt(b):
                    pool.wait_ge(ln_s, 2 * b + 2)
                    if not (isinstance(b, int) and b == 0):
                        wait_apart(pool, xn_done, 4 * b)
                    rsqrt_steps(pool, ln_b, RSQRT_STEPS * b, rstd[:], mv[:, :, 1], nv[:], na[:])

                def shift(b):
                    pool.wait_ge(xm_done, b + 1)
                    if not (isinstance(b, int) and b == 0):
                        pool.wait_ge(ht_full, 2 * b)
                        pool.wait_ge(h2_kept, b)
                    pool.tensor_tensor(h2[:], xn[:], bsc[:, 0, None, :].broadcast_to([P, KT, D]), ALU.add).then_inc(h2_done, 1)

                def low(b, first, last):
                    for m in range(first, last):
                        pool.wait_ge(hidh_done, FC * b + m + 1)
                        pool.tensor_tensor(hidT[1][:, m, :], hid[:, m % 2, :], hidT[0][:, m, :].bitcast(F32),
                                           ALU.subtract).then_inc(hidl_done, 1)

                def residual(b):
                    for half in range(2):
                        pool.wait_ge(y_done, 2 * b + half + 1)
                        rows = xr[:, 2 * half:2 * half + 2, :]
                        pool.tensor_tensor(rows, rows, xn[:, 2 * half:2 * half + 2, :], ALU.add).then_inc(x2_done, 1)

                def batch(b, nxt=True, nxt2=True):
                    low(b, 0, 1)
                    if nxt:
                        shift(b + 1)
                    low(b, 1, FC)
                    residual(b)
                    if nxt2:
                        rsqrt(b + 2)

                rsqrt(0)
                shift(0)
                rsqrt(1)
                batch(0)
                with pool.Fori(1, B - 2) as b:
                    batch(b)
                batch(B - 2, nxt2=False)
                batch(B - 1, nxt=False, nxt2=False)

            @block.sync
            def _(sp):
                def rows(ap, b):
                    return ap[bass.ds(b * S, S), :].rearrange("(k p) n -> p k n", p=P)

                def load_x(b):
                    if not (isinstance(b, int) and b == 0):
                        sp.wait_ge(xn_done, 4 * b)
                    sp.dma_start(xa[:], rows(d["x1"], b)).then_inc(x_in, 16)
                    if not (isinstance(b, int) and b == 0):
                        sp.wait_ge(h2_done, b)
                    sp.dma_start(bsc[:].rearrange("p k n -> p (k n)"),
                                 d["mod"][bass.ds(b, 1), 3 * D:5 * D].broadcast_to([P, 2 * D])).then_inc(bs_in, 16)

                def load_aux(b):
                    if not (isinstance(b, int) and b == 0):
                        wait_apart(sp, x2_out, 16 * b)
                        sp.wait_ge(y_done, 2 * b)
                    sp.dma_start(xr[:], rows(d["x1"], b)).then_inc(aux_in, 16)
                    sp.dma_start(bg[:], d["mod"][bass.ds(b, 1), 5 * D:6 * D].broadcast_to([P, D])).then_inc(aux_in, 16)

                def store(b):
                    sp.wait_ge(x2_done, 2 * b + 2)
                    sp.dma_start(rows(d["x2"], b), xr[:]).then_inc(x2_out, 16)

                load_x(0)
                sp.dma_start(wgu32, d["sgu"].rearrange("(c p) n -> p c n", p=P)).then_inc(w_in, 16)
                sp.dma_start(wdn32, d["sdn"].rearrange("(c p) n -> p c n", p=P)).then_inc(w_in, 16)
                sp.dma_start(wr32[:], d["wr"].rearrange("(c p) n -> p c n", p=P)).then_inc(wr_in, 16)
                sp.dma_start(t["experts"][:], d["c_experts"]).then_inc(wr_in, 16)
                load_aux(0)
                load_x(1)
                for c in range(DC):
                    sp.dma_start(rgu[:, c], d["rgu"][c * P:(c + 1) * P]).then_inc(big_in, 16)
                sp.wait_ge(w_low, 3)
                for c in range(FC):
                    sp.dma_start(rdn[:, c], d["rdn"][c * P:(c + 1) * P]).then_inc(big_in, 16)
                def batch(b, nxt=True, nxt2=True):
                    if nxt2:
                        load_x(b + 2)
                    if nxt:
                        store(b)
                        load_aux(b + 1)

                batch(0)
                with sp.Fori(1, B - 2) as b:
                    batch(b)
                batch(B - 2, nxt2=False)
                store(B - 1)
                sp.wait_ge(x2_out, 16 * B)
                sp.wait_ge(big_in, 16 * (DC + FC))
                sp.wait_ge(wr_in, 32)


def route(nc, d, t):
    with ExitStack() as ctx:
        sb = lambda n, s, dt=F32: ctx.enter_context(nc.sbuf_tensor(n, s, dt))
        sem = lambda n: ctx.enter_context(nc.semaphore(n))
        onehot, best, h2all = t["onehot"], t["best"], t["h2all"]
        before = sb("before", [P, P])
        beforeb, onesb = sb("beforeb", [P, P], BF16), sb("onesb", [P, P], BF16)
        ohb = sb("ohb", [P, NT, NE], BF16)
        starts = sb("starts", [P, 40, NE])
        ones = sb("ones", [P, NT])
        count = sb("count", [P, NT, NE])
        upto = sb("upto", [P, NT, NE])
        over = sb("over", [P, NE, NT])
        tiles, ends, base = sb("tiles", [P, NE]), sb("ends", [P, NE]), sb("base", [P, NE])
        slot, slotf = sb("slot", [P, NT, NE]), sb("slotf", [P, NT])
        past, eidf = sb("past", [P, 40, NE]), sb("eidf", [P, 40])
        score = sb("score", [P, NT])
        pR = ctx.enter_context(nc.psum_tensor("pR", [P, 512], F32))
        pC = ctx.enter_context(nc.psum_tensor("pC", [P, 512], F32))
        c_in, r, mm_done, ex, sc_done, scaled = sem("c3_in"), sem("r_step"), sem("r_mm"), sem("r_exp"), sem("score_done"), sem("scaled")
        scattered = sem("scattered")
        with nc.Block() as block:

            @block.sync
            def _(sp):
                sp.dma_start(before[:], d["c_before"]).then_inc(c_in, 16)
                sp.dma_start(starts[:], d["c_starts"]).then_inc(c_in, 16)

            @block.tensor
            def _(pe):
                pe.wait_ge(r, 4)
                pe.matmul(pR[:, 0:NT * NE], beforeb[:], ohb[:], start=True, stop=True).then_inc(mm_done, 1)
                pe.matmul(pC[:, 0:NT * NE], onesb[:], ohb[:], start=True, stop=True).then_inc(mm_done, 1)

            @block.scalar
            def _(act):
                act.activation(score[:], best[:], ACT.Exp, scale=-1.0).then_inc(ex, 1)

            @block.vector
            def _(dve):
                n = 4

                def then(ins):
                    nonlocal n
                    n += 1
                    ins.then_inc(r, 1)
                    dve.wait_ge(r, n)

                dve.memset(onesb[:], 1.0).then_inc(r, 1)
                dve.memset(ones[:], 1.0).then_inc(r, 1)
                dve.tensor_copy(ohb[:], onehot[:]).then_inc(r, 1)
                dve.wait_ge(c_in, 32)
                dve.tensor_copy(beforeb[:], before[:]).then_inc(r, 1)
                dve.wait_ge(r, 4)
                dve.wait_ge(ex, 1)
                then(dve.tensor_scalar(score[:], score[:], 1.0, None, ALU.add))
                dve.reciprocal(score[:], score[:]).then_inc(sc_done, 1)
                dve.wait_ge(mm_done, 2)
                then(dve.tensor_copy(count[:], pC[:, 0:NT * NE].rearrange("p (k e) -> p k e", e=NE)))
                for e in range(NE):
                    ins = dve.tensor_tensor_scan(upto[:, :, e], ones[:], count[:, :, e], 0.0, ALU.mult, ALU.add)
                then(ins)
                then(dve.tensor_tensor(over[:], upto[:, NT - 1, :, None].broadcast_to([P, NE, NT]),
                                       starts[:, 0:NT, 0][:, None, :].broadcast_to([P, NE, NT]), ALU.is_gt))
                then(dve.tensor_reduce(tiles[:], over[:], AX.X, ALU.add))
                then(dve.tensor_tensor_scan(ends[:], ones[:, 0:NE], tiles[:], 0.0, ALU.mult, ALU.add))
                then(dve.tensor_tensor(base[:], ends[:], tiles[:], ALU.subtract))
                then(dve.tensor_scalar(base[:], base[:], float(P), None, ALU.mult))
                then(dve.tensor_scalar(ends[:], ends[:], float(P), None, ALU.mult))
                then(dve.tensor_tensor(slot[:], pR[:, 0:NT * NE].rearrange("p (k e) -> p k e", e=NE), upto[:], ALU.add))
                then(dve.tensor_tensor(slot[:], slot[:], count[:], ALU.subtract))
                then(dve.tensor_tensor(slot[:], slot[:], base[:, None, :].broadcast_to([P, NT, NE]), ALU.add))
                then(dve.tensor_tensor(slot[:], slot[:], onehot[:], ALU.mult))
                then(dve.tensor_reduce(slotf[:], slot[:], AX.X, ALU.add))
                then(dve.tensor_copy(t["slots"][:], slotf[:]))
                then(dve.tensor_tensor(past[:], ends[:, None, :].broadcast_to([P, 40, NE]), starts[:], ALU.is_le))
                then(dve.tensor_reduce(eidf[:], past[:], AX.X, ALU.add))
                then(dve.tensor_scalar(eidf[:], eidf[:], float(NE - 1), None, ALU.min))
                then(dve.tensor_copy(t["eid"][:], eidf[:]))
                dve.wait_ge(sc_done, 1)
                for k in range(NT):
                    dve.tensor_scalar(h2all[:, k, :], h2all[:, k, :], score[:, k:k + 1], None, ALU.mult).then_inc(scaled, 1)

            @block.gpsimd
            def _(pool):
                for k in range(NT):
                    pool.wait_ge(scaled, k + 1)
                    pool.indirect_dma_start(
                        out=d["sorted"], out_offset=bass.IndirectOffsetOnAxis(ap=t["slots"][:, k:k + 1].bitcast(U32), axis=0),
                        in_=h2all[:, k, :], in_offset=None).then_inc(scattered, 16)
                pool.wait_ge(scattered, 16 * NT)


def routed_experts(nc, d, t):
    with ExitStack() as ctx:
        sb = lambda n, s, dt=F32: ctx.enter_context(nc.sbuf_tensor(n, s, dt))
        ps = lambda n: ctx.enter_context(nc.psum_tensor(n, [P, 512], F32))
        sem = lambda n: ctx.enter_context(nc.semaphore(n))
        ident, rgu, rdn, eid = t["ident"], t["rgu"], t["rdn"], t["eid"]
        xs = sb("xs", [P, 2, D])
        xT = sb("xT", [P, 2, DC, P])
        sg = sb("sg4", [P, 2, F])
        hid = sb("hid4", [P, 2, F])
        hT = sb("hT4", [P, 2, FC, P])
        y = sb("y4", [P, 2, D])
        pX, pH = ps("rX"), ps("rH")
        pG, pU, pY = ([ps(f"r{n}{i}") for i in range(2)] for n in "GUY")
        xs_in = [sem(f"xs_in{k}") for k in range(2)]
        y_out = [sem(f"y4_out{k}") for k in range(2)]
        xt_full, xt_done = sem("xt4_full"), sem("xt4_done")
        g_full, u_full, silu_done, hid_done = sem("g4_full"), sem("u4_full"), sem("silu4"), sem("hid4")
        h_full, h_done, y_full, y_done = sem("h4_full"), sem("h4_done"), sem("y4_full"), sem("y4_done")
        early = lambda n, k: isinstance(n, int) and n < k

        with nc.Block() as block:

            @block.tensor
            def _(pe):
                def x_transpose(s, k):
                    pe.wait_ge(xs_in[k], 8 * (s - k) + 16)
                    if not early(s, 1):
                        pe.wait_ge(xt_done, s)
                    for c in range(DC):
                        mm = pe.transpose(pX[:, c * P:(c + 1) * P], xs[:, k, c * P:(c + 1) * P], ident[:])
                    mm.then_inc(xt_full, 1)

                def gate_up(s, k):
                    e = pe.value_load(eid[0:1, bass.ds(s, 1)], min_val=0, max_val=NE - 1)
                    pe.wait_ge(xt_done, s + 1)
                    for bank, off, free, full in ((pG[k], 0, silu_done, g_full), (pU[k], F, hid_done, u_full)):
                        if not early(s, 2):
                            pe.wait_ge(free, s - 1)
                        for c in range(DC):
                            mm = pe.matmul(bank[:], xT[:, k, c, :],
                                           rgu[:, c, bass.ds(e, 1), off:off + F].rearrange("p o n -> p (o n)"),
                                           start=(c == 0), stop=(c == DC - 1))
                        mm.then_inc(full, 1)
                    return e

                def h_transpose(s, k):
                    pe.wait_ge(hid_done, s + 1)
                    if not early(s, 1):
                        pe.wait_ge(h_done, s)
                    for m in range(FC):
                        mm = pe.transpose(pH[:, m * P:(m + 1) * P], hid[:, k, m * P:(m + 1) * P], ident[:])
                    mm.then_inc(h_full, 1)

                def down(s, k):
                    e = pe.value_load(eid[0:1, bass.ds(s, 1)], min_val=0, max_val=NE - 1)
                    pe.wait_ge(h_done, s + 1)
                    if not early(s, 2):
                        pe.wait_ge(y_done, s - 1)
                    for m in range(FC):
                        mm = pe.matmul(pY[k][:, 0:D], hT[:, k, m, :],
                                       rdn[:, m, bass.ds(e, 1), :].rearrange("p o n -> p (o n)"),
                                       start=(m == 0), stop=(m == FC - 1))
                    mm.then_inc(y_full, 1)

                def step(s, k):
                    x_transpose(s + 1, 1 - k)
                    h_transpose(s, k)
                    gate_up(s + 1, 1 - k)
                    down(s, k)

                x_transpose(0, 0)
                gate_up(0, 0)
                step(0, 0)
                step(1, 1)
                with pe.Fori(1, ST // 2) as i:
                    step(2 * i, 0)
                    step(2 * i + 1, 1)
                h_transpose(ST - 1, 0)
                down(ST - 1, 0)

            @block.scalar
            def _(act):
                def x_evac(s, k):
                    act.wait_ge(xt_full, s + 1)
                    if not early(s, 2):
                        act.wait_ge(u_full, s - 1)
                    act.activation(xT[:, k], pX[:, 0:D].rearrange("p (c n) -> p c n", c=DC), ACT.Copy).then_inc(xt_done, 1)

                def silu(s, k):
                    act.wait_ge(g_full, s + 1)
                    if not early(s, 2):
                        act.wait_ge(hid_done, s - 1)
                    act.activation(sg[:, k, :], pG[k][:], ACT.Silu).then_inc(silu_done, 1)

                def y_evac(s, k):
                    act.wait_ge(y_full, s + 1)
                    if not early(s, 2):
                        act.wait_ge(y_out[k], 8 * (s - k))
                    act.activation(y[:, k, :], pY[k][:, 0:D], ACT.Copy).then_inc(y_done, 1)

                def step(s, k):
                    x_evac(s + 1, 1 - k)
                    silu(s + 1, 1 - k)
                    y_evac(s, k)

                x_evac(0, 0)
                silu(0, 0)
                step(0, 0)
                step(1, 1)
                with act.Fori(1, ST // 2) as i:
                    step(2 * i, 0)
                    step(2 * i + 1, 1)
                y_evac(ST - 1, 0)

            @block.vector
            def _(dve):
                def hidden(s, k):
                    dve.wait_ge(silu_done, s + 1)
                    dve.wait_ge(u_full, s + 1)
                    if not early(s, 2):
                        dve.wait_ge(h_full, s - 1)
                    dve.tensor_tensor(hid[:, k, :], pU[k][:], sg[:, k, :], ALU.mult).then_inc(hid_done, 1)

                def h_evac(s, k):
                    dve.wait_ge(h_full, s + 1)
                    if not early(s, 2):
                        dve.wait_ge(y_full, s - 1)
                    dve.tensor_copy(hT[:, k], pH[:].rearrange("p (m n) -> p m n", m=FC)).then_inc(h_done, 1)

                def step(s, k):
                    h_evac(s, k)
                    hidden(s + 1, 1 - k)

                hidden(0, 0)
                step(0, 0)
                step(1, 1)
                with dve.Fori(1, ST // 2) as i:
                    step(2 * i, 0)
                    step(2 * i + 1, 1)
                h_evac(ST - 1, 0)

            @block.sync
            def _(sp):
                def load(s, k):
                    if not early(s, 2):
                        sp.wait_ge(xt_full, s - 1)
                    sp.dma_start(xs[:, k, :], d["sorted"][bass.ds(s * P, P), :]).then_inc(xs_in[k], 16)

                def store(s, k):
                    sp.wait_ge(y_done, s + 1)
                    sp.dma_start(d["ysorted"][bass.ds(s * P, P), :], y[:, k, :]).then_inc(y_out[k], 16)

                load(0, 0)
                load(1, 1)
                with sp.Fori(0, ST // 2) as i:
                    load(2 * i + 2, 0)
                    store(2 * i, 0)
                    if True:
                        load(2 * i + 3, 1)
                    store(2 * i + 1, 1)
                store(ST - 1, 0)
                sp.wait_ge(y_out[0], 16 * (ST // 2 + 1))
                sp.wait_ge(y_out[1], 16 * (ST // 2))


def combine(nc, d, t):
    with ExitStack() as ctx:
        sb = lambda n, s, dt=F32: ctx.enter_context(nc.sbuf_tensor(n, s, dt))
        sem = lambda n: ctx.enter_context(nc.semaphore(n))
        yg = sb("yg", [P, NT, D])
        x2 = sb("x2", [P, NT, D])
        bg = sb("bg5", [P, B, D])
        g_in, x_in, b_in, gated, summed, out_s = sem("g5_in"), sem("x5_in"), sem("b5_in"), sem("gated"), sem("summed"), sem("out_stored")
        g_in = [sem(f"g5_in{b}") for b in range(B)]
        with nc.Block() as block:

            @block.gpsimd
            def _(pool):
                for k in range(NT):
                    pool.indirect_dma_start(
                        out=yg[:, k, :], out_offset=None, in_=d["ysorted"],
                        in_offset=bass.IndirectOffsetOnAxis(ap=t["slots"][:, k:k + 1].bitcast(U32), axis=0),
                    ).then_inc(g_in[k // KT], 16)

            @block.sync
            def _(sp):
                sp.dma_start(bg[:], d["mod"][:, 5 * D:6 * D][None].broadcast_to([P, B, D])).then_inc(b_in, 16)
                sp.dma_start(x2[:], d["x2"].rearrange("(k p) n -> p k n", p=P)).then_inc(x_in, 16)
                for b in range(B):
                    sp.wait_ge(summed, b + 1)
                    sp.dma_start(d["out"][b * S:(b + 1) * S, :].rearrange("(k p) n -> p k n", p=P),
                                 x2[:, b * KT:(b + 1) * KT, :]).then_inc(out_s, 16)
                sp.wait_ge(out_s, 16 * B)

            @block.vector
            def _(dve):
                dve.wait_ge(b_in, 16)
                dve.wait_ge(x_in, 16)
                for b in range(B):
                    rows = slice(b * KT, (b + 1) * KT)
                    dve.wait_ge(g_in[b], 16 * KT)
                    dve.tensor_tensor(yg[:, rows, :], yg[:, rows, :], bg[:, b, None, :].broadcast_to([P, KT, D]),
                                      ALU.mult).then_inc(gated, 1)
                    dve.wait_ge(gated, b + 1)
                    dve.tensor_tensor(x2[:, rows, :], x2[:, rows, :], yg[:, rows, :], ALU.add).then_inc(summed, 1)


def program(nc, d):
    with ExitStack() as whole:
        keep = lambda n, s, dt=F32: whole.enter_context(nc.sbuf_tensor(n, s, dt))
        t = {"ident": keep("ident", [P, P]), "slots": keep("slots", [P, NT], I32), "eid": keep("eid", [P, 40], I32),
             "best": keep("best", [P, NT]), "onehot": keep("onehot", [P, NT, NE]), "experts": keep("experts", [P, NE]),
             "big_in": whole.enter_context(nc.semaphore("big_in"))}
        with ExitStack() as ctx:
            sb = lambda n, s, dt=F32: ctx.enter_context(nc.sbuf_tensor(n, s, dt))
            t |= {
                "wh": sb("wh", [P, DC, 4 * D], F32R), "wl": sb("wl", [P, DC, 4 * D], F32R),
                "rope": sb("rope", [P, 2, S]), "mask": sb("mask", [P, S]),
                "modT": sb("modT", [P, 4, B]),
                "sel": sb("sel", [P, 4, 4, P], F32R), "ones": sb("key_ones", [P, 1]),
                "qs": sb("qs", [P, NH // 2, S], F32R), "ks": sb("ks", [P, NH, S], F32R),
                "vaug": sb("vaug", [P, KT, NH, 32]),
            }
            setup(nc, d, t)
            attention(nc, d, t)
        with ExitStack() as ctx:
            sb = lambda n, s, dt=F32: ctx.enter_context(nc.sbuf_tensor(n, s, dt))
            t |= {"rgu": sb("rgu", [P, DC, NE, 2 * F]), "rdn": sb("rdn", [P, FC, NE, D])}
            with ExitStack() as rows:
                t["h2all"] = rows.enter_context(nc.sbuf_tensor("h2all", [P, NT, D], F32))
                shared_expert(nc, d, t)
                route(nc, d, t)
            routed_experts(nc, d, t)
        combine(nc, d, t)


def kernel(**inputs):
    import numpy as _np
    import concourse.bacc as _bacc
    from concourse.bass_utils import run_bass_kernel_spmd as _run

    i = {k: _np.asarray(v) for k, v in inputs.items()}
    arrays = {
        "x": i["L0_attn_x"].reshape(B * S, D),
        "cT": i["L0_c"].T, "wmod": i["L0_wmod"],
        "qw": i["L0_attn_qw"], "kw": i["L0_attn_kw"], "vw": i["L0_attn_vw"], "ow": i["L0_attn_ow"],
        "wr": i["L0_ffn_gate_w"].T,
        "sgu": _np.concatenate([i["L0_ffn_shared_gate"], i["L0_ffn_shared_up"]], axis=0).T,
        "sdn": i["L0_ffn_shared_down"].T,
        "rgu": _np.concatenate([i["L0_ffn_r_gate"], i["L0_ffn_r_up"]], axis=1).transpose(2, 0, 1),
        "rdn": i["L0_ffn_r_down"].transpose(2, 0, 1),
        **constants(),
    }
    arrays = {f"in_{k}": _np.ascontiguousarray(v) for k, v in arrays.items()}
    nc = _bacc.Bacc("TRN2", target_bir_lowering=False, num_devices=1)
    d = {k[3:]: nc.dram_tensor(k, v.shape, mybir.dt.from_np(v.dtype), kind="ExternalInput").ap()
         for k, v in arrays.items()}
    for name, shape in (("mod", (B, 6 * D)), ("x1", (B * S, D)), ("x2", (B * S, D)),
                        ("sorted", ((ST + 1) * P, D)), ("ysorted", (ST * P, D))):
        d[name] = nc.dram_tensor(f"scratch_{name}", shape, F32, kind="Internal").ap()
    d["out"] = nc.dram_tensor("out_0", (B * S, D), F32, kind="ExternalOutput").ap()
    program(nc, d)
    r = _run(nc, [arrays], core_ids=[0])
    return r.results[0]["out_0"].reshape(B, S, D)
```

```python
from contextlib import ExitStack

import concourse.bass as bass
import numpy as np
from concourse import mybir

F32 = mybir.dt.float32
F32R = mybir.dt.float32r
BF16 = mybir.dt.bfloat16
I32 = mybir.dt.int32
U32 = mybir.dt.uint32
ALU = mybir.AluOpType
ACT = mybir.ActivationFunctionType
AX = mybir.AxisListType

P = 128
B, S, D = 8, 512, 256
NH, HD = 16, 16
F, NE = 512, 8
KT = S // P
DC = D // P
FC = F // P
NT = B * KT
ST = NT + NE - 1
GH = 4
NG = NH // GH
PAIRW = 2 * 1280
MAXB = 10
EXPB = 10
RE = B * S + P
SPARE = NE * RE
RW = D + 2
EPS = 1e-5
NEG = -1e10


def constants():
    row = np.arange(P) % HD
    inv = (1.0 / np.float32(10000.0) ** (np.arange(0, HD, 2, dtype=np.float32) / HD)).astype(np.float32)
    ang = (np.arange(S, dtype=np.float32)[None, :] * inv[row // 2][:, None]).astype(np.float32)
    cos, sin = np.cos(ang), np.sin(ang) * np.where(row % 2 == 0, -1.0, 1.0)[:, None]
    rope = np.stack([cos, sin], axis=1).astype(np.float32)
    ident = np.eye(P, dtype=np.float32)
    mask = np.zeros((P, S), np.float32)
    mask[:, S - P:] = np.where(np.arange(P)[None, :] > np.arange(P)[:, None], NEG, 0.0)
    before = (np.arange(P)[:, None] < np.arange(P)[None, :]).astype(np.float32)
    experts = np.broadcast_to(np.arange(NE, dtype=np.float32), (P, NE))
    sel = np.zeros((4, P, 4, P), np.float32)
    for pair in range(4):
        for s_ in range(2):
            for e in range(HD):
                for kind, parts in enumerate(((0, 1), (2,), (0, 2), (1,))):
                    for part in parts:
                        sel[kind, 32 * pair + HD * s_ + e, pair, 64 * s_ + HD * part + e] = HD ** -0.5 if kind < 2 else 1.0
    ones = np.zeros((P, 1), np.float32)
    ones[48::64] = 1.0
    starts = np.broadcast_to(P * np.arange(40, dtype=np.float32)[:, None], (P, 40, NE))
    token = np.arange(P)[:, None] + P * np.arange(NT)[None, :]
    return {
        "c_rope": rope, "c_ident": ident, "c_mask": mask, "c_before": before,
        "c_sel": np.ascontiguousarray(sel.transpose(1, 0, 2, 3)), "c_ones": ones,
        "c_tokens": np.stack([token, token // S], axis=2).astype(np.int32),
        "c_padding": np.stack([B * S + np.arange(P), np.full(P, B)], axis=1).astype(np.int32),
        "c_experts": np.ascontiguousarray(experts), "c_starts": np.ascontiguousarray(starts),
    }


RSQRT_STEPS = 14
RANK_STEPS = 6


def wait_apart(eng, sem, value):
    eng.wait_ge(sem, value)
    if not isinstance(value, int):
        eng.nop(nofuse=True)


def rsqrt_steps(pool, step, base, out, var, v, a):
    n = 0

    def then(ins):
        nonlocal n
        n += 1
        ins.then_inc(step, 1)
        wait_apart(pool, step, base + n)

    then(pool.tensor_scalar(v, var, EPS, None, ALU.add))
    then(pool.tensor_scalar(out.bitcast(I32), v.bitcast(I32), -0.5, float(0x5F3759DF), ALU.mult, ALU.add))
    for _ in range(3):
        then(pool.tensor_tensor(a, out, out, ALU.mult))
        then(pool.tensor_tensor(a, a, v, ALU.mult))
        then(pool.tensor_scalar(a, a, -0.5, 1.5, ALU.mult, ALU.add))
        then(pool.tensor_tensor(out, out, a, ALU.mult))
    assert n == RSQRT_STEPS


def setup(nc, d, t):
    with ExitStack() as ctx:
        sb = lambda n, s, dt=F32: ctx.enter_context(nc.sbuf_tensor(n, s, dt))
        sem = lambda n: ctx.enter_context(nc.semaphore(n))
        w32 = sb("w32", [P, DC, 4 * D])
        sel32 = sb("sel32", [P, 4, 4, P])
        wmod = sb("wmod", [P, DC, 6 * D])
        cT = sb("cT", [P, DC, B])
        ce = sb("ce", [P, DC, B])
        sc = sb("sc", [P, DC, B])
        modrow = sb("modrow", [B, 6 * D])
        sgn = sb("sgn", [B, 2, D])
        pm = [ctx.enter_context(nc.psum_tensor(f"pm{i}", [P, 512], F32)) for i in range(3)]
        pt = ctx.enter_context(nc.psum_tensor("pt", [P, 512], F32))
        loaded, cloaded, split = sem("set_loaded"), sem("set_cloaded"), sem("set_split")
        scdone, rows, cols = sem("set_sc"), sem("set_rows"), sem("set_cols")
        ex, rowsb, stored = sem("set_exp"), sem("set_rowsb"), sem("set_stored")
        tables, sel_in = sem("set_tables"), sem("sel_in")
        with nc.Block() as block:

            @block.sync
            def _(sp):
                sp.dma_start(cT[:], d["cT"].rearrange("(c p) b -> p c b", p=P)).then_inc(cloaded, 16)
                sp.dma_start(wmod[:], d["wmod"].rearrange("(c p) n -> p c n", p=P)).then_inc(cloaded, 16)
                for i, n in enumerate(("qw", "kw", "vw", "ow")):
                    sp.dma_start(w32[:, :, i * D:(i + 1) * D],
                                 d[n].rearrange("(c p) n -> p c n", p=P)).then_inc(loaded, 16)
                sp.dma_start(t["rope"][:], d["c_rope"]).then_inc(tables, 16)
                sp.dma_start(t["ident"][:], d["c_ident"]).then_inc(tables, 16)
                sp.dma_start(t["mask"][:], d["c_mask"]).then_inc(tables, 16)
                sp.dma_start(t["ones"][:], d["c_ones"]).then_inc(tables, 16)
                sp.dma_start(sel32[:], d["c_sel"]).then_inc(sel_in, 16)
                sp.wait_ge(rowsb, 3)
                sp.dma_start(d["mod"], modrow[:]).then_inc(stored, 16)
                sp.dma_start(d["gb"][0:B, :], modrow[:, 5 * D:6 * D]).then_inc(stored, 16)
                sp.dma_start(d["gb"][B:B + 1, :], modrow[0:1, 5 * D:6 * D]).then_inc(stored, 16)
                sp.wait_ge(stored, 48)
                sp.wait_ge(tables, 64)

            @block.scalar
            def _(act):
                act.wait_ge(cloaded, 32)
                act.activation(ce[:], cT[:], ACT.Exp, scale=-1.0).then_inc(ex, 1)
                act.wait_ge(sel_in, 16)
                act.activation(t["sel"][:], sel32[:], ACT.Copy)

            @block.vector
            def _(dve):
                dve.wait_ge(ex, 1)
                dve.tensor_scalar(ce[:], ce[:], 1.0, None, ALU.add).then_inc(scdone, 1)
                dve.wait_ge(scdone, 1)
                dve.reciprocal(ce[:], ce[:]).then_inc(scdone, 1)
                dve.wait_ge(scdone, 2)
                dve.tensor_tensor(sc[:], cT[:], ce[:], ALU.mult).then_inc(scdone, 1)
                dve.wait_ge(loaded, 64)
                dve.tensor_copy(t["wh"][:], w32[:]).then_inc(split, 1)
                dve.wait_ge(cols, 1)
                dve.tensor_copy(t["modT"][:, 0:2, :], pt[:, 0:16].rearrange("p (k b) -> p k b", b=B)).then_inc(split, 1)
                dve.tensor_scalar(t["modT"][:, 2:4, :], pt[:, 16:32].rearrange("p (k b) -> p k b", b=B),
                                  1.0, None, ALU.add).then_inc(split, 1)
                dve.wait_ge(rows, 1)
                dve.tensor_copy(modrow[:, 0:512], pm[0][0:B, :]).then_inc(rowsb, 1)
                dve.tensor_copy(modrow[:, 768:1024], pm[1][0:B, 256:512]).then_inc(rowsb, 1)
                dve.tensor_scalar(modrow[:, 1024:1280], pm[2][0:B, 0:256], 1.0, None, ALU.add)
                gates = [(pm[1][0:B, 0:256], modrow[:, 512:768]), (pm[2][0:B, 256:512], modrow[:, 1280:1536])]
                n = 3
                for k, (g, out) in enumerate(gates):
                    dve.tensor_scalar(sgn[:, k, :], g, 0.0, 2.0, ALU.is_ge, ALU.mult).then_inc(scdone, 1)
                    dve.wait_ge(scdone, n + 1)
                    dve.tensor_scalar(sgn[:, k, :], sgn[:, k, :], -1.0, None, ALU.add).then_inc(scdone, 1)
                    dve.wait_ge(scdone, n + 2)
                    dve.tensor_tensor(out, g, sgn[:, k, :], ALU.mult).then_inc(scdone, 1)
                    dve.wait_ge(scdone, n + 3)
                    n += 3
                    ins = dve.scalar_tensor_tensor(out, out, 0.25, sgn[:, k, :], ALU.max, ALU.mult)
                ins.then_inc(rowsb, 1)

            @block.gpsimd
            def _(pool):
                pool.memset(t["ks"][:].bitcast(F32), 0.0)
                pool.memset(t["vaug"][:], 1.0)
                pool.wait_ge(split, 1)
                pool.tensor_tensor(t["wl"][:], w32[:], t["wh"][:].bitcast(F32), ALU.subtract)

            @block.tensor
            def _(pe):
                pe.wait_ge(scdone, 3)
                for k in range(4):
                    for c in range(DC):
                        mm = pe.matmul(pt[:, k * B:(k + 1) * B], wmod[:, c, k * P:(k + 1) * P], sc[:, c, :],
                                       start=(c == 0), stop=(c == DC - 1))
                mm.then_inc(cols, 1)
                for k in range(3):
                    for c in range(DC):
                        mm = pe.matmul(pm[k][0:B, :], sc[:, c, :], wmod[:, c, k * 512:(k + 1) * 512],
                                       start=(c == 0), stop=(c == DC - 1))
                mm.then_inc(rows, 1)


def max_banks():
    return ([[(2, h, 0), (0, h, 384)] for h in range(GH)] + [[(1, h, 0), (1, h + 2, 256)] for h in range(2)]
            + [[(3, h, 0)] for h in range(GH)])


def exp_banks():
    out = []
    for pair in range(2):
        for u in range(2):
            h, base = pair + 2 * u, pair * PAIRW + u * 1024
            out.append(([(0, h, 0)], base))
            out.append(([(1, h, 0), (3, h, 384)], base + 512))
        out.append(([(2, pair, 0), (2, pair + 2, 256)], pair * PAIRW + 2048))
    return out


def prob_column(kt, h):
    base, u = (h % 2) * PAIRW, h // 2
    return base + {0: u * 1024, 1: u * 1024 + 512, 3: u * 1024 + 896, 2: 2048 + u * 256}[kt]


PRODUCTS = ((0, 0), (0, 1), (1, 0))


def attention(nc, d, t):
    with ExitStack() as ctx:
        sb = lambda n, s, dt=F32: ctx.enter_context(nc.sbuf_tensor(n, s, dt))
        ps = lambda n: ctx.enter_context(nc.psum_tensor(n, [P, 512], F32))
        sem = lambda n: ctx.enter_context(nc.semaphore(n))
        W = (t["wh"], t["wl"])
        ident, mask, rope, modT = t["ident"], t["mask"], t["rope"], t["modT"]
        qs, ks, vaug, sel, ones = t["qs"], t["ks"], t["vaug"], t["sel"], t["ones"]
        xb = sb("xb", [P, KT, D])
        xn = sb("xn", [P, KT, D])
        att = xn
        stats = sb("stats", [P, KT, 6])
        mv = sb("mv", [P, KT, 2])
        rstd, nv, na = sb("rstd", [P, KT]), sb("nv", [P, KT]), sb("na", [P, KT])
        ht32 = sb("ht32", [P, DC, S])
        hT = (sb("hTh", [P, DC, S], F32R), sb("hTl", [P, DC, S], F32R))
        qk = sb("qk", [P, 4, S])
        qkl = sb("qkl", [P, 4, S], F32R)
        qksw = sb("qksw", [P, 4, S])
        qkh = sb("qkh", [P, 4, S], F32R)
        mx = sb("mx", [P, 2, KT, GH])
        mrow = [sb(f"mrow{i}", [GH, S], F32R) for i in range(2)]
        probs = sb("probs", [P, 2, 2 * PAIRW])
        oT = sb("oT", [P, NG, S])
        rden = sb("rden", [P, KT, NH])
        attT = (sb("attTh", [P, DC, S], F32R), sb("attTl", [P, DC, S], F32R))
        gab = sb("gab", [P, D])
        xr = sb("xr", [P, KT, D])
        yo = sb("yo", [P, 2, D])
        pM, pS, pO, pX = ([ps(f"p{n}{i}") for i in range(2)] for n in "MSOX")

        x_in, x_free = sem("x_in"), sem("x_free")
        ln_a, ln_b, ln_s = sem("ln_stats"), sem("ln_rstd"), sem("ln_step")
        xn_done = sem("xn_done")
        v_full, qk_full, xt_full = sem("v_full"), sem("qk_full"), sem("xt_full")
        v_ready, th_done, tl_done, qk_ev = sem("v_ready"), sem("th_done"), sem("tl_done"), sem("qk_ev")
        swapped, rope1, rope2, rope3 = sem("swapped"), sem("rope1"), sem("rope2"), sem("rope3")
        qkh_done, qkl_done = sem("qkh_done"), sem("qkl_done")
        hh_done, stk_full, qs_done, ks_done, ks3_done = sem("hh_done"), sem("stk_full"), sem("qs_done"), sem("ks_done"), sem("ks3_done")
        m_full, m_free, s_full, s_free = sem("m_full"), sem("m_free"), sem("s_full"), sem("s_free")
        neg_full, mrow_done, mrow_in = sem("neg_full"), sem("mrow_done"), sem("mrow_in")
        sel_done, o_full, o_free = sem("sel_done"), sem("o_full"), sem("o_free")
        ot_full, rd_done, att_done = sem("ot_full"), sem("rd_done"), sem("att_done")
        at_full, ath_done, atl_done = sem("at_full"), sem("ath_done"), sem("atl_done")
        y_full, y_ga, x1_done, x1_out = sem("y_full"), sem("y_ga"), sem("x1_done"), sem("x1_out")
        aux_in = sem("aux_in")

        QK_BANKS = (pM[1], pS[1], pX[1], pX[0])
        STACK_BANKS = (pX, pS, pM, pX)

        with nc.Block() as block:

            @block.tensor
            def _(pe):
                read = [None, None]

                def take(k, signal, value):
                    if read[k] is not None:
                        pe.wait_ge(*read[k])
                    read[k] = (signal, value)
                    return pX[k]

                def max_bank(b, g, i):
                    n = 10 * (4 * b + g) + i
                    if not (isinstance(n, int) and n < 2):
                        pe.wait_ge(m_free, n - 1)
                    for qt, h, col in max_banks()[i]:
                        hh = GH * g + h
                        mm = pe.matmul(pM[i % 2][:, col:col + P * (qt + 1)],
                                       qs[:, hh // 2, qt * P:qt * P + P], ks[:, hh, 0:P * (qt + 1)], start=True, stop=True)
                    mm.then_inc(m_full, 1)

                def exp_bank(b, g, i):
                    n = 40 * b + 10 * g + i
                    if not (isinstance(n, int) and n < 2):
                        pe.wait_ge(s_free, n - 1)
                    for kt, h, col in exp_banks()[i][0]:
                        hh = GH * g + h
                        mm = pe.matmul(pS[i % 2][:, col:col + S - kt * P],
                                       ks[:, hh, kt * P:kt * P + P], qs[:, hh // 2, kt * P:S], start=True, stop=True)
                    mm.then_inc(s_full, 1)
                    return mm

                def group(b, g, nxt, vals=None, more=True):
                    pe.wait_ge(mrow_in, 32 * (4 * b + g + 1))
                    if nxt is not None and nxt[1] < 2:
                        n = 2 * nxt[0] + nxt[1]
                        pe.wait_ge(qs_done, 4 * n + 3)
                        pe.wait_ge(ks_done, 3 * n + 3)
                        if nxt[1] == 1:
                            pe.wait_ge(ks3_done, n)
                    if g == 1:
                        pe.wait_ge(qs_done, 8 * (b + 1))
                        pe.wait_ge(ks3_done, 2 * (b + 1))
                    if g == 1:
                        pe.wait_ge(v_ready, 2 * (b + 1))
                        if more:
                            pe.wait_ge(rope1, 4 * (b + 1) + 2)
                    for i in range(MAXB):
                        exp_bank(b, g, i)
                        if nxt is not None:
                            max_bank(*nxt, i)
                        if vals is not None and i in (2, 4, 6, 8):
                            values(*vals, i // 2 - 1)

                def negate(b, g):
                    s = 4 * b + g
                    bank = pM[0]
                    pe.wait_ge(m_free, 10 * (s + 1))
                    for qt in range(KT):
                        mm = pe.transpose(bank[0:GH, qt * P:(qt + 1) * P], mx[:, g % 2, qt, :], ident[:])
                    mm.then_inc(neg_full, 1)

                def values(b, g, kt):
                    s = 4 * b + g
                    if kt == 0:
                        pe.wait_ge(sel_done, 2 * (s + 1))
                        if not (isinstance(s, int) and s < 2):
                            pe.wait_ge(o_free, s - 1)
                    for h in range(GH):
                        at = prob_column(kt, h)
                        mm = pe.matmul(pO[g % 2][32 * h:32 * h + 32, kt * P:S],
                                       vaug[:, kt, GH * g + h, :],
                                       probs[:, g % 2, at:at + S - kt * P],
                                       start=(kt == 0), stop=(kt == KT - 1))
                    if kt == KT - 1:
                        mm.then_inc(o_full, 1)

                def v_proj(b, halves):
                    for half in halves:
                        if half == 0:
                            bank = take(0, v_ready, 2 * b + 1)
                        else:
                            bank = pS[0]
                            pe.wait_ge(s_free, 40 * b + 10)
                        for k2 in range(2):
                            kt = 2 * half + k2
                            for n, (c, (s_, m_)) in enumerate((c, p) for c in range(DC) for p in PRODUCTS):
                                mm = pe.matmul(bank[:, k2 * D:(k2 + 1) * D], hT[s_][:, c, kt * P:(kt + 1) * P],
                                               W[m_][:, c, 2 * D:3 * D], start=(n == 0), stop=(n == 5))
                        mm.then_inc(v_full, 1)

                def x_transpose(b):
                    pe.wait_ge(xn_done, 4 * (b + 1))
                    for c in range(DC):
                        bank = take(c, th_done, 2 * b + c + 1)
                        for kt in range(KT):
                            mm = pe.transpose(bank[:, kt * P:(kt + 1) * P], xn[:, kt, c * P:(c + 1) * P], ident[:])
                        mm.then_inc(xt_full, 1)

                def qk_proj(b):
                    pe.wait_ge(tl_done, 2 * (b + 1))
                    for i in range(4):
                        bank = QK_BANKS[i] if i < 2 else take((i + 1) % 2, rope1, 4 * b + i + 1)
                        for n, (c, (s_, m_)) in enumerate((c, p) for c in range(DC) for p in PRODUCTS):
                            mm = pe.matmul(bank[:], W[s_][:, c, i * P:(i + 1) * P], hT[m_][:, c, :],
                                           start=(n == 0), stop=(n == 5))
                        mm.then_inc(qk_full, 1)

                def stacks(b, half, pairs):
                    pe.wait_ge(qkl_done, b + 1)
                    n = 2 * b + half
                    for pair in pairs:
                        for k in range(2):
                            bank = STACK_BANKS[pair][k]
                            if pair == 0:
                                take(k, (qs_done, ks3_done)[k], (4 * n + 4, n + 1)[k])
                            elif pair == 1 and not (isinstance(n, int) and n < 2):
                                pe.wait_ge(s_free, 40 * b + 10 * half - 10)
                            elif pair == 2 and k == 0 and not (isinstance(n, int) and n < 2):
                                pe.wait_ge(mrow_done, 4 * b + half)
                            elif pair == 3:
                                pe.wait_ge((qs_done, ks_done)[k], (4 * n + 1, 3 * n + 1)[k])
                            pe.matmul(bank[:], sel[:, 2 * k, pair, :], qkh[:, 2 * k + half, :], start=True, stop=False)
                            pe.matmul(bank[:], sel[:, 2 * k + 1, pair, :], qkl[:, 2 * k + half, :],
                                      start=False, stop=True).then_inc(stk_full, 1)

                def out_transpose(b, tiles):
                    pe.wait_ge(o_free, 4 * (b + 1))
                    for qt in tiles:
                        bank = take((qt + 1) % 2, att_done, 4 * b + qt + 1)
                        for g in range(NG):
                            mm = pe.transpose(bank[:, g * P:(g + 1) * P], oT[:, g, qt * P:(qt + 1) * P], ident[:])
                        mm.then_inc(ot_full, 1)

                def att_transpose(b):
                    pe.wait_ge(att_done, 4 * (b + 1))
                    for c in range(DC):
                        bank = take(c, atl_done, 2 * b + c + 1)
                        for qt in range(KT):
                            mm = pe.transpose(bank[:, qt * P:(qt + 1) * P], att[:, qt, c * P:(c + 1) * P], ident[:])
                        mm.then_inc(at_full, 1)

                def out_proj(b):
                    pe.wait_ge(atl_done, 2 * (b + 1))
                    for half in range(2):
                        bank = take(half, y_ga, 2 * b + half + 1)
                        for q2 in range(2):
                            qt = 2 * half + q2
                            for n, (c, (s_, m_)) in enumerate((c, p) for c in range(DC) for p in PRODUCTS):
                                mm = pe.matmul(bank[:, q2 * D:(q2 + 1) * D], attT[s_][:, c, qt * P:(qt + 1) * P],
                                               W[m_][:, c, 3 * D:4 * D], start=(n == 0), stop=(n == 5))
                        mm.then_inc(y_full, 1)

                def batch(b, first=False, nxt=True, nxt2=True):
                    group(b, 0, (b, 1), None if first else (b - 1, 3))
                    v_proj(b, [0])
                    negate(b, 1)
                    if not first:
                        out_transpose(b - 1, [0, 1])
                    v_proj(b, [1])
                    if not first:
                        out_transpose(b - 1, [2, 3])
                    if nxt:
                        qk_proj(b + 1)
                    group(b, 1, (b, 2), (b, 0), more=nxt)
                    if not first:
                        att_transpose(b - 1)
                    negate(b, 2)
                    if not first:
                        out_proj(b - 1)
                    group(b, 2, (b, 3), (b, 1))
                    if nxt:
                        stacks(b + 1, 0, [0])
                    negate(b, 3)
                    if nxt:
                        stacks(b + 1, 0, [1, 2, 3])
                    group(b, 3, (b + 1, 0) if nxt else None, (b, 2))
                    if nxt2:
                        x_transpose(b + 2)
                    if nxt:
                        negate(b + 1, 0)
                        stacks(b + 1, 1, range(4))

                x_transpose(0)
                qk_proj(0)
                x_transpose(1)
                stacks(0, 0, range(4))
                pe.wait_ge(qs_done, 4)
                pe.wait_ge(ks_done, 3)
                pe.wait_ge(ks3_done, 1)
                for i in range(MAXB):
                    max_bank(0, 0, i)
                negate(0, 0)
                pe.wait_ge(mrow_done, 1)
                stacks(0, 1, range(4))
                batch(0, first=True)
                with pe.Fori(1, B - 2) as b:
                    read[:] = (qs_done, 8 * b + 8), (ks3_done, 2 * b + 2)
                    batch(b)
                read[:] = (qs_done, 8 * B - 8), (ks3_done, 2 * B - 2)
                batch(B - 2, nxt2=False)
                batch(B - 1, nxt=False, nxt2=False)
                for kt in range(KT):
                    values(B - 1, 3, kt)
                out_transpose(B - 1, range(KT))
                att_transpose(B - 1)
                out_proj(B - 1)

            @block.scalar
            def _(act):
                def exps(b, g, rotated=None):
                    s = 4 * b + g
                    if not (isinstance(s, int) and s < 2):
                        act.wait_ge(o_full, s - 1)
                    for i, (_, at) in enumerate(exp_banks()):
                        act.wait_ge(s_full, 10 * s + i + 1)
                        act.activation(probs[:, g % 2, at:at + 512], pS[i % 2][:], ACT.Exp).then_inc(s_free, 1)
                        if rotated is not None and i in (0, 2, 4, 6):
                            rotated_high(rotated, i // 2)

                def max_row(b, g):
                    s = 4 * b + g
                    act.wait_ge(neg_full, s + 1)
                    if not (isinstance(s, int) and s < 2):
                        act.wait_ge(mrow_in, 32 * (s - 1))
                    act.activation(mrow[g % 2][:], pM[0][0:GH, :], ACT.Copy, scale=-1.0).then_inc(mrow_done, 1)

                def out_evac(b, g, more=True):
                    act.wait_ge(o_full, 4 * b + g + 1)
                    if g == 0 and not (isinstance(b, int) and b == 0):
                        act.wait_ge(ot_full, 4 * b)
                    if g == 0 and more:
                        act.wait_ge(rope3, b + 2)
                    act.activation(oT[:, g, :], pO[g % 2][:], ACT.Copy).then_inc(o_free, 1)

                def v_evac(b, halves):
                    for half in halves:
                        act.wait_ge(v_full, 2 * b + half + 1)
                        if half == 0 and not (isinstance(b, int) and b == 0):
                            act.wait_ge(o_full, 4 * b)
                        act.activation(vaug[:, 2 * half:2 * half + 2, :, 0:HD],
                                       (pX[0], pS[0])[half][:].rearrange("p (k h e) -> p k h e", k=2, h=NH),
                                       ACT.Copy).then_inc(v_ready, 1)

                def x_evac(b):
                    for c in range(DC):
                        act.wait_ge(xt_full, 2 * b + c + 1)
                        if c == 0 and not (isinstance(b, int) and b == 0):
                            act.wait_ge(tl_done, 2 * b)
                        scale, bias = modT[:, 2 + c, bass.ds(b, 1)], modT[:, c, bass.ds(b, 1)]
                        act.activation(ht32[:, c, :], pX[c][:], ACT.Identity, scale=scale, bias=bias).then_inc(th_done, 1)

                def high(b):
                    for c in range(DC):
                        act.wait_ge(th_done, 2 * b + c + 1)
                        if c == 0 and not (isinstance(b, int) and b == 0):
                            act.wait_ge(v_full, 2 * b)
                        act.activation(hT[0][:, c, :], ht32[:, c, :], ACT.Copy).then_inc(hh_done, 1)

                def rotated_high(b, i):
                    act.wait_ge(rope3, b + 1)
                    if i == 0 and not (isinstance(b, int) and b == 0):
                        act.wait_ge(stk_full, 16 * b)
                    act.activation(qkh[:, i, :], qk[:, i, :], ACT.Copy).then_inc(qkh_done, 1)

                def key_stacks(b, half):
                    for pair in range(3):
                        n = 8 * b + 4 * half + pair
                        act.wait_ge(stk_full, 2 * n + 2)
                        if pair == 0 and not (isinstance(b, int) and b == 0):
                            act.wait_ge(s_full, 40 * (b - 1) + 20 * half + 20)
                        bank = STACK_BANKS[pair][1]
                        for h in range(2):
                            half_rows = slice(64 * h, 64 * h + 64)
                            ins = act.activation(ks[half_rows, 8 * half + 2 * pair + h, :], bank[half_rows, :], ACT.Identity,
                                                 bias=ones[half_rows, :])
                        ins.then_inc(ks_done, 1)

                def qk_evac(b):
                    for i in range(4):
                        act.wait_ge(qk_full, 4 * b + i + 1)
                        if i == 0 and not (isinstance(b, int) and b == 0):
                            act.wait_ge(qkl_done, b)
                        act.activation(qk[:, i, :], QK_BANKS[i][:], ACT.Copy).then_inc(qk_ev, 1)

                def att_high(b):
                    for c in range(DC):
                        act.wait_ge(at_full, 2 * b + c + 1)
                        if c == 0 and not (isinstance(b, int) and b == 0):
                            act.wait_ge(y_full, 2 * b)
                        act.activation(attT[0][:, c, :], pX[c][:], ACT.Copy).then_inc(ath_done, 1)

                def batch(b, first=False, nxt=True, nxt2=True):
                    exps(b, 0)
                    if not first:
                        out_evac(b - 1, 3)
                    v_evac(b, [0])
                    max_row(b, 1)
                    if nxt:
                        high(b + 1)
                    v_evac(b, [1])
                    if nxt:
                        qk_evac(b + 1)
                    exps(b, 1)
                    if not first:
                        att_high(b - 1)
                    max_row(b, 2)
                    exps(b, 2, b + 1 if nxt else None)
                    max_row(b, 3)
                    if nxt:
                        key_stacks(b + 1, 0)
                    out_evac(b, 0, more=nxt)
                    out_evac(b, 1)
                    exps(b, 3)
                    if nxt2:
                        x_evac(b + 2)
                    if nxt:
                        max_row(b + 1, 0)
                        key_stacks(b + 1, 1)
                    out_evac(b, 2)

                x_evac(0)
                high(0)
                qk_evac(0)
                x_evac(1)
                for i in range(4):
                    rotated_high(0, i)
                key_stacks(0, 0)
                max_row(0, 0)
                key_stacks(0, 1)
                batch(0, first=True)
                with act.Fori(1, B - 2) as b:
                    batch(b)
                batch(B - 2, nxt2=False)
                batch(B - 1, nxt=False, nxt2=False)
                out_evac(B - 1, 3)
                att_high(B - 1)

            @block.vector
            def _(dve):
                def maxima(b, g):
                    s = 4 * b + g
                    if not (isinstance(s, int) and s < 2):
                        dve.wait_ge(neg_full, s - 1)
                    for i, bank in enumerate(max_banks()):
                        wait_apart(dve, m_full, 10 * s + i + 1)
                        for qt, h, col in bank:
                            w = P * (qt + 1)
                            scores = pM[i % 2][:, col:col + w]
                            ins = dve.tensor_tensor_reduce(
                                out=scores, in0=scores, in1=mask[:, S - w:S],
                                scale=1.0, scalar=-3e38, op0=ALU.add, op1=ALU.max,
                                accum_out=mx[:, g % 2, qt, h:h + 1])
                        ins.then_inc(m_free, 1)

                def ln_stats(b):
                    dve.wait_ge(x_in, 16 * (b + 1))
                    if not (isinstance(b, int) and b == 0):
                        dve.wait_ge(xn_done, 4 * b)
                    for k in range(KT):
                        ins = dve.bn_stats(stats[:, k, :], xb[:, k, :])
                    ins.then_inc(ln_s, 1)
                    wait_apart(dve, ln_s, 2 * b + 1)
                    for k in range(KT):
                        ins = dve.bn_aggr(mv[:, k, :], stats[:, k, :])
                    ins.then_inc(ln_s, 1)

                def low(b):
                    for c in range(DC):
                        dve.wait_ge(hh_done, 2 * b + c + 1)
                        dve.tensor_tensor(hT[1][:, c, :], ht32[:, c, :], hT[0][:, c, :].bitcast(F32),
                                          ALU.subtract).then_inc(tl_done, 1)

                def cosine(b):
                    if not (isinstance(b, int) and b < 2):
                        dve.wait_ge(ot_full, 4 * (b - 1))
                    for i in range(4):
                        dve.wait_ge(qk_ev, 4 * b + i + 1)
                        dve.tensor_tensor(oT[:, i, :], QK_BANKS[i][:], rope[:, 0, :], ALU.mult).then_inc(rope1, 1)

                def rotate(b):
                    dve.wait_ge(rope1, 4 * (b + 1))
                    dve.wait_ge(rope2, b + 1)
                    dve.tensor_tensor(qk[:], oT[:], qksw[:], ALU.add).then_inc(rope3, 1)

                def query_stacks(b, half):
                    for pair in range(4):
                        n = 8 * b + 4 * half + pair
                        dve.wait_ge(stk_full, 2 * n + 1)
                        if pair == 0 and not (isinstance(b, int) and b == 0):
                            dve.wait_ge(s_full, 40 * (b - 1) + 20 * half + 20)
                        dve.tensor_copy(qs[:, 4 * half + pair, :], STACK_BANKS[pair][0][:]).then_inc(qs_done, 1)
                    dve.wait_ge(stk_full, 16 * b + 8 * half + 8)
                    for h in range(2):
                        half_rows = slice(64 * h, 64 * h + 64)
                        ins = dve.tensor_scalar(ks[half_rows, 8 * half + 6 + h, :], STACK_BANKS[3][1][half_rows, :],
                                                ones[half_rows, :], None, ALU.add)
                    ins.then_inc(ks3_done, 1)

                def normalise(b, tiles):
                    for qt in tiles:
                        dve.wait_ge(ot_full, 4 * b + qt + 1)
                        o = pX[(qt + 1) % 2][:].rearrange("p (h e) -> p h e", e=32)
                        dve.reciprocal(rden[:, qt, :], o[:, :, HD]).then_inc(rd_done, 1)
                        dve.wait_ge(rd_done, 4 * b + qt + 1)
                        if qt == 0:
                            dve.wait_ge(xt_full, min(2 * b + 6, 2 * B) if isinstance(b, int) else 2 * b + 6)
                        dve.tensor_tensor(att[:, qt, :].rearrange("p (h e) -> p h e", e=HD), o[:, :, 0:HD],
                                          rden[:, qt, :, None].broadcast_to([P, NH, HD]), ALU.mult).then_inc(att_done, 1)

                def att_low(b):
                    for c in range(DC):
                        dve.wait_ge(ath_done, 2 * b + c + 1)
                        dve.tensor_tensor(attT[1][:, c, :], pX[c][:], attT[0][:, c, :].bitcast(F32),
                                          ALU.subtract).then_inc(atl_done, 1)

                def gate(b, halves):
                    dve.wait_ge(aux_in, 32 * (b + 1))
                    for half in halves:
                        dve.wait_ge(y_full, 2 * b + half + 1)
                        if half == 1 or not (isinstance(b, int) and b == 0):
                            dve.wait_ge(x1_done, 2 * b + half)
                        dve.tensor_tensor(yo[:], pX[half][:].rearrange("p (k n) -> p k n", k=2),
                                          gab[:, None, :].broadcast_to([P, 2, D]), ALU.mult).then_inc(y_ga, 1)

                def batch(b, first=False, nxt=True, nxt2=True):
                    maxima(b, 1)
                    if not first:
                        normalise(b - 1, [0, 1])
                    if nxt:
                        low(b + 1)
                    if not first:
                        normalise(b - 1, [2, 3])
                    if nxt2:
                        ln_stats(b + 2)
                    if nxt:
                        cosine(b + 1)
                    maxima(b, 2)
                    if not first:
                        att_low(b - 1)
                    if not first:
                        gate(b - 1, [0])
                    if nxt:
                        rotate(b + 1)
                    if not first:
                        gate(b - 1, [1])
                    maxima(b, 3)
                    if nxt:
                        query_stacks(b + 1, 0)
                    if nxt:
                        maxima(b + 1, 0)
                        query_stacks(b + 1, 1)

                ln_stats(0)
                low(0)
                ln_stats(1)
                cosine(0)
                rotate(0)
                query_stacks(0, 0)
                maxima(0, 0)
                query_stacks(0, 1)
                batch(0, first=True)
                with dve.Fori(1, B - 2) as b:
                    batch(b)
                batch(B - 2, nxt2=False)
                batch(B - 1, nxt=False, nxt2=False)
                normalise(B - 1, range(KT))
                att_low(B - 1)
                gate(B - 1, range(2))

            @block.gpsimd
            def _(pool):
                def rsqrt(b):
                    pool.wait_ge(ln_s, 2 * b + 2)
                    if not (isinstance(b, int) and b == 0):
                        wait_apart(pool, xn_done, 4 * b)
                    rsqrt_steps(pool, ln_b, RSQRT_STEPS * b, rstd[:], mv[:, :, 1], nv[:], na[:])

                def ln_apply(b):
                    wait_apart(pool, ln_s, 2 * b + 2)
                    if not (isinstance(b, int) and b == 0):
                        wait_apart(pool, xt_full, 2 * b)
                    if not (isinstance(b, int) and b < 3):
                        wait_apart(pool, at_full, 2 * b - 4)
                    for k in range(KT):
                        pool.tensor_scalar(xn[:, k, :], xb[:, k, :], mv[:, k, 0:1], rstd[:, k:k + 1],
                                           ALU.subtract, ALU.mult).then_inc(xn_done, 1)

                def rotate(b):
                    pool.wait_ge(swapped, 32 * (b + 1))
                    pool.tensor_tensor(qksw[:], qksw[:], rope[:, 1, None, :].broadcast_to([P, 4, S]),
                                       ALU.mult).then_inc(rope2, 1)

                def rotate_low(b):
                    for i in range(4):
                        pool.wait_ge(qkh_done, 4 * b + i + 1)
                        ins = pool.tensor_tensor(qkl[:, i, :], qk[:, i, :], qkh[:, i, :].bitcast(F32), ALU.subtract)
                    ins.then_inc(qkl_done, 1)

                def select(b, g):
                    s = 4 * b + g
                    for pair in range(2):
                        wait_apart(pool, s_free, 10 * s + 5 * pair + 5)
                        pp = probs[:, g % 2, pair * PAIRW:(pair + 1) * PAIRW]
                        heads = pp[:, 0:2048].rearrange("p (u n) -> p u n", u=2)
                        for view, pat in (
                            (heads.rearrange("p u (k n) -> p u k n", k=2)[:, :, :, 0:P], [[0, 2], [0, 2], [1, P]]),
                            (heads[:, :, 896:1024], [[0, 2], [1, P]]),
                            (pp[:, 2048:2560].rearrange("p (u n) -> p u n", u=2)[:, :, 0:P], [[0, 2], [1, P]]),
                        ):
                            ins = pool.affine_select(out=view, in_=view, compare_op=ALU.is_ge, fill=0.0, base=0,
                                                     pattern=pat, channel_multiplier=-1)
                        ins.then_inc(sel_done, 1)

                def residual(b):
                    if not (isinstance(b, int) and b == 0):
                        wait_apart(pool, x1_out, 16 * b)
                    for half in range(2):
                        pool.wait_ge(y_ga, 2 * b + half + 1)
                        rows = xr[:, 2 * half:2 * half + 2, :]
                        pool.tensor_tensor(rows, rows, yo[:], ALU.add).then_inc(x1_done, 1)

                def batch(b, first=False, nxt=True, nxt2=True):
                    select(b, 0)
                    if nxt:
                        rotate(b + 1)
                    select(b, 1)
                    if not first:
                        residual(b - 1)
                    if nxt:
                        rotate_low(b + 1)
                    if nxt2:
                        rsqrt(b + 2)
                    select(b, 2)
                    if nxt2:
                        ln_apply(b + 2)
                    select(b, 3)

                rsqrt(0)
                ln_apply(0)
                rsqrt(1)
                ln_apply(1)
                rotate(0)
                rotate_low(0)
                batch(0, first=True)
                with pool.Fori(1, B - 2) as b:
                    batch(b)
                batch(B - 2, nxt2=False)
                batch(B - 1, nxt=False, nxt2=False)
                residual(B - 1)

            @block.sync
            def _(sp):
                def rows(ap, b):
                    return ap[bass.ds(b * S, S), :].rearrange("(k p) n -> p k n", p=P)

                def load_x(b):
                    if not (isinstance(b, int) and b == 0):
                        sp.wait_ge(xn_done, 4 * b)
                    sp.dma_start(xb[:], rows(d["x"], b)).then_inc(x_in, 16)

                def load_aux(b):
                    if not (isinstance(b, int) and b == 0):
                        wait_apart(sp, x1_out, 16 * b)
                        sp.wait_ge(y_ga, 2 * b)
                    sp.dma_start(xr[:], rows(d["x"], b)).then_inc(aux_in, 16)
                    sp.dma_start(gab[:], d["mod"][bass.ds(b, 1), 2 * D:3 * D].broadcast_to([P, D])).then_inc(aux_in, 16)

                def max_rows(b, g):
                    s = 4 * b + g
                    sp.wait_ge(mrow_done, s + 1)
                    for u in range(2):
                        sp.dma_start(qs[48:128:64, 2 * g + u, :].bitcast(F32), mrow[g % 2][2 * u:2 * u + 2, :].bitcast(F32)).then_inc(mrow_in, 16)

                def swap(b):
                    wait_apart(sp, qk_ev, 4 * (b + 1))
                    if not (isinstance(b, int) and b == 0):
                        sp.wait_ge(rope3, b)
                    for k in range(2):
                        sp.dma_start(qksw[k:P:2, :, :], qk[1 - k:P:2, :, :]).then_inc(swapped, 16)

                def store(b):
                    sp.wait_ge(x1_done, 2 * b + 2)
                    sp.dma_start(rows(d["x1"], b), xr[:]).then_inc(x1_out, 16)

                def batch(b, first=False, nxt=True, nxt2=True):
                    if nxt2:
                        load_x(b + 2)
                    max_rows(b, 1)
                    if nxt:
                        swap(b + 1)
                    max_rows(b, 2)
                    max_rows(b, 3)
                    if not first:
                        store(b - 1)
                        load_aux(b)
                    if nxt:
                        max_rows(b + 1, 0)

                load_x(0)
                load_aux(0)
                load_x(1)
                swap(0)
                max_rows(0, 0)
                batch(0, first=True)
                with sp.Fori(1, B - 2) as b:
                    batch(b)
                batch(B - 2, nxt2=False)
                batch(B - 1, nxt=False, nxt2=False)
                store(B - 1)
                sp.wait_ge(x1_out, 16 * B)


def shared_expert(nc, d, t):
    with ExitStack() as ctx:
        sb = lambda n, s, dt=F32: ctx.enter_context(nc.sbuf_tensor(n, s, dt))
        ps = lambda n: ctx.enter_context(nc.psum_tensor(n, [P, 512], F32))
        sem = lambda n: ctx.enter_context(nc.semaphore(n))
        ident, rgu, rdn, x2 = t["ident"], t["rgu"], t["rdn"], t["x2"]
        wgu = (sb("wguh", [P, DC, 2 * F], F32R), sb("wgul", [P, DC, 2 * F], F32R))
        wdn = (sb("wdnh", [P, FC, D], F32R), sb("wdnl", [P, FC, D], F32R))
        wr = (sb("wrh", [P, DC, NE], F32R), sb("wrl", [P, DC, NE], F32R))
        room = rdn[:].rearrange("p c e n -> p (c e n)")
        wgu32 = room[:, 0:2 * DC * F].rearrange("p (c n) -> p c n", c=DC)
        wdn32 = room[:, 2 * DC * F:2 * DC * F + FC * D].rearrange("p (c n) -> p c n", c=FC)
        wr32 = sb("wr32", [P, DC, NE])
        h2k = sb("h2k", [P, KT, D])
        h2s = sb("h2s", [P, KT, RW])
        bsc = sb("bsc", [P, 2, D])
        bg = sb("bg", [P, D])
        best, score = sb("best", [P, KT]), sb("score", [P, KT])
        oh, seen = sb("oh", [P, KT, NE], BF16), t["seen"]
        ohsum, rank = sb("ohsum", [P, NE]), sb("rank", [P, KT, NE])
        place, slots = sb("place", [P, KT]), sb("slots", [P, KT], I32)
        before = h2s[:, 0, 0:P]
        beforeb = sb("beforeb", [P, P], BF16)
        tokens = sb("tokens", [P, NT, 2], I32)
        xn = sb("xn2", [P, KT, D])
        h2 = sb("h2", [P, KT, D])
        stats, mv = sb("stats2", [P, KT, 6]), sb("mv2", [P, KT, 2])
        rstd, nv, na = sb("rstd2", [P, KT]), sb("nv2", [P, KT]), sb("na2", [P, KT])
        hT = (sb("h2Th", [P, DC, S], F32R), sb("h2Tl", [P, DC, S], F32R))
        lgT = sb("lgT", [NE, S])
        lg, m8 = sb("lg", [P, KT, NE]), sb("m8", [P, KT, 8])
        i8, top = sb("i8", [P, KT, 8], U32), sb("top", [P, KT])
        sg = sb("sg", [P, 2, S])
        hid = sb("hid", [P, 2, S])
        hidT = (sb("hidh", [P, FC, S], F32R), sb("hidl", [P, FC, S], F32R))
        pT, pG, pU, pD = ([ps(f"q{n}{i}") for i in range(2)] for n in "TGUD")

        w_in, wr_in, w_high, w_low = sem("w_in"), sem("wr_in"), sem("w_high"), sem("w_low")
        big_in = t["big_in"]
        x_in, bs_in, gb_in = [sem(f"x2_in{i}") for i in range(3)], sem("bs_in"), sem("gb_in")
        helpers, ex_done, score_step, scaled = sem("helpers"), sem("ex_done"), sem("score_step"), sem("scaled")
        rk_full, rank_step, scattered = sem("rk_full"), sem("rank_step"), sem("scattered")
        ln_s, ln_b, xn_done, xm_done, h2_done = sem("ln2_s"), sem("ln2_b"), sem("xn2_done"), sem("xm_done"), sem("h2_done")
        h2_kept = sem("h2_kept")
        ht_full, hh_done, hl_done = sem("ht_full"), sem("hh_done"), sem("hl_done")
        lt_full, lt_done = sem("lt_full"), sem("lt_done")
        lg_full, lg_done, top_step, oh_done = sem("lg_full"), sem("lg_done"), sem("top_step"), sem("oh_done")
        g_full, u_full, silu_done, hid_done = sem("g_full"), sem("u_full"), sem("silu_done"), sem("hid_done")
        hidh_done, hidl_done = sem("hidh_done"), sem("hidl_done")
        d_full, y_done, x2_done, x2_out = sem("d_full"), sem("y_done"), sem("x2_done"), sem("x2_out")
        c_in, pad_in, r, mm_done, padded = sem("c3_in"), sem("pad_in"), sem("r_step"), sem("r_mm"), sem("padded")
        kept = h2k[:].rearrange("p k n -> p (k n)")
        starts, inside, ended = (kept[:, 320 * i:320 * (i + 1)].rearrange("p (j e) -> p j e", e=NE) for i in range(3))
        over, pad = hid[:, 0, 0:NE * NT].rearrange("p (e j) -> p e j", e=NE), hid[:, 1, 0:RW]
        count, counti, ones8, tiles, ends, begin, moved = (sg[:, 0, NE * i:NE * (i + 1)] for i in range(7))
        used, row, eid = (sg[:, 1, 40 * i:40 * (i + 1)] for i in range(3))

        def pad_rows(eng, e):
            n = eng.value_load(counti[0:1, e:e + 1].bitcast(I32), min_val=0, max_val=B * S)
            eng.dma_start(d["sorted"][bass.ds(n + e * RE, P), :], pad).then_inc(padded, 16)

        def x1_rows(b):
            return x2[:, bass.ds(KT * b, KT), :]

        with nc.Block() as block:

            @block.tensor
            def _(pe):
                def transpose(b):
                    pe.wait_ge(h2_done, b + 1)
                    for c in range(DC):
                        if c == 0 and not (isinstance(b, int) and b == 0):
                            pe.wait_ge(lg_done, b)
                            if not (isinstance(b, int) and b == 1):
                                pe.wait_ge(rank_step, RANK_STEPS * (b - 2) + 1)
                        for k in range(KT):
                            mm = pe.transpose(pT[c][:, k * P:(k + 1) * P], h2[:, k, c * P:(c + 1) * P], ident[:])
                        mm.then_inc(ht_full, 1)

                def logits(b):
                    pe.wait_ge(hl_done, 2 * (b + 1))
                    for n, (c, (s_, m_)) in enumerate((c, p) for c in range(DC) for p in PRODUCTS):
                        mm = pe.matmul(pT[0][0:NE, :], wr[s_][:, c, :], hT[m_][:, c, :], start=(n == 0), stop=(n == 5))
                    mm.then_inc(lt_full, 1)

                def logits_back(b):
                    if not (isinstance(b, int) and b == 0):
                        pe.wait_ge(rank_step, RANK_STEPS * (b - 1) + 1)
                    wait_apart(pe, lt_done, b + 1)
                    for k in range(KT):
                        mm = pe.transpose(pT[1][:, k * NE:(k + 1) * NE], lgT[:, k * P:(k + 1) * P], ident[0:NE, 0:NE])
                    mm.then_inc(lg_full, 1)

                def gate_up(b, first, last):
                    for m in range(first, last):
                        n = FC * b + m
                        for bank, off, free, full in ((pG[m % 2], 0, silu_done, g_full), (pU[m % 2], F, hid_done, u_full)):
                            if not (isinstance(n, int) and n < 2):
                                pe.wait_ge(free, n - 1)
                            for k, (c, (s_, m_)) in enumerate((c, p) for c in range(DC) for p in PRODUCTS):
                                mm = pe.matmul(bank[:], wgu[s_][:, c, off + m * P:off + (m + 1) * P], hT[m_][:, c, :],
                                               start=(k == 0), stop=(k == 5))
                            mm.then_inc(full, 1)

                def down(b):
                    if isinstance(b, int) and b == 0:
                        pe.wait_ge(w_low, 3)
                    pe.wait_ge(hidh_done, FC * (b + 1))
                    for q, low in ((0, 0), (2, 0), (0, 1), (1, 0), (1, 1), (2, 1), (3, 0), (3, 1)):
                        half = q // 2
                        if (q, low) in ((0, 0), (2, 0)) and not (isinstance(b, int) and b == 0):
                            pe.wait_ge(y_done, 2 * b - 1 + half)
                        if (q, low) == (0, 1):
                            pe.wait_ge(hidl_done, FC * (b + 1))
                        steps = [(m, p) for m in range(FC) for p in PRODUCTS if p[0] == low]
                        for n, (m, (s_, m_)) in enumerate(steps):
                            mm = pe.matmul(pD[half][:, (q % 2) * D:(q % 2 + 1) * D], hidT[s_][:, m, q * P:(q + 1) * P],
                                           wdn[m_][:, m, :], start=(n == 0 and not low),
                                           stop=(n == len(steps) - 1 and bool(low)))
                        if (q, low) in ((1, 1), (3, 1)):
                            mm.then_inc(d_full, 1)

                def ranks(b):
                    pe.wait_ge(oh_done, b + 1)
                    bank = pT[1][:, 64:64 + KT * NE].rearrange("p (k e) -> p k e", e=NE)
                    pe.matmul(bank, beforeb[:], oh[:], start=True, stop=False)
                    for k in range(1, KT):
                        pe.matmul(bank[:, k:KT, :], t["onesb"][:], oh[:, k - 1, None, :].broadcast_to([P, KT - k, NE]),
                                  start=False, stop=False)
                    pe.matmul(bank, t["onesb"][:], seen[:, None, :].broadcast_to([P, KT, NE]),
                              start=False, stop=True).then_inc(rk_full, 1)

                def batch(b, nxt=True):
                    gate_up(b, 0, 2)
                    logits_back(b)
                    gate_up(b, 2, FC)
                    if nxt:
                        transpose(b + 1)
                    down(b)
                    if nxt:
                        logits(b + 1)
                    ranks(b)

                transpose(0)
                pe.wait_ge(w_low, 2)
                logits(0)
                pe.wait_ge(helpers, 4)
                batch(0)
                with pe.Fori(1, B - 1) as b:
                    batch(b)
                batch(B - 1, nxt=False)
                pe.wait_ge(rank_step, RANK_STEPS * B)
                pe.wait_ge(lt_done, B)
                pe.matmul(pT[0][:, 0:NE], t["onesb"][:], seen[:], start=True, stop=True).then_inc(mm_done, 1)

            @block.scalar
            def _(act):
                def keep(b):
                    act.wait_ge(h2_done, b + 1)
                    if not (isinstance(b, int) and b == 0):
                        act.wait_ge(scaled, 4 * b)
                    act.activation(h2k[:], h2[:], ACT.Copy).then_inc(h2_kept, 1)

                def exp_best(b):
                    act.wait_ge(top_step, 3 * b + 3)
                    if not (isinstance(b, int) and b == 0):
                        act.wait_ge(scaled, 4 * b)
                    act.activation(score[:], best[:], ACT.Exp, scale=-1.0).then_inc(ex_done, 1)

                def high(b):
                    for c in range(DC):
                        act.wait_ge(ht_full, 2 * b + c + 1)
                        if c == 0 and not (isinstance(b, int) and b == 0):
                            act.wait_ge(u_full, FC * b)
                            act.wait_ge(lt_full, b)
                        act.activation(hT[0][:, c, :], pT[c][:], ACT.Copy).then_inc(hh_done, 1)

                def silu(b):
                    for m in range(FC):
                        n = FC * b + m
                        act.wait_ge(g_full, n + 1)
                        if not (isinstance(n, int) and n < 2):
                            act.wait_ge(hid_done, n - 1)
                        act.activation(sg[:, m % 2, :], pG[m % 2][:], ACT.Silu).then_inc(silu_done, 1)
                        act.wait_ge(hid_done, n + 1)
                        if m == 0 and not (isinstance(b, int) and b == 0):
                            act.wait_ge(d_full, 2 * b)
                        act.activation(hidT[0][:, m, :], hid[:, m % 2, :], ACT.Copy).then_inc(hidh_done, 1)

                act.wait_ge(w_in, 32)
                act.activation(wgu[0][:], wgu32, ACT.Copy).then_inc(w_high, 1)
                act.wait_ge(wr_in, 64)
                act.activation(wr[0][:], wr32[:], ACT.Copy).then_inc(w_high, 1)
                act.activation(wdn[0][:], wdn32, ACT.Copy).then_inc(w_high, 1)
                def batch(b, nxt=True):
                    silu(b)
                    if nxt:
                        high(b + 1)
                    exp_best(b)
                    if nxt:
                        keep(b + 1)

                keep(0)
                high(0)
                batch(0)
                with act.Fori(1, B - 1) as b:
                    batch(b)
                batch(B - 1, nxt=False)
                act.wait_ge(pad_in, 16)
                act.wait_ge(r, 3)
                for e in range(NE // 2, NE):
                    pad_rows(act, e)

            @block.vector
            def _(dve):
                def ln_stats(b):
                    dve.wait_ge(x_in[min(b, 2) if isinstance(b, int) else 2], 16)
                    if not (isinstance(b, int) and b == 0):
                        dve.wait_ge(ln_s, 2 * b)
                    for k in range(KT):
                        ins = dve.bn_stats(stats[:, k, :], x2[:, bass.ds(KT * b + k, 1), :].rearrange("p o n -> p (o n)"))
                    ins.then_inc(ln_s, 1)
                    wait_apart(dve, ln_s, 2 * b + 1)
                    for k in range(KT):
                        ins = dve.bn_aggr(mv[:, k, :], stats[:, k, :])
                    ins.then_inc(ln_s, 1)

                def ln_apply(b):
                    dve.wait_ge(ln_s, 2 * b + 2)
                    dve.wait_ge(ln_b, RSQRT_STEPS * (b + 1))
                    if not (isinstance(b, int) and b == 0):
                        dve.wait_ge(h2_done, b)
                    if not (isinstance(b, int) and b < 2):
                        dve.wait_ge(x2_done, 2 * b - 2)
                    for k in range(KT):
                        dve.tensor_scalar(xn[:, k, :], x2[:, bass.ds(KT * b + k, 1), :].rearrange("p o n -> p (o n)"), mv[:, k, 0:1], rstd[:, k:k + 1],
                                          ALU.subtract, ALU.mult).then_inc(xn_done, 1)
                    dve.wait_ge(xn_done, 4 * (b + 1))
                    dve.wait_ge(bs_in, 16 * (b + 1))
                    dve.tensor_tensor(xn[:], xn[:], bsc[:, 1, None, :].broadcast_to([P, KT, D]),
                                      ALU.mult).then_inc(xm_done, 1)

                def low(b):
                    for c in range(DC):
                        dve.wait_ge(hh_done, 2 * b + c + 1)
                        dve.tensor_tensor(hT[1][:, c, :], pT[c][:], hT[0][:, c, :].bitcast(F32),
                                          ALU.subtract).then_inc(hl_done, 1)

                def logits_out(b):
                    dve.wait_ge(lt_full, b + 1)
                    dve.tensor_copy(lgT[:], pT[0][0:NE, :]).then_inc(lt_done, 1)

                def choose(b):
                    dve.wait_ge(lg_full, b + 1)
                    dve.tensor_copy(lg[:], pT[1][:, 0:KT * NE].rearrange("p (k e) -> p k e", e=NE)).then_inc(lg_done, 1)
                    wait_apart(dve, lg_done, b + 1)
                    for k in range(KT):
                        ins = dve.max(m8[:, k, :], lg[:, k, :])
                    ins.then_inc(top_step, 1)
                    wait_apart(dve, top_step, 3 * b + 1)
                    for k in range(KT):
                        ins = dve.max_index(i8[:, k, :], m8[:, k, :], lg[:, k, :])
                    ins.then_inc(top_step, 1)
                    dve.wait_ge(top_step, 3 * b + 2)
                    if not (isinstance(b, int) and b == 0):
                        dve.wait_ge(ex_done, b)
                    dve.tensor_copy(best[:], m8[:, :, 0])
                    dve.tensor_copy(top[:], i8[:, :, 0]).then_inc(top_step, 1)
                    dve.wait_ge(top_step, 3 * b + 3)
                    if not (isinstance(b, int) and b == 0):
                        dve.wait_ge(rank_step, RANK_STEPS * b)
                    dve.tensor_tensor(oh[:], top[:, :, None].broadcast_to([P, KT, NE]),
                                      t["experts"][:, None, :].broadcast_to([P, KT, NE]), ALU.is_equal).then_inc(oh_done, 1)

                def scale(b):
                    dve.wait_ge(ex_done, b + 1)
                    dve.tensor_scalar(score[:], score[:], 1.0, None, ALU.add).then_inc(score_step, 1)
                    dve.wait_ge(score_step, 2 * b + 1)
                    dve.reciprocal(score[:], score[:]).then_inc(score_step, 1)
                    dve.wait_ge(score_step, 2 * b + 2)
                    if not (isinstance(b, int) and b == 0):
                        dve.wait_ge(scattered, 64 * b)
                    dve.tensor_copy(h2s[:, :, D:RW].bitcast(I32), tokens[:, bass.ds(KT * b, KT), :])
                    dve.wait_ge(h2_kept, b + 1)
                    for k in range(KT):
                        dve.tensor_scalar(h2s[:, k, 0:D], h2k[:, k, :], score[:, k:k + 1], None, ALU.mult).then_inc(scaled, 1)

                def slot(b):
                    n = 0

                    def then(ins):
                        nonlocal n
                        n += 1
                        ins.then_inc(rank_step, 1)
                        dve.wait_ge(rank_step, RANK_STEPS * b + n)

                    dve.wait_ge(rk_full, b + 1)
                    then(dve.tensor_tensor(rank[:], pT[1][:, 64:64 + KT * NE].rearrange("p (k e) -> p k e", e=NE),
                                           t["first"][:, None, :].broadcast_to([P, KT, NE]), ALU.add))
                    then(dve.tensor_tensor(rank[:], rank[:], oh[:], ALU.mult))
                    then(dve.tensor_reduce(place[:], rank[:], AX.X, ALU.add))
                    if not (isinstance(b, int) and b == 0):
                        dve.wait_ge(scattered, 64 * b)
                    then(dve.tensor_copy(slots[:], place[:]))
                    then(dve.tensor_reduce(ohsum[:], oh[:].rearrange("p k e -> p e k"), AX.X, ALU.add))
                    then(dve.tensor_tensor(seen[:], seen[:], ohsum[:], ALU.add))
                    assert n == RANK_STEPS

                def hidden(b, first, last):
                    for m in range(first, last):
                        n = FC * b + m
                        dve.wait_ge(silu_done, n + 1)
                        dve.wait_ge(u_full, n + 1)
                        if not (isinstance(n, int) and n < 2):
                            dve.wait_ge(hidl_done, n - 1)
                        dve.tensor_tensor(hid[:, m % 2, :], pU[m % 2][:], sg[:, m % 2, :], ALU.mult).then_inc(hid_done, 1)

                def gate(b):
                    dve.wait_ge(gb_in, 16 * (b + 1))
                    for half in range(2):
                        dve.wait_ge(d_full, 2 * b + half + 1)
                        if half == 0:
                            dve.wait_ge(h2_done, min(b + 2, B) if isinstance(b, int) else b + 2)
                        dve.tensor_tensor(xn[:, 2 * half:2 * half + 2, :], pD[half][:].rearrange("p (k n) -> p k n", k=2),
                                          bg[:, None, :].broadcast_to([P, 2, D]), ALU.mult).then_inc(y_done, 1)

                def batch(b, nxt=True, nxt2=True):
                    if nxt:
                        ln_apply(b + 1)
                    hidden(b, 0, 2)
                    choose(b)
                    hidden(b, 2, 3)
                    if nxt2:
                        ln_stats(b + 2)
                    hidden(b, 3, FC)
                    if nxt:
                        low(b + 1)
                    scale(b)
                    gate(b)
                    if nxt:
                        logits_out(b + 1)
                    slot(b)

                def slot_tiles():
                    n = 0

                    def then(ins):
                        nonlocal n
                        n += 1
                        ins.then_inc(r, 1)
                        dve.wait_ge(r, n)

                    experts, first = t["experts"][:], t["first"][:]
                    tile_wise = lambda v: v[:, None, :].broadcast_to([P, 40, NE])
                    dve.wait_ge(hidh_done, FC * B)
                    dve.wait_ge(hidl_done, FC * B)
                    then(dve.memset(pad[:, 0:D], 0.0))
                    dve.wait_ge(mm_done, 1)
                    then(dve.tensor_copy(count, pT[0][:, 0:NE]))
                    then(dve.tensor_copy(counti.bitcast(I32), count))
                    then(dve.memset(ones8, 1.0))
                    dve.wait_ge(c_in, 16)
                    then(dve.tensor_tensor(over, count[:, :, None].broadcast_to([P, NE, NT]),
                                           starts[:, 0:NT, 0][:, None, :].broadcast_to([P, NE, NT]), ALU.is_gt))
                    then(dve.tensor_reduce(tiles, over, AX.X, ALU.add))
                    then(dve.tensor_scalar(tiles, tiles, float(P), None, ALU.mult))
                    then(dve.tensor_tensor_scan(ends, ones8, tiles, 0.0, ALU.mult, ALU.add))
                    then(dve.tensor_tensor(begin, ends, tiles, ALU.subtract))
                    then(dve.tensor_tensor(moved, first, begin, ALU.subtract))
                    then(dve.tensor_tensor(inside, tile_wise(begin), starts, ALU.is_le))
                    then(dve.tensor_tensor(ended, tile_wise(ends), starts, ALU.is_gt))
                    then(dve.tensor_tensor(inside, inside, ended, ALU.mult))
                    then(dve.tensor_reduce(used, inside, AX.X, ALU.add))
                    then(dve.tensor_tensor(ended, inside, tile_wise(experts), ALU.mult))
                    then(dve.tensor_reduce(eid, ended, AX.X, ALU.add))
                    then(dve.tensor_copy(t["eid"][:], eid))
                    then(dve.tensor_tensor(inside, inside, tile_wise(moved), ALU.mult))
                    then(dve.tensor_reduce(row, inside, AX.X, ALU.add))
                    then(dve.tensor_scalar(eid, starts[:, :, 0], float(SPARE), None, ALU.subtract))
                    then(dve.tensor_tensor(eid, eid, used, ALU.mult))
                    then(dve.tensor_tensor(row, row, eid, ALU.add))
                    then(dve.tensor_scalar(row, row, float(SPARE), None, ALU.add))
                    then(dve.tensor_copy(t["rows"][:], row))

                ln_stats(0)
                ln_apply(0)
                def split(n, parts, whole):
                    dve.wait_ge(w_high, n)
                    dve.tensor_tensor(parts[1][:], whole, parts[0][:].bitcast(F32), ALU.subtract).then_inc(w_low, 1)

                split(1, wgu, wgu32)
                split(2, wr, wr32[:])
                low(0)
                split(3, wdn, wdn32)
                ln_stats(1)
                dve.wait_ge(wr_in, 64)
                dve.tensor_copy(beforeb[:], before).then_inc(helpers, 1)
                dve.tensor_scalar(t["first"][:], t["experts"][:], float(RE), None, ALU.mult).then_inc(helpers, 1)
                dve.wait_ge(helpers, 4)
                logits_out(0)
                batch(0)
                with dve.Fori(1, B - 2) as b:
                    batch(b)
                batch(B - 2, nxt2=False)
                batch(B - 1, nxt=False, nxt2=False)
                slot_tiles()

            @block.gpsimd
            def _(pool):
                def rsqrt(b):
                    pool.wait_ge(ln_s, 2 * b + 2)
                    if not (isinstance(b, int) and b == 0):
                        wait_apart(pool, xn_done, 4 * b)
                    rsqrt_steps(pool, ln_b, RSQRT_STEPS * b, rstd[:], mv[:, :, 1], nv[:], na[:])

                def shift(b):
                    pool.wait_ge(xm_done, b + 1)
                    if not (isinstance(b, int) and b == 0):
                        pool.wait_ge(ht_full, 2 * b)
                        pool.wait_ge(h2_kept, b)
                    pool.tensor_tensor(h2[:], xn[:], bsc[:, 0, None, :].broadcast_to([P, KT, D]), ALU.add).then_inc(h2_done, 1)

                def low(b, first, last):
                    for m in range(first, last):
                        pool.wait_ge(hidh_done, FC * b + m + 1)
                        pool.tensor_tensor(hidT[1][:, m, :], hid[:, m % 2, :], hidT[0][:, m, :].bitcast(F32),
                                           ALU.subtract).then_inc(hidl_done, 1)

                def residual(b):
                    for half in range(2):
                        pool.wait_ge(y_done, 2 * b + half + 1)
                        rows = x2[:, bass.ds(KT * b + 2 * half, 2), :]
                        pool.tensor_tensor(rows, rows, xn[:, 2 * half:2 * half + 2, :], ALU.add).then_inc(x2_done, 1)

                def scatter(b):
                    pool.wait_ge(scaled, 4 * (b + 1))
                    wait_apart(pool, rank_step, RANK_STEPS * b + 4)
                    for k in range(KT):
                        pool.indirect_dma_start(
                            out=d["sorted"], out_offset=bass.IndirectOffsetOnAxis(ap=slots[:, k:k + 1].bitcast(U32), axis=0),
                            in_=h2s[:, k, :], in_offset=None).then_inc(scattered, 16)

                def batch(b, nxt=True, nxt2=True):
                    if nxt:
                        shift(b + 1)
                    low(b, 0, 1)
                    low(b, 1, FC)
                    if nxt2:
                        rsqrt(b + 2)
                    residual(b)
                    scatter(b)

                pool.memset(t["onesb"][:], 1.0).then_inc(helpers, 1)
                pool.memset(seen[:], 0.0).then_inc(helpers, 1)
                rsqrt(0)
                shift(0)
                rsqrt(1)
                batch(0)
                with pool.Fori(1, B - 2) as b:
                    batch(b)
                batch(B - 2, nxt2=False)
                batch(B - 1, nxt=False, nxt2=False)
                pool.wait_ge(scattered, 64 * B)

            @block.sync
            def _(sp):
                def rows(ap, b):
                    return ap[bass.ds(b * S, S), :].rearrange("(k p) n -> p k n", p=P)

                def load_bs(b):
                    if not (isinstance(b, int) and b == 0):
                        sp.wait_ge(h2_done, b)
                    sp.dma_start(bsc[:].rearrange("p k n -> p (k n)"),
                                 d["mod"][bass.ds(b, 1), 3 * D:5 * D].broadcast_to([P, 2 * D])).then_inc(bs_in, 16)

                def load_bg(b):
                    if not (isinstance(b, int) and b == 0):
                        sp.wait_ge(y_done, 2 * b)
                    sp.dma_start(bg[:], d["mod"][bass.ds(b, 1), 5 * D:6 * D].broadcast_to([P, D])).then_inc(gb_in, 16)

                sp.dma_start(x1_rows(0), rows(d["x1"], 0)).then_inc(x_in[0], 16)
                load_bs(0)
                sp.dma_start(wgu32, d["sgu"].rearrange("(c p) n -> p c n", p=P)).then_inc(w_in, 16)
                sp.dma_start(wdn32, d["sdn"].rearrange("(c p) n -> p c n", p=P)).then_inc(w_in, 16)
                sp.dma_start(wr32[:], d["wr"].rearrange("(c p) n -> p c n", p=P)).then_inc(wr_in, 16)
                sp.dma_start(t["experts"][:], d["c_experts"]).then_inc(wr_in, 16)
                sp.dma_start(before, d["c_before"]).then_inc(wr_in, 16)
                sp.dma_start(tokens[:], d["c_tokens"]).then_inc(wr_in, 16)
                sp.dma_start(x1_rows(1), rows(d["x1"], 1)).then_inc(x_in[1], 16)
                load_bg(0)
                sp.dma_start(x2[:, 2 * KT:NT, :], d["x1"][2 * S:B * S, :].rearrange("(k p) n -> p k n", p=P)).then_inc(x_in[2], 16)
                load_bs(1)
                def load_expert(e):
                    for tile, name in ((rgu, "rgu"), (rdn, "rdn")):
                        sp.dma_start(tile[:, :, bass.ds(e, 1), :],
                                     d[name][:, bass.ds(e, 1), :].rearrange("(c p) e n -> p c e n", p=P)).then_inc(big_in, 16)

                def store(b):
                    sp.wait_ge(x2_done, 2 * b + 2)
                    sp.dma_start(rows(d["out"], b), x1_rows(b)).then_inc(x2_out, 16)

                load_bs(2)
                sp.wait_ge(w_low, 3)
                load_expert(0)
                load_bg(1)
                store(0)
                with sp.Fori(1, B - 2) as b:
                    load_bs(b + 2)
                    load_expert(b)
                    load_bg(b + 1)
                    store(b)
                load_expert(B - 2)
                load_bg(B - 1)
                load_expert(B - 1)
                store(B - 2)
                sp.wait_ge(scaled, 4 * B)
                sp.dma_start(starts, d["c_starts"]).then_inc(c_in, 16)
                sp.wait_ge(hidh_done, FC * B)
                sp.wait_ge(hidl_done, FC * B)
                sp.dma_start(pad[:, D:RW].bitcast(I32), d["c_padding"]).then_inc(pad_in, 16)
                sp.wait_ge(pad_in, 16)
                sp.wait_ge(r, 3)
                for e in range(NE // 2):
                    pad_rows(sp, e)
                sp.dma_start(d["sorted"][SPARE:SPARE + P, :], pad).then_inc(padded, 16)
                sp.dma_start(d["out"][B * S:B * S + P, :], pad[:, 0:D]).then_inc(padded, 16)
                store(B - 1)
                sp.wait_ge(padded, 16 * (NE + 2))
                sp.wait_ge(x2_out, 16 * B)
                sp.wait_ge(big_in, 32 * NE)


def routed_experts(nc, d, t):
    with ExitStack() as ctx:
        sb = lambda n, s, dt=F32: ctx.enter_context(nc.sbuf_tensor(n, s, dt))
        ps = lambda n: ctx.enter_context(nc.psum_tensor(n, [P, 512], F32))
        sem = lambda n: ctx.enter_context(nc.semaphore(n))
        ident, rgu, rdn, eid = t["ident"], t["rgu"], t["rdn"], t["eid"]
        xs = sb("xs", [P, 2, RW])
        idx = sb("idx", [P, 2, 2], I32)
        gbr = sb("gbr", [P, 2, D])
        gb_in = sem("gbr_in")
        xT = sb("xT", [P, 2, DC, P])
        sg = sb("sg4", [P, 2, F])
        hid = sb("hid4", [P, 2, F])
        hT = sb("hT4", [P, 2, FC, P])
        y = sb("y4", [P, 2, D])
        pX, pH = ps("rX"), ps("rH")
        pG, pU, pY = ([ps(f"r{n}{i}") for i in range(2)] for n in "GUY")
        xs_in = [sem(f"xs_in{k}") for k in range(2)]
        idx_done, y_out = sem("idx_done"), sem("y4_out")
        xt_full, xt_done = sem("xt4_full"), sem("xt4_done")
        g_full, u_full, silu_done, hid_done = sem("g4_full"), sem("u4_full"), sem("silu4"), sem("hid4")
        h_full, h_done, y_full, y_done = sem("h4_full"), sem("h4_done"), sem("y4_full"), sem("y4_done")
        early = lambda n, k: isinstance(n, int) and n < k

        with nc.Block() as block:

            @block.tensor
            def _(pe):
                def x_transpose(s, k):
                    pe.wait_ge(xs_in[k], 8 * (s - k) + 16)
                    if not early(s, 1):
                        pe.wait_ge(xt_done, s)
                    for c in range(DC):
                        mm = pe.transpose(pX[:, c * P:(c + 1) * P], xs[:, k, c * P:(c + 1) * P], ident[:])
                    mm.then_inc(xt_full, 1)

                def gate_up(s, k):
                    e = pe.value_load(eid[0:1, bass.ds(s, 1)], min_val=0, max_val=NE - 1)
                    pe.wait_ge(xt_done, s + 1)
                    for bank, off, free, full in ((pG[k], 0, silu_done, g_full), (pU[k], F, hid_done, u_full)):
                        if not early(s, 2):
                            pe.wait_ge(free, s - 1)
                        for c in range(DC):
                            mm = pe.matmul(bank[:], xT[:, k, c, :],
                                           rgu[:, c, bass.ds(e, 1), off:off + F].rearrange("p o n -> p (o n)"),
                                           start=(c == 0), stop=(c == DC - 1))
                        mm.then_inc(full, 1)
                    return e

                def h_transpose(s, k):
                    pe.wait_ge(hid_done, s + 1)
                    if not early(s, 1):
                        pe.wait_ge(h_done, s)
                    for m in range(FC):
                        mm = pe.transpose(pH[:, m * P:(m + 1) * P], hid[:, k, m * P:(m + 1) * P], ident[:])
                    mm.then_inc(h_full, 1)

                def down(s, k):
                    e = pe.value_load(eid[0:1, bass.ds(s, 1)], min_val=0, max_val=NE - 1)
                    pe.wait_ge(h_done, s + 1)
                    if not early(s, 2):
                        pe.wait_ge(y_done, s - 1)
                    for m in range(FC):
                        mm = pe.matmul(pY[k][:, 0:D], hT[:, k, m, :],
                                       rdn[:, m, bass.ds(e, 1), :].rearrange("p o n -> p (o n)"),
                                       start=(m == 0), stop=(m == FC - 1))
                    mm.then_inc(y_full, 1)

                def step(s, k):
                    x_transpose(s + 1, 1 - k)
                    h_transpose(s, k)
                    gate_up(s + 1, 1 - k)
                    down(s, k)

                x_transpose(0, 0)
                gate_up(0, 0)
                step(0, 0)
                step(1, 1)
                with pe.Fori(1, ST // 2) as i:
                    step(2 * i, 0)
                    step(2 * i + 1, 1)
                h_transpose(ST - 1, 0)
                down(ST - 1, 0)

            @block.scalar
            def _(act):
                def x_evac(s, k):
                    act.wait_ge(xt_full, s + 1)
                    if not early(s, 2):
                        act.wait_ge(u_full, s - 1)
                    act.activation(xT[:, k], pX[:, 0:D].rearrange("p (c n) -> p c n", c=DC), ACT.Copy).then_inc(xt_done, 1)

                def silu(s, k):
                    act.wait_ge(g_full, s + 1)
                    if not early(s, 2):
                        act.wait_ge(hid_done, s - 1)
                    act.activation(sg[:, k, :], pG[k][:], ACT.Silu).then_inc(silu_done, 1)

                def step(s, k):
                    x_evac(s + 1, 1 - k)
                    silu(s + 1, 1 - k)

                x_evac(0, 0)
                silu(0, 0)
                step(0, 0)
                step(1, 1)
                with act.Fori(1, ST // 2) as i:
                    step(2 * i, 0)
                    step(2 * i + 1, 1)

            @block.vector
            def _(dve):
                def hidden(s, k):
                    dve.wait_ge(silu_done, s + 1)
                    dve.wait_ge(u_full, s + 1)
                    if not early(s, 2):
                        dve.wait_ge(h_full, s - 1)
                    dve.tensor_tensor(hid[:, k, :], pU[k][:], sg[:, k, :], ALU.mult).then_inc(hid_done, 1)

                def h_evac(s, k):
                    dve.wait_ge(h_full, s + 1)
                    if not early(s, 2):
                        dve.wait_ge(y_full, s - 1)
                    dve.tensor_copy(hT[:, k], pH[:].rearrange("p (m n) -> p m n", m=FC)).then_inc(h_done, 1)

                def index(s, k):
                    dve.wait_ge(xs_in[k], 8 * (s - k) + 16)
                    if not early(s, 2):
                        dve.wait_ge(y_out, 16 * (s - 1))
                    dve.tensor_copy(idx[:, k, :], xs[:, k, D:RW].bitcast(I32)).then_inc(idx_done, 1)

                def gate(s, k):
                    dve.wait_ge(gb_in, 16 * (s + 1))
                    dve.wait_ge(y_full, s + 1)
                    dve.tensor_tensor(y[:, k, :], pY[k][:, 0:D], gbr[:, k, :], ALU.mult).then_inc(y_done, 1)

                def step(s, k):
                    h_evac(s, k)
                    index(s, k)
                    hidden(s + 1, 1 - k)
                    gate(s, k)

                hidden(0, 0)
                step(0, 0)
                step(1, 1)
                with dve.Fori(1, ST // 2) as i:
                    step(2 * i, 0)
                    step(2 * i + 1, 1)
                h_evac(ST - 1, 0)
                index(ST - 1, 0)
                gate(ST - 1, 0)

            @block.gpsimd
            def _(pool):
                def scatter(s, k):
                    wait_apart(pool, idx_done, s + 1)
                    if not early(s, 2):
                        wait_apart(pool, y_done, s - 1)
                    pool.indirect_dma_start(
                        out=gbr[:, k, :], out_offset=None, in_=d["gb"],
                        in_offset=bass.IndirectOffsetOnAxis(ap=idx[:, k, 1:2].bitcast(U32), axis=0)).then_inc(gb_in, 16)
                    if not early(s, 1):
                        pool.wait_ge(y_out, 16 * s)
                    wait_apart(pool, y_done, s + 1)
                    pool.indirect_dma_start(
                        out=d["out"], out_offset=bass.IndirectOffsetOnAxis(ap=idx[:, k, 0:1].bitcast(U32), axis=0),
                        in_=y[:, k, :], in_offset=None, compute_op=ALU.add).then_inc(y_out, 16)

                scatter(0, 0)
                scatter(1, 1)
                with pool.Fori(1, ST // 2) as i:
                    scatter(2 * i, 0)
                    scatter(2 * i + 1, 1)
                scatter(ST - 1, 0)
                pool.wait_ge(y_out, 16 * ST)

            @block.sync
            def _(sp):
                def load(s, k):
                    n = sp.value_load(t["rows"][0:1, bass.ds(s, 1)], min_val=0, max_val=SPARE)
                    if not early(s, 2):
                        sp.wait_ge(xt_full, s - 1)
                        wait_apart(sp, idx_done, s - 1)
                    sp.dma_start(xs[:, k, :], d["sorted"][bass.ds(n, P), :]).then_inc(xs_in[k], 16)

                load(0, 0)
                load(1, 1)
                load(2, 0)
                load(3, 1)
                with sp.Fori(1, ST // 2) as i:
                    load(2 * i + 2, 0)
                    load(2 * i + 3, 1)
                sp.wait_ge(xs_in[1], 16 * (ST // 2 + 1))


def program(nc, d):
    with ExitStack() as whole:
        keep = lambda n, s, dt=F32: whole.enter_context(nc.sbuf_tensor(n, s, dt))
        t = {"ident": keep("ident", [P, P]),
             "big_in": whole.enter_context(nc.semaphore("big_in"))}
        with ExitStack() as ctx:
            sb = lambda n, s, dt=F32: ctx.enter_context(nc.sbuf_tensor(n, s, dt))
            t |= {
                "wh": sb("wh", [P, DC, 4 * D], F32R), "wl": sb("wl", [P, DC, 4 * D], F32R),
                "rope": sb("rope", [P, 2, S]), "mask": sb("mask", [P, S]),
                "modT": sb("modT", [P, 4, B]),
                "sel": sb("sel", [P, 4, 4, P], F32R), "ones": sb("key_ones", [P, 1]),
                "qs": sb("qs", [P, NH // 2, S], F32R), "ks": sb("ks", [P, NH, S], F32R),
                "vaug": sb("vaug", [P, KT, NH, 32]),
            }
            setup(nc, d, t)
            attention(nc, d, t)
        with ExitStack() as ctx:
            sb = lambda n, s, dt=F32: ctx.enter_context(nc.sbuf_tensor(n, s, dt))
            t |= {"rgu": sb("rgu", [P, DC, NE, 2 * F]), "rdn": sb("rdn", [P, FC, NE, D])}
            t |= {"eid": sb("eid", [P, 40], I32), "rows": sb("rows", [P, 40], I32),
                  "experts": sb("experts", [P, NE]), "first": sb("first", [P, NE]), "seen": sb("seen", [P, NE], BF16),
                  "onesb": sb("onesb", [P, P], BF16)}
            t |= {"x2": sb("x2", [P, NT, D])}
            shared_expert(nc, d, t)
            routed_experts(nc, d, t)


def kernel(**inputs):
    import numpy as _np
    import concourse.bacc as _bacc
    from concourse.bass_utils import run_bass_kernel_spmd as _run

    i = {k: _np.asarray(v) for k, v in inputs.items()}
    arrays = {
        "x": i["L0_attn_x"].reshape(B * S, D),
        "cT": i["L0_c"].T, "wmod": i["L0_wmod"],
        "qw": i["L0_attn_qw"], "kw": i["L0_attn_kw"], "vw": i["L0_attn_vw"], "ow": i["L0_attn_ow"],
        "wr": i["L0_ffn_gate_w"].T,
        "sgu": _np.concatenate([i["L0_ffn_shared_gate"], i["L0_ffn_shared_up"]], axis=0).T,
        "sdn": i["L0_ffn_shared_down"].T,
        "rgu": _np.concatenate([i["L0_ffn_r_gate"], i["L0_ffn_r_up"]], axis=1).transpose(2, 0, 1),
        "rdn": i["L0_ffn_r_down"].transpose(2, 0, 1),
        **constants(),
    }
    arrays = {f"in_{k}": _np.ascontiguousarray(v) for k, v in arrays.items()}
    nc = _bacc.Bacc("TRN2", target_bir_lowering=False, num_devices=1)
    d = {k[3:]: nc.dram_tensor(k, v.shape, mybir.dt.from_np(v.dtype), kind="ExternalInput").ap()
         for k, v in arrays.items()}
    for name, shape in (("mod", (B, 6 * D)), ("x1", (B * S, D)), ("gb", (B + 1, D)), ("sorted", (SPARE + P, RW))):
        d[name] = nc.dram_tensor(f"scratch_{name}", shape, F32, kind="Internal").ap()
    d["out"] = nc.dram_tensor("out_0", (B * S + P, D), F32, kind="ExternalOutput").ap()
    program(nc, d)
    r = _run(nc, [arrays], core_ids=[0])
    return r.results[0]["out_0"][:B * S].reshape(B, S, D)
```
